# Optimizing a Trainium2 kernel written in Bass

```python
import numpy as np
import jax
import jax.numpy as jnp

def _softmax(x, axis=-1):
    return jax.nn.softmax(x, axis=axis)

def _gelu(x):
    return jax.nn.gelu(x, approximate=True)

def _silu(x):
    return jax.nn.silu(x)

def _sigmoid(x):
    return jax.nn.sigmoid(x)

def _layernorm(x, axis=-1, eps=1e-05):
    m = jnp.mean(x, axis=axis, keepdims=True)
    v = jnp.var(x, axis=axis, keepdims=True)
    return (x - m) / jnp.sqrt(v + eps)

def _scatter_add(tgt, idx, src, axis=0):
    return tgt.at[idx].add(src)

def _segment_sum(src, seg, n):
    return jax.ops.segment_sum(src, seg, n)
kernel_name = 'mk_sandwich_d2_jaxref_r8_24f71e'

def setup_inputs(seed: int=0):
    np.random.seed(seed)
    _w = jnp.asarray

    def _L0_attn_setup():
        import jax, jax.numpy as jnp
        import numpy as np
        import math
        N_HEAD = 16
        V_HEAD = 32
        NOPE = 32
        ROPE_D = 64
        KEEP = 32
        EPS = 1e-06

        def _freqs(T, dim=ROPE_D, theta=10000.0):
            f = 1.0 / theta ** (jnp.arange(0, dim, 2, dtype=jnp.float32) / dim)
            t = jnp.arange(T, dtype=jnp.float32)
            a = jnp.outer(t, f)
            return (jnp.cos(a), jnp.sin(a))

        def _rope(x, cos, sin):
            S = x.shape[-2]
            c = cos[:S][None, None]
            s = sin[:S][None, None]
            x1, x2 = jnp.split(x, 2, axis=-1)
            return jnp.concatenate([x1 * c - x2 * s, x1 * s + x2 * c], axis=-1)

        def _rms(x, g, eps=EPS):
            return x * jax.lax.rsqrt(jnp.mean(x * x, axis=-1, keepdims=True) + eps) * g

        def _attn(q, k, v, causal):
            scale = 1.0 / math.sqrt(q.shape[-1])
            s = jnp.einsum('bhqd,bhkd->bhqk', q, k) * scale
            if causal:
                Tq, Tk = (s.shape[-2], s.shape[-1])
                mask = jnp.tril(jnp.ones((Tq, Tk), dtype=bool))
                s = jnp.where(mask, s, jnp.finfo(s.dtype).min)
            return jnp.einsum('bhqk,bhkd->bhqd', jax.nn.softmax(s, axis=-1), v)

        def _forward(x, w_cq, g_qnorm, w_dq_nope, w_dq_rope, w_ckv, g_kvnorm, w_dk_nope, w_dv, w_krope, w_imp, w_selk, w_selv, w_wink, w_winv, w_gate, w_proj):
            B, T, C = x.shape
            cos, sin = _freqs(T)
            nq = _rms(x @ w_cq, g_qnorm)
            q_nope = (nq @ w_dq_nope).reshape(B, T, N_HEAD, NOPE).transpose(0, 2, 1, 3)
            q_rope = (nq @ w_dq_rope).reshape(B, T, N_HEAD, ROPE_D).transpose(0, 2, 1, 3)
            q_rope = _rope(q_rope, cos, sin)
            q = jnp.concatenate([q_nope, q_rope], axis=-1)
            gate = jax.nn.softmax((x @ w_gate).mean(axis=1), axis=-1)
            ckv = _rms(x @ w_ckv, g_kvnorm)
            k_nope = (ckv @ w_dk_nope).reshape(B, T, N_HEAD, NOPE).transpose(0, 2, 1, 3)
            v1 = (ckv @ w_dv).reshape(B, T, N_HEAD, V_HEAD).transpose(0, 2, 1, 3)
            k_rope = (x @ w_krope).reshape(B, T, 1, ROPE_D).transpose(0, 2, 1, 3) / N_HEAD
            k_rope = _rope(k_rope, cos, sin)
            k1 = jnp.concatenate([k_nope, jnp.broadcast_to(k_rope, (B, N_HEAD, T, ROPE_D))], axis=-1)
            scores = (x @ w_imp)[..., 0]
            _, idx = jax.lax.top_k(scores, KEEP)
            idx = jnp.sort(idx, axis=1)
            sel = jnp.take_along_axis(x, idx[:, :, None], axis=1)
            ks = (sel @ w_selk).reshape(B, KEEP, N_HEAD, NOPE + ROPE_D).transpose(0, 2, 1, 3)
            vs = (sel @ w_selv).reshape(B, KEEP, N_HEAD, V_HEAD).transpose(0, 2, 1, 3)
            ks = jnp.concatenate([ks[..., :NOPE], _rope(ks[..., NOPE:], cos, sin)], axis=-1)
            kw = (x @ w_wink).reshape(B, T, N_HEAD, NOPE + ROPE_D).transpose(0, 2, 1, 3)
            vw = (x @ w_winv).reshape(B, T, N_HEAD, V_HEAD).transpose(0, 2, 1, 3)
            kw = jnp.concatenate([kw[..., :NOPE], _rope(kw[..., NOPE:], cos, sin)], axis=-1)
            a1 = _attn(q, k1, v1, causal=True)
            a2 = _attn(q, ks, vs, causal=False)
            a3 = _attn(q, kw, vw, causal=True)
            g = gate[:, :, None, None, None]
            out = g[:, 0] * a1 + g[:, 1] * a2 + g[:, 2] * a3
            out = out.transpose(0, 2, 1, 3).reshape(B, T, N_HEAD * V_HEAD)
            return out @ w_proj
        key = jax.random.key(seed)
        ks = jax.random.split(key, 20)
        B, T, C = (2, 128, 128)
        q_lora, kv_lora = (96, 32)
        std = 0.02

        def w(k, shape):
            return jax.random.normal(k, shape, dtype=jnp.float32) * std
        return {'x': jax.random.normal(ks[0], (B, T, C), dtype=jnp.float32), 'w_cq': w(ks[1], (C, q_lora)), 'g_qnorm': jnp.ones((q_lora,), jnp.float32), 'w_dq_nope': w(ks[2], (q_lora, N_HEAD * NOPE)), 'w_dq_rope': w(ks[3], (q_lora, N_HEAD * ROPE_D)), 'w_ckv': w(ks[4], (C, kv_lora)), 'g_kvnorm': jnp.ones((kv_lora,), jnp.float32), 'w_dk_nope': w(ks[5], (kv_lora, N_HEAD * NOPE)), 'w_dv': w(ks[6], (kv_lora, N_HEAD * V_HEAD)), 'w_krope': w(ks[7], (C, ROPE_D)), 'w_imp': w(ks[8], (C, 1)), 'w_selk': w(ks[9], (C, N_HEAD * (NOPE + ROPE_D))), 'w_selv': w(ks[10], (C, N_HEAD * V_HEAD)), 'w_wink': w(ks[11], (C, N_HEAD * (NOPE + ROPE_D))), 'w_winv': w(ks[12], (C, N_HEAD * V_HEAD)), 'w_gate': w(ks[13], (C, 3)), 'w_proj': w(ks[14], (N_HEAD * V_HEAD, C))}
    _L0_attn_in = _L0_attn_setup()

    def _L0_ffn_setup():
        import jax, jax.numpy as jnp
        import numpy as np
        B, S, D, E, H, K = (64, 256, 128, 32, 512, 8)
        key = jax.random.key(seed)
        k0, k1, k2, k3 = jax.random.split(key, 4)
        x = jax.random.normal(k0, (B, S, D), jnp.float32)
        gate_w = jax.random.normal(k1, (E, D), jnp.float32) * (1.0 / np.sqrt(D))
        gate_b = jnp.zeros((E,), jnp.float32)
        w1 = jax.random.normal(k2, (E, D + 1, H), jnp.float32) * (1.0 / np.sqrt(D + 1))
        w2 = jax.random.normal(k3, (E, H + 1, D), jnp.float32) * (1.0 / np.sqrt(H + 1))
        return {'x': x, 'gate_w': gate_w, 'gate_b': gate_b, 'w1': w1, 'w2': w2}
    _L0_ffn_in = _L0_ffn_setup()

    def _L1_attn_setup():
        import jax, jax.numpy as jnp
        import numpy as np
        D_MODEL, N_HEADS, N_KV, HEAD_DIM, D_LAT = (128, 8, 2, 128, 32)
        N_REP = N_HEADS // N_KV
        B, T = (2, 256)
        key = jax.random.key(seed)
        ks = jax.random.split(key, 8)
        s = lambda fan_in: 1.0 / np.sqrt(fan_in)
        return {'x': jax.random.normal(ks[0], (B, T, D_MODEL), jnp.float32), 'wq': jax.random.normal(ks[1], (D_MODEL, N_HEADS * HEAD_DIM), jnp.float32) * s(D_MODEL), 'wk_down': jax.random.normal(ks[2], (D_MODEL, N_KV * D_LAT), jnp.float32) * s(D_MODEL), 'wv_down': jax.random.normal(ks[3], (D_MODEL, N_KV * D_LAT), jnp.float32) * s(D_MODEL), 'wk_up': jax.random.normal(ks[4], (D_LAT, HEAD_DIM), jnp.float32) * s(D_LAT), 'wv_up': jax.random.normal(ks[5], (D_LAT, HEAD_DIM), jnp.float32) * s(D_LAT), 'wo': jax.random.normal(ks[6], (N_HEADS * HEAD_DIM, D_MODEL), jnp.float32) * s(N_HEADS * HEAD_DIM)}
    _L1_attn_in = _L1_attn_setup()

    def _L1_ffn_setup():
        import jax, jax.numpy as jnp
        import numpy as np
        DIM = 128
        INTER = 128
        E = 8
        TOPK = 2
        ROUTE_SCALE = 1.0
        SHARED_INTER = 256
        B, S = (4, 256)

        def _moe_forward(x, gate_w, gate_b, w1, b1, w3, b3, w2, b2, ws1, bs1, ws3, bs3, ws2, bs2):
            Bq, Sq, D = x.shape
            xt = x.reshape(-1, D)
            logits = (xt @ gate_w.T + gate_b).astype(jnp.float32)
            scores = jax.nn.softmax(logits, axis=-1)
            top_w, top_i = jax.lax.top_k(scores, TOPK)
            weights = (top_w * ROUTE_SCALE).astype(x.dtype)
            gate_dense = jnp.sum(jax.nn.one_hot(top_i, E, dtype=x.dtype) * weights[..., None], axis=1)

            def expert(w1e, b1e, w3e, b3e, w2e, b2e):
                h = jax.nn.silu(xt @ w1e.T + b1e) * (xt @ w3e.T + b3e)
                return h @ w2e.T + b2e
            outs = jax.vmap(expert)(w1, b1, w3, b3, w2, b2)
            y = jnp.einsum('etd,te->td', outs, gate_dense)
            z = jax.nn.silu(xt @ ws1.T + bs1) * (xt @ ws3.T + bs3) @ ws2.T + bs2
            return (y + z).reshape(Bq, Sq, D)
        key = jax.random.key(seed)
        ks = jax.random.split(key, 10)

        def w(k, shape, scale=0.02):
            return jax.random.normal(k, shape, jnp.float32) * scale
        return {'x': jax.random.normal(ks[0], (B, S, DIM), jnp.float32), 'gate_w': w(ks[1], (E, DIM)), 'gate_b': jnp.zeros((E,), jnp.float32), 'w1': w(ks[2], (E, INTER, DIM)), 'b1': jnp.zeros((E, INTER), jnp.float32), 'w3': w(ks[3], (E, INTER, DIM)), 'b3': jnp.zeros((E, INTER), jnp.float32), 'w2': w(ks[4], (E, DIM, INTER)), 'b2': jnp.zeros((E, DIM), jnp.float32), 'ws1': w(ks[5], (SHARED_INTER, DIM)), 'bs1': jnp.zeros((SHARED_INTER,), jnp.float32), 'ws3': w(ks[6], (SHARED_INTER, DIM)), 'bs3': jnp.zeros((SHARED_INTER,), jnp.float32), 'ws2': w(ks[7], (DIM, SHARED_INTER)), 'bs2': jnp.zeros((DIM,), jnp.float32)}
    _L1_ffn_in = _L1_ffn_setup()
    _d = {'L0_attn_x': _L0_attn_in['x'], 'L0_attn_w_cq': _L0_attn_in['w_cq'], 'L0_attn_g_qnorm': _L0_attn_in['g_qnorm'], 'L0_attn_w_dq_nope': _L0_attn_in['w_dq_nope'], 'L0_attn_w_dq_rope': _L0_attn_in['w_dq_rope'], 'L0_attn_w_ckv': _L0_attn_in['w_ckv'], 'L0_attn_g_kvnorm': _L0_attn_in['g_kvnorm'], 'L0_attn_w_dk_nope': _L0_attn_in['w_dk_nope'], 'L0_attn_w_dv': _L0_attn_in['w_dv'], 'L0_attn_w_krope': _L0_attn_in['w_krope'], 'L0_attn_w_imp': _L0_attn_in['w_imp'], 'L0_attn_w_selk': _L0_attn_in['w_selk'], 'L0_attn_w_selv': _L0_attn_in['w_selv'], 'L0_attn_w_wink': _L0_attn_in['w_wink'], 'L0_attn_w_winv': _L0_attn_in['w_winv'], 'L0_attn_w_gate': _L0_attn_in['w_gate'], 'L0_attn_w_proj': _L0_attn_in['w_proj'], 'L0_ffn_gate_w': _L0_ffn_in['gate_w'], 'L0_ffn_gate_b': _L0_ffn_in['gate_b'], 'L0_ffn_w1': _L0_ffn_in['w1'], 'L0_ffn_w2': _L0_ffn_in['w2'], 'L1_attn_wq': _L1_attn_in['wq'], 'L1_attn_wk_down': _L1_attn_in['wk_down'], 'L1_attn_wv_down': _L1_attn_in['wv_down'], 'L1_attn_wk_up': _L1_attn_in['wk_up'], 'L1_attn_wv_up': _L1_attn_in['wv_up'], 'L1_attn_wo': _L1_attn_in['wo'], 'L1_ffn_gate_w': _L1_ffn_in['gate_w'], 'L1_ffn_gate_b': _L1_ffn_in['gate_b'], 'L1_ffn_w1': _L1_ffn_in['w1'], 'L1_ffn_b1': _L1_ffn_in['b1'], 'L1_ffn_w3': _L1_ffn_in['w3'], 'L1_ffn_b3': _L1_ffn_in['b3'], 'L1_ffn_w2': _L1_ffn_in['w2'], 'L1_ffn_b2': _L1_ffn_in['b2'], 'L1_ffn_ws1': _L1_ffn_in['ws1'], 'L1_ffn_bs1': _L1_ffn_in['bs1'], 'L1_ffn_ws3': _L1_ffn_in['ws3'], 'L1_ffn_bs3': _L1_ffn_in['bs3'], 'L1_ffn_ws2': _L1_ffn_in['ws2'], 'L1_ffn_bs2': _L1_ffn_in['bs2']}
    _x0 = _d['L0_attn_x']
    _d['L0_attn_x'] = jax.random.normal(jax.random.fold_in(jax.random.key(seed), 1), (16, 256, 128), dtype=_x0.dtype)
    del _x0
    return _d

def reference(L0_attn_x, L0_attn_w_cq, L0_attn_g_qnorm, L0_attn_w_dq_nope, L0_attn_w_dq_rope, L0_attn_w_ckv, L0_attn_g_kvnorm, L0_attn_w_dk_nope, L0_attn_w_dv, L0_attn_w_krope, L0_attn_w_imp, L0_attn_w_selk, L0_attn_w_selv, L0_attn_w_wink, L0_attn_w_winv, L0_attn_w_gate, L0_attn_w_proj, L0_ffn_gate_w, L0_ffn_gate_b, L0_ffn_w1, L0_ffn_w2, L1_attn_wq, L1_attn_wk_down, L1_attn_wv_down, L1_attn_wk_up, L1_attn_wv_up, L1_attn_wo, L1_ffn_gate_w, L1_ffn_gate_b, L1_ffn_w1, L1_ffn_b1, L1_ffn_w3, L1_ffn_b3, L1_ffn_w2, L1_ffn_b2, L1_ffn_ws1, L1_ffn_bs1, L1_ffn_ws3, L1_ffn_bs3, L1_ffn_ws2, L1_ffn_bs2):

    def _L0_attn_ref(x, w_cq, g_qnorm, w_dq_nope, w_dq_rope, w_ckv, g_kvnorm, w_dk_nope, w_dv, w_krope, w_imp, w_selk, w_selv, w_wink, w_winv, w_gate, w_proj):
        import jax, jax.numpy as jnp
        import numpy as np
        import math
        N_HEAD = 16
        V_HEAD = 32
        NOPE = 32
        ROPE_D = 64
        KEEP = 32
        EPS = 1e-06

        def _freqs(T, dim=ROPE_D, theta=10000.0):
            f = 1.0 / theta ** (jnp.arange(0, dim, 2, dtype=jnp.float32) / dim)
            t = jnp.arange(T, dtype=jnp.float32)
            a = jnp.outer(t, f)
            return (jnp.cos(a), jnp.sin(a))

        def _rope(x, cos, sin):
            S = x.shape[-2]
            c = cos[:S][None, None]
            s = sin[:S][None, None]
            x1, x2 = jnp.split(x, 2, axis=-1)
            return jnp.concatenate([x1 * c - x2 * s, x1 * s + x2 * c], axis=-1)

        def _rms(x, g, eps=EPS):
            return x * jax.lax.rsqrt(jnp.mean(x * x, axis=-1, keepdims=True) + eps) * g

        def _attn(q, k, v, causal):
            scale = 1.0 / math.sqrt(q.shape[-1])
            s = jnp.einsum('bhqd,bhkd->bhqk', q, k) * scale
            if causal:
                Tq, Tk = (s.shape[-2], s.shape[-1])
                mask = jnp.tril(jnp.ones((Tq, Tk), dtype=bool))
                s = jnp.where(mask, s, jnp.finfo(s.dtype).min)
            return jnp.einsum('bhqk,bhkd->bhqd', jax.nn.softmax(s, axis=-1), v)

        def _forward(x, w_cq, g_qnorm, w_dq_nope, w_dq_rope, w_ckv, g_kvnorm, w_dk_nope, w_dv, w_krope, w_imp, w_selk, w_selv, w_wink, w_winv, w_gate, w_proj):
            B, T, C = x.shape
            cos, sin = _freqs(T)
            nq = _rms(x @ w_cq, g_qnorm)
            q_nope = (nq @ w_dq_nope).reshape(B, T, N_HEAD, NOPE).transpose(0, 2, 1, 3)
            q_rope = (nq @ w_dq_rope).reshape(B, T, N_HEAD, ROPE_D).transpose(0, 2, 1, 3)
            q_rope = _rope(q_rope, cos, sin)
            q = jnp.concatenate([q_nope, q_rope], axis=-1)
            gate = jax.nn.softmax((x @ w_gate).mean(axis=1), axis=-1)
            ckv = _rms(x @ w_ckv, g_kvnorm)
            k_nope = (ckv @ w_dk_nope).reshape(B, T, N_HEAD, NOPE).transpose(0, 2, 1, 3)
            v1 = (ckv @ w_dv).reshape(B, T, N_HEAD, V_HEAD).transpose(0, 2, 1, 3)
            k_rope = (x @ w_krope).reshape(B, T, 1, ROPE_D).transpose(0, 2, 1, 3) / N_HEAD
            k_rope = _rope(k_rope, cos, sin)
            k1 = jnp.concatenate([k_nope, jnp.broadcast_to(k_rope, (B, N_HEAD, T, ROPE_D))], axis=-1)
            scores = (x @ w_imp)[..., 0]
            _, idx = jax.lax.top_k(scores, KEEP)
            idx = jnp.sort(idx, axis=1)
            sel = jnp.take_along_axis(x, idx[:, :, None], axis=1)
            ks = (sel @ w_selk).reshape(B, KEEP, N_HEAD, NOPE + ROPE_D).transpose(0, 2, 1, 3)
            vs = (sel @ w_selv).reshape(B, KEEP, N_HEAD, V_HEAD).transpose(0, 2, 1, 3)
            ks = jnp.concatenate([ks[..., :NOPE], _rope(ks[..., NOPE:], cos, sin)], axis=-1)
            kw = (x @ w_wink).reshape(B, T, N_HEAD, NOPE + ROPE_D).transpose(0, 2, 1, 3)
            vw = (x @ w_winv).reshape(B, T, N_HEAD, V_HEAD).transpose(0, 2, 1, 3)
            kw = jnp.concatenate([kw[..., :NOPE], _rope(kw[..., NOPE:], cos, sin)], axis=-1)
            a1 = _attn(q, k1, v1, causal=True)
            a2 = _attn(q, ks, vs, causal=False)
            a3 = _attn(q, kw, vw, causal=True)
            g = gate[:, :, None, None, None]
            out = g[:, 0] * a1 + g[:, 1] * a2 + g[:, 2] * a3
            out = out.transpose(0, 2, 1, 3).reshape(B, T, N_HEAD * V_HEAD)
            return out @ w_proj
        return _forward(x, w_cq, g_qnorm, w_dq_nope, w_dq_rope, w_ckv, g_kvnorm, w_dk_nope, w_dv, w_krope, w_imp, w_selk, w_selv, w_wink, w_winv, w_gate, w_proj)

    def _L0_ffn_ref(x, gate_w, gate_b, w1, w2):
        import jax, jax.numpy as jnp
        import numpy as np
        B, S, D, E, H, K = (64, 256, 128, 32, 512, 8)
        b, s, d = x.shape
        logits = jnp.einsum('bsd,ed->bse', x, gate_w) + gate_b
        probs = jax.nn.softmax(logits, axis=-2)
        vals_t, idx_t = jax.lax.top_k(probs.transpose(0, 2, 1), K)
        vals = vals_t.transpose(0, 2, 1)
        idx = idx_t.transpose(0, 2, 1)
        flat_idx = idx.reshape(b, K * E)
        tok = jnp.take_along_axis(x, flat_idx[:, :, None], axis=1)
        tok = tok.reshape(b, K, E, d)
        merged = jnp.einsum('bked,bke->bed', tok, vals)
        ones = jnp.ones(merged.shape[:-1] + (1,), merged.dtype)
        h = jnp.einsum('bei,eih->beh', jnp.concatenate([merged, ones], -1), w1)
        h = jax.nn.gelu(h, approximate=False)
        o = jnp.einsum('bej,ejo->beo', jnp.concatenate([h, ones], -1), w2)
        out_tok = jnp.einsum('beo,bke->bkeo', o, vals).reshape(b, K * E, d)
        out = jnp.zeros_like(x).at[jnp.arange(b)[:, None], flat_idx].add(out_tok)
        return out

    def _L1_attn_ref(x, wq, wk_down, wv_down, wk_up, wv_up, wo):
        import jax, jax.numpy as jnp
        import numpy as np
        D_MODEL, N_HEADS, N_KV, HEAD_DIM, D_LAT = (128, 8, 2, 128, 32)
        N_REP = N_HEADS // N_KV
        B, T = (2, 256)
        Bq, Tq, _ = x.shape
        scale = HEAD_DIM ** (-0.5)
        q = (x @ wq).reshape(Bq, Tq, N_KV, N_REP, HEAD_DIM)
        k_lat = (x @ wk_down).reshape(Bq, Tq, N_KV, D_LAT)
        v_lat = (x @ wv_down).reshape(Bq, Tq, N_KV, D_LAT)
        k = jnp.einsum('bkhl,ld->bkhd', k_lat, wk_up)
        v = jnp.einsum('bkhl,ld->bkhd', v_lat, wv_up)
        scores = jnp.einsum('bqhrd,bkhd->bhrqk', q, k) * scale
        causal = jnp.tril(jnp.ones((Tq, Tq), dtype=bool))
        scores = jnp.where(causal, scores, jnp.finfo(scores.dtype).min)
        probs = jax.nn.softmax(scores, axis=-1)
        y = jnp.einsum('bhrqk,bkhd->bqhrd', probs, v)
        y = y.reshape(Bq, Tq, N_HEADS * HEAD_DIM)
        return y @ wo

    def _L1_ffn_ref(x, gate_w, gate_b, w1, b1, w3, b3, w2, b2, ws1, bs1, ws3, bs3, ws2, bs2):
        import jax, jax.numpy as jnp
        import numpy as np
        DIM = 128
        INTER = 128
        E = 8
        TOPK = 2
        ROUTE_SCALE = 1.0
        SHARED_INTER = 256
        B, S = (4, 256)

        def _moe_forward(x, gate_w, gate_b, w1, b1, w3, b3, w2, b2, ws1, bs1, ws3, bs3, ws2, bs2):
            Bq, Sq, D = x.shape
            xt = x.reshape(-1, D)
            logits = (xt @ gate_w.T + gate_b).astype(jnp.float32)
            scores = jax.nn.softmax(logits, axis=-1)
            top_w, top_i = jax.lax.top_k(scores, TOPK)
            weights = (top_w * ROUTE_SCALE).astype(x.dtype)
            gate_dense = jnp.sum(jax.nn.one_hot(top_i, E, dtype=x.dtype) * weights[..., None], axis=1)

            def expert(w1e, b1e, w3e, b3e, w2e, b2e):
                h = jax.nn.silu(xt @ w1e.T + b1e) * (xt @ w3e.T + b3e)
                return h @ w2e.T + b2e
            outs = jax.vmap(expert)(w1, b1, w3, b3, w2, b2)
            y = jnp.einsum('etd,te->td', outs, gate_dense)
            z = jax.nn.silu(xt @ ws1.T + bs1) * (xt @ ws3.T + bs3) @ ws2.T + bs2
            return (y + z).reshape(Bq, Sq, D)
        return _moe_forward(x, gate_w, gate_b, w1, b1, w3, b3, w2, b2, ws1, bs1, ws3, bs3, ws2, bs2)
    x = L0_attn_x
    x = x + _layernorm(_L0_attn_ref(_layernorm(x, axis=-1), L0_attn_w_cq, L0_attn_g_qnorm, L0_attn_w_dq_nope, L0_attn_w_dq_rope, L0_attn_w_ckv, L0_attn_g_kvnorm, L0_attn_w_dk_nope, L0_attn_w_dv, L0_attn_w_krope, L0_attn_w_imp, L0_attn_w_selk, L0_attn_w_selv, L0_attn_w_wink, L0_attn_w_winv, L0_attn_w_gate, L0_attn_w_proj), axis=-1)
    x = x + _layernorm(_L0_ffn_ref(_layernorm(x, axis=-1), L0_ffn_gate_w, L0_ffn_gate_b, L0_ffn_w1, L0_ffn_w2), axis=-1)
    x = x + _layernorm(_L1_attn_ref(_layernorm(x, axis=-1), L1_attn_wq, L1_attn_wk_down, L1_attn_wv_down, L1_attn_wk_up, L1_attn_wv_up, L1_attn_wo), axis=-1)
    x = x + _layernorm(_L1_ffn_ref(_layernorm(x, axis=-1), L1_ffn_gate_w, L1_ffn_gate_b, L1_ffn_w1, L1_ffn_b1, L1_ffn_w3, L1_ffn_b3, L1_ffn_w2, L1_ffn_b2, L1_ffn_ws1, L1_ffn_bs1, L1_ffn_ws3, L1_ffn_bs3, L1_ffn_ws2, L1_ffn_bs2), axis=-1)
    return x

_drawn_inputs = setup_inputs


def setup_inputs(seed=0):
    import zlib

    import numpy as np

    out = dict(_drawn_inputs(seed))
    spreads = {'L0_attn_g_qnorm': (1.0, 0.6),
     'L0_attn_g_kvnorm': (1.0, 0.2),
     'L0_ffn_gate_b': (0.0, 2.0),
     'L1_ffn_gate_b': (0.0, 0.1),
     'L1_ffn_b1': (0.0, 0.8),
     'L1_ffn_b3': (0.0, 0.8),
     'L1_ffn_b2': (0.0, 0.475),
     'L1_ffn_bs1': (0.0, 1.515),
     'L1_ffn_bs3': (0.0, 1.272),
     'L1_ffn_bs2': (0.0, 0.1)}
    factors = {'L0_attn_w_dk_nope': 3.586,
     'L0_attn_w_krope': 8.0,
     'L0_attn_w_gate': 4.077,
     'L1_ffn_w1': 7.175,
     'L1_ffn_w3': 7.056,
     'L1_ffn_w2': 6.569,
     'L1_ffn_ws1': 4.801,
     'L1_ffn_ws3': 4.846}
    for name, (base, spread) in spreads.items():
        noise = np.random.default_rng([zlib.crc32(name.encode()), seed]).standard_normal(out[name].shape)
        drawn = base * np.exp(spread * noise) if base else spread * noise
        out[name] = jnp.asarray(drawn.astype(out[name].dtype))
    for name, factor in factors.items():
        out[name] = (out[name] * factor).astype(out[name].dtype)
    return out
```

```python
from contextlib import ExitStack

import numpy as np
import concourse.bass as bass
from concourse import mybir
from concourse.alu_op_type import AluOpType as ALU

F32, BF16 = mybir.dt.float32, mybir.dt.bfloat16
ACT, AX = mybir.ActivationFunctionType, mybir.AxisListType
ds = bass.ds

B, T, C = 16, 256, 128
NT = B * T // 128
LN_EPS, RMS_EPS = 1e-5, 1e-6
H0, NOPE, ROPE, V0, KEEP = 16, 32, 64, 32, 32
HALF = ROPE // 2
QL, KVL = 96, 32
D0 = NOPE + ROPE
NEG = -1e30


def causal_constants():
    p = np.arange(128)
    ident = np.eye(128, dtype=np.float32)
    above = (p[None, :] > p[:, None])
    mask = np.tile(np.where(above, NEG, 0.0).astype(np.float32), (1, 4))
    s = np.arange(T)
    before = np.stack([(s[None, :] < (p[:, None] + 128 * t)) for t in range(2)], 1).astype(np.float32)
    upper = (p[:, None] < p[None, :]).astype(np.float32)
    iota = np.tile(np.arange(KEEP, dtype=np.float32), (128, 1))
    f = (1.0 / np.float32(10000.0) ** (np.arange(0, ROPE, 2, dtype=np.float32) / np.float32(ROPE))).astype(np.float32)
    a = np.outer(np.arange(T, dtype=np.float32), f).astype(np.float32)
    cos, sin = np.cos(a).astype(np.float32), np.sin(a).astype(np.float32)
    cT, sT = np.tile(cos.T, (4, 1)), np.tile(sin.T, (4, 1))
    rope_k = np.concatenate([cT, cT, -sT, sT], 1)
    rope_q = (rope_k * np.float32(D0 ** -0.5)).astype(np.float32)
    tok = np.concatenate([cos, cos, -sin, sin], 1).reshape(2, 128, 4 * HALF).transpose(1, 0, 2)
    rope_t = (tok / np.float32(H0)).astype(np.float32)
    return {
        "c_ident": ident, "c_before8": np.tile((np.arange(8)[None, :] < np.arange(8)[:, None]).astype(np.float32), (128, 1, 1)),
        "c_rows": np.repeat(np.eye(4, dtype=np.float32), 32, 1) * (p % 32 < B), "c_mask": mask, "c_before": before, "c_upper": upper, "c_iota": iota,
        "c_rope_k": rope_k.astype(np.float32), "c_rope_q": rope_q, "c_rope_t": rope_t,
    }


class Phase:

    def __init__(self, nc, stack, name):
        self.nc, self.stack, self.name = nc, stack, name

    def sb(self, name, shape, dt=F32):
        return self.stack.enter_context(self.nc.sbuf_tensor(f"{self.name}_{name}", shape, dt))

    def ps(self, name, shape, dt=F32):
        return self.stack.enter_context(self.nc.psum_tensor(f"{self.name}_{name}", shape, dt))


def count_in_register(engine, count):
    register = engine.alloc_register()
    engine.reg_mov(register, count)
    return register


def settle(engine, passed):
    engine.wait_ge(passed, 1)


def flat(ap):
    return ap.rearrange("p a b -> p (a b)")


def phase_weights(nc, sem, io, g):
    with ExitStack() as stack:
        ph = Phase(nc, stack, "wts")
        wqT = ph.sb("wqT", [128, 4, QL])
        wkd = ph.sb("wkd", [128, 4, 128])
        ckvT = ph.sb("ckvT", [KVL, C])
        wdv = ph.sb("wdv", [KVL, 512])
        gq = ph.sb("gq", [QL, 1])
        gkv = ph.sb("gkv", [KVL, 1])
        ps = ph.ps("ps", [128, 2, 512])
        loaded, resident = sem("wts_loaded"), sem("wts_resident")
        scaled, dv_scaled, prod, done = sem("wts_scaled"), sem("wts_dv_scaled"), sem("wts_prod"), sem("wts_done")
        with nc.Block() as block:
            @block.sync
            def _(sp):
                for dst, src in ((wqT, "w_dq_nopeT"), (wkd, "w_dk_diag"), (ckvT, "w_ckvT"), (wdv, "w_dv"),
                                 (gq, "g_q"), (gkv, "g_kv")):
                    sp.dma_start(dst[:], io[src]).then_inc(loaded, 16)
                for dst, src in ((g["resid"], "x"), (g["w_q"][:, 0:3], "w_q"), (g["w_val"][:, 1, :], "w_winv"),
                                 (g["ident"], "c_ident")):
                    sp.dma_start(dst[:] if src in ("x", "c_ident") else dst, io[src]).then_inc(resident, 16)
                sp.dma_start(g["kv_scale"][96:128, :], io["g_kv"]).then_inc(resident, 16)
                sp.wait_ge(resident, 16 * 5)

            @block.gpsimd
            def _(pool):
                nc.gpsimd.memset(g["kv_scale"][0:96, :], 1.0).then_inc(scaled, 1)

            @block.vector
            def _(dve):
                dve.wait_ge(loaded, 16 * 6)
                nc.vector.tensor_scalar(wdv[:], wdv[:], gkv[:], None, ALU.mult).then_inc(dv_scaled, 1)
                dve.wait_ge(resident, 16 * 5)
                dve.wait_ge(prod, 2)
                nc.vector.tensor_scalar(g["w_q"][:, 3].rearrange("p g m -> p (g m)"), ps[0:QL, 0, :], gq[:], None,
                                        ALU.mult).then_inc(done, 1)
                wq3 = g["w_q"][:, 0:3].rearrange("p a g m -> p (a g m)")
                nc.vector.tensor_scalar(wq3, wq3, gq[:], None, ALU.mult).then_inc(done, 1)
                nc.vector.tensor_copy(g["w_val"][:, 0, :], ps[:, 1, :]).then_inc(done, 1)
                dve.wait_ge(done, 3)
                nc.vector.tensor_copy(g["ident_b"][:], g["ident"][:]).then_inc(done, 1)

            @block.tensor
            def _(pe):
                pe.wait_ge(loaded, 16 * 6)
                for k in range(4):
                    last = nc.tensor.matmul(ps[0:QL, 0, 128 * k:128 * k + 128], wqT[:, k, :], wkd[:, k, :],
                                            start=True, stop=True)
                last.then_inc(prod, 1)
                pe.wait_ge(dv_scaled, 1)
                nc.tensor.matmul(ps[:, 1, :], ckvT[:], wdv[:], start=True, stop=True).then_inc(prod, 1)


def phase_select(nc, sem, io, g):
    resid, ident = g["resid"], g["ident"]
    with ExitStack() as stack:
        ph = Phase(nc, stack, "sel")
        stats = ph.sb("stats", [128, 8, 6])
        mv = ph.sb("mv", [128, 8, 2])
        var = ph.sb("var", [128, 8])
        rstd = ph.sb("rstd", [128, 8])
        halfneg = ph.sb("halfneg", [128, 8])
        eps = ph.sb("eps", [128, 8])
        xn = ph.sb("xn", [128, 8, C])
        xTq = ph.sb("xTq", [C, 8, 128])
        w_imp = ph.sb("w_imp", [C, 128])
        before = ph.sb("before", [128, 2, T])
        upper = ph.sb("upper", [128, 128])
        upper_b = ph.sb("upper_b", [128, 128], BF16)
        ones_b = ph.sb("ones_b", [128, 128], BF16)
        iota = ph.sb("iota", [128, KEEP])
        score = ph.sb("score", [128, 8])
        junk = ph.sb("junk", [128, 2, T])
        rank_gt = ph.sb("rank_gt", [128, 8])
        rank_eq = ph.sb("rank_eq", [128, 8])
        rank = ph.sb("rank", [128, 8])
        kept = ph.sb("kept", [128, 8])
        kept_b = ph.sb("kept_b", [128, 8], BF16)
        place = ph.sb("place", [128, 8])
        onehot = ph.sb("onehot", [128, 8, KEEP + 1])
        psT = ph.ps("psT", [128, 8, 128])
        psS = ph.ps("psS", [128, 4, T])
        psP = ph.ps("psP", [128, 8])
        psX = ph.ps("psX", [128, 4, KEEP + 1])
        psG = ph.ps("psG", [128, 48])
        token_sum = ph.sb("token_sum", [C, B])
        g16 = ph.sb("g16", [16, 3])
        gmax = ph.sb("gmax", [16, 1])
        gsum = ph.sb("gsum", [16, 1])
        grec = ph.sb("grec", [16, 1])
        gdiag = ph.sb("gdiag", [16, 16, 3])
        w_gate = ph.sb("w_gate", [C, 3])
        ones16 = ph.sb("ones16", [16, 128])
        loaded, const, upper_ready = sem("sel_loaded"), sem("sel_const"), sem("sel_upper_ready")
        s_stats, s_mv, s_var, s_rstd, s_xn = (sem("sel_" + n) for n in ("stats", "mv", "var", "rstd", "xn"))
        s_psT, s_xT, s_stored, s_psS = (sem("sel_" + n) for n in ("psT", "xT", "stored", "psS"))
        s_score, s_counted, s_rank, s_kept, s_keptb = (sem("sel_" + n) for n in ("score", "counted", "rank", "kept", "keptb"))
        s_psP, s_place, s_onehot, s_psX, s_sel = (sem("sel_" + n) for n in ("psP", "place", "onehot", "psX", "sel"))
        s_gate = sem("sel_gate")
        with nc.Block() as block:
            @block.sync
            def _(sp):
                for dst, src in ((w_imp, "w_imp"), (before, "c_before"), (upper, "c_upper"), (iota, "c_iota"),
                                 (w_gate, "w_gate")):
                    sp.dma_start(dst[:], io[src]).then_inc(loaded, 16)
                with sp.Fori(0, 4) as q:
                    sp.wait_ge(s_xT, 2 * q + 2)
                    sp.dma_start(g["xT_all"][:, ds(1024 * q, 1024)], flat(xTq[:])).then_inc(s_stored, 16)
                sp.wait_ge(s_stored, 16 * 4)

            @block.gpsimd
            def _(pool):
                nc.gpsimd.memset(eps[:], LN_EPS)
                nc.gpsimd.memset(halfneg[:], -0.5).then_inc(const, 1)
                nc.gpsimd.memset(ones_b[:], 1.0).then_inc(const, 1)
                nc.gpsimd.memset(ones16[:], 1.0).then_inc(const, 1)
                nc.gpsimd.memset(onehot[:, :, KEEP:KEEP + 1], 1.0).then_inc(const, 1)
                pool.wait_ge(const, 4)
                with pool.Fori(0, 4) as q:
                    pool.wait_ge(s_mv, q + 1)
                    nc.gpsimd.tensor_tensor(var[:], mv[:, :, 1], eps[:], ALU.add).then_inc(s_var, 1)
                    pool.wait_ge(s_var, q + 1)
                    nc.gpsimd.tensor_tensor(rstd[:], var[:], halfneg[:], ALU.pow).then_inc(s_rstd, 1)

            @block.vector
            def _(dve):
                dve.wait_ge(loaded, 16 * 5)
                nc.vector.tensor_copy(upper_b[:], upper[:]).then_inc(upper_ready, 1)
                with dve.Fori(0, 4) as q:
                    for i in range(8):
                        last = nc.vector.bn_stats(stats[:, i, :], resid[:, ds(8 * q + i, 1), :])
                    last.then_inc(s_stats, 1)
                    settled = count_in_register(dve, q + 1)
                    settle(dve, loaded)
                    dve.wait_ge(s_stats, settled)
                    dve.wait_ge(s_rstd, q)
                    for i in range(8):
                        last = nc.vector.bn_aggr(mv[:, i, :], stats[:, i, :])
                    last.then_inc(s_mv, 1)
                    dve.wait_ge(s_rstd, q + 1)
                    dve.wait_ge(s_psX, q)
                    for i in range(8):
                        last = nc.vector.tensor_scalar(xn[:, i, :], resid[:, ds(8 * q + i, 1), :].rearrange("p o c -> p (o c)"),
                                                       mv[:, i, 0:1], rstd[:, i:i + 1], ALU.subtract, ALU.mult)
                    last.then_inc(s_xn, 1)
                    dve.wait_ge(s_psS, q + 1)
                    for i in range(8):
                        last = nc.vector.scalar_tensor_tensor(junk[:, i % 2, 0:128], psS[:, i // 2, 128 * (i % 2):128 * (i % 2) + 128],
                                                              1.0, ident[:], ALU.mult, ALU.mult, accum_out=score[:, i:i + 1])
                        last.then_inc(s_score, 1)
                        dve.wait_ge(s_score, 24 * q + i + 1)
                    for i in range(8):
                        nc.vector.tensor_scalar(junk[:, 0, :], psS[:, i // 2, :], score[:, i:i + 1], 0.0, ALU.is_gt, ALU.add,
                                                accum_out=rank_gt[:, i:i + 1]).then_inc(s_score, 1)
                        nc.vector.scalar_tensor_tensor(junk[:, 1, :], psS[:, i // 2, :], score[:, i:i + 1],
                                                       before[:, i % 2, :], ALU.is_equal, ALU.mult,
                                                       accum_out=rank_eq[:, i:i + 1]).then_inc(s_score, 1)
                        dve.wait_ge(s_score, 24 * q + 8 + 2 * i + 2)
                    nc.vector.tensor_tensor(rank[:], rank_gt[:], rank_eq[:], ALU.add).then_inc(s_rank, 1)
                    dve.wait_ge(s_rank, q + 1)
                    nc.vector.tensor_scalar(kept[:], rank[:], KEEP - 0.5, None, ALU.is_lt).then_inc(s_kept, 1)
                    dve.wait_ge(s_kept, q + 1)
                    nc.vector.tensor_copy(kept_b[:], kept[:]).then_inc(s_keptb, 1)
                    dve.wait_ge(s_psP, q + 1)
                    nc.vector.tensor_copy(place[:], psP[:]).then_inc(s_place, 1)
                    dve.wait_ge(s_place, q + 1)
                    for i in range(8):
                        last = nc.vector.tensor_scalar(onehot[:, i, 0:KEEP], iota[:], place[:, i:i + 1], kept[:, i:i + 1],
                                                       ALU.is_equal, ALU.mult)
                    last.then_inc(s_onehot, 1)
                dve.wait_ge(s_psX, 5)
                nc.vector.reduce_max(gmax[:], psG[0:16, 0:3], AX.X).then_inc(s_gate, 1)
                dve.wait_ge(s_gate, 1)
                nc.vector.tensor_scalar(g16[:], psG[0:16, 0:3], gmax[:], 1.0 / T, ALU.subtract, ALU.mult).then_inc(s_gate, 1)
                dve.wait_ge(s_gate, 3)
                nc.vector.reciprocal(grec[:], gsum[:]).then_inc(s_gate, 1)
                dve.wait_ge(s_gate, 4)
                nc.vector.tensor_scalar(g16[:], g16[:], grec[:], None, ALU.mult).then_inc(s_gate, 1)
                dve.wait_ge(s_gate, 5)
                for a in range(3):
                    last = nc.vector.tensor_scalar(gdiag[:, :, a], ident[0:16, 0:16], g16[:, a:a + 1], None, ALU.mult)
                last.then_inc(s_gate, 1)
                dve.wait_ge(s_psX, 6)
                nc.vector.tensor_copy(g["gates"][:].rearrange("p b a -> p (b a)"), psG[:]).then_inc(s_gate, 1)

            @block.scalar
            def _(act):
                with act.Fori(0, 4) as q:
                    act.wait_ge(s_stored, 16 * q)
                    for k in range(2):
                        act.wait_ge(s_psT, 2 * q + k + 1)
                        if k == 0:
                            act.wait_ge(s_psS, q)
                        nc.scalar.copy(flat(xTq[:, 4 * k:4 * k + 4, :]), flat(psT[:, 4 * k:4 * k + 4, :])).then_inc(s_xT, 1)
                    act.wait_ge(s_psX, q + 1)
                    nc.scalar.copy(g["sel"][:, ds(4 * q, 4), :], psX[:, :, 0:KEEP])
                    nc.scalar.copy(token_sum[:, ds(4 * q, 4)], psX[:, :, KEEP]).then_inc(s_sel, 1)
                act.wait_ge(s_gate, 2)
                nc.scalar.activation(g16[:], g16[:], ACT.Exp, accum_out=gsum[:]).then_inc(s_gate, 1)

            @block.tensor
            def _(pe):
                pe.wait_ge(loaded, 16 * 5)
                pe.wait_ge(const, 4)
                pe.wait_ge(upper_ready, 1)
                with pe.Fori(0, 4) as q:
                    pe.wait_ge(s_xn, q + 1)
                    for k in range(2):
                        for i in range(4 * k, 4 * k + 4):
                            last = nc.tensor.transpose(psT[:, i, :], xn[:, i, :], ident[:])
                        last.then_inc(s_psT, 1)
                    pe.wait_ge(s_xT, 2 * q + 2)
                    pe.wait_ge(s_score, 24 * q)
                    for i in range(4):
                        last = nc.tensor.matmul(psS[:, i, :], w_imp[:], flat(xTq[:, 2 * i:2 * i + 2, :]), start=True, stop=True)
                    last.then_inc(s_psS, 1)
                    pe.wait_ge(s_keptb, q + 1)
                    pe.wait_ge(s_place, q)
                    nc.tensor.matmul(psP[:], upper_b[:], kept_b[:], start=True, stop=False, skip_group_check=True)
                    nc.tensor.matmul(psP[:, 1::2], ones_b[:], kept_b[:, 0::2], start=False, stop=True,
                                     skip_group_check=True).then_inc(s_psP, 1)
                    pe.wait_ge(s_onehot, q + 1)
                    pe.wait_ge(s_sel, q)
                    for i in range(8):
                        last = nc.tensor.matmul(psX[:, i // 2, :], xn[:, i, :], onehot[:, i, :], start=(i % 2 == 0), stop=(i % 2 == 1))
                    last.then_inc(s_psX, 1)
                pe.wait_ge(s_sel, 4)
                nc.tensor.matmul(psG[0:16, 0:3], token_sum[:], w_gate[:], start=True, stop=True).then_inc(s_psX, 1)
                pe.wait_ge(s_gate, 6)
                nc.tensor.matmul(psG[:], ones16[:], gdiag[:].rearrange("p b a -> p (b a)"), start=True, stop=True).then_inc(s_psX, 1)


def phase_sel_kv(nc, sem, io, g):
    with ExitStack() as stack:
        ph = Phase(nc, stack, "skv")
        w_k = ph.sb("w_k", [C, 3, 4, 128])
        w_v = ph.sb("w_v", [C, 512])
        rope = ph.sb("rope", [128, 4, T])
        kst = ph.sb("kst", [128, B, 3, 4, KEEP])
        vst = ph.sb("vst", [128, 4, 512])
        tc = ph.sb("tc", [128, 2, 2, B, KEEP])
        tsn = ph.sb("tsn", [128, 2, 2, B, KEEP])
        ps = ph.ps("ps", [128, 2, 3, 512])
        psv = ph.ps("psv", [128, 2, 512])
        loaded = sem("skv_loaded")
        s_ps, s_nope, s_rot, s_sum, s_psv, s_v, s_out = (sem("skv_" + n) for n in ("ps", "nope", "rot", "sum", "psv", "v", "out"))
        with nc.Block() as block:
            @block.sync
            def _(sp):
                for dst, src in ((w_k, "w_selk"), (w_v, "w_selv")):
                    sp.dma_start(dst[:], io[src]).then_inc(loaded, 16)
                sp.dma_start(rope[:], io["c_rope_k"].rearrange("p (a t) -> p a t", a=4)).then_inc(loaded, 16)
                sp.wait_ge(s_v, 4)
                sp.dma_start(io["vs_dram"].rearrange("(q a) s n -> (a s) q n", q=4), vst[:]).then_inc(s_out, 16)
                sp.wait_ge(s_nope, 4)
                sp.wait_ge(s_sum, 4)
                for part in range(3):
                    for j in range(4):
                        sp.dma_start(io["ks_dram"][:, 32 * part:32 * part + 32, j].rearrange("b r g s -> r b g s"),
                                     kst[32 * j:32 * j + 32, :, part]).then_inc(s_out, 16)
                sp.wait_ge(s_out, 16 * 13)

            @block.tensor
            def _(pe):
                pe.wait_ge(loaded, 16 * 3)
                keys = g["sel"]
                for k in range(4):
                    if k >= 2:
                        pe.wait_ge(s_nope, k - 1)
                        pe.wait_ge(s_rot, k - 1)
                    for part in range(3):
                        last = nc.tensor.matmul(ps[:, k % 2, part, :], w_k[:, part, k, :], flat(keys[:]), start=True, stop=True)
                    last.then_inc(s_ps, 1)
                for k in range(4):
                    if k >= 2:
                        pe.wait_ge(s_v, k - 1)
                    nc.tensor.matmul(psv[:, k % 2, :], flat(keys[:, 4 * k:4 * k + 4, :]), w_v[:], start=True, stop=True).then_inc(s_psv, 1)

            @block.scalar
            def _(act):
                for k in range(4):
                    act.wait_ge(s_ps, k + 1)
                    nc.scalar.copy(kst[:, :, 0, k, :], ps[:, k % 2, 0, :].rearrange("p (b s) -> p b s", b=B)).then_inc(s_nope, 1)
                for k in range(4):
                    act.wait_ge(s_psv, k + 1)
                    nc.scalar.copy(vst[:, k, :], psv[:, k % 2, :]).then_inc(s_v, 1)

            @block.vector
            def _(dve):
                dve.wait_ge(loaded, 16 * 3)
                for k in range(4):
                    dve.wait_ge(s_ps, k + 1)
                    if k >= 2:
                        dve.wait_ge(s_sum, k - 1)
                    for half in range(2):
                        x = ps[:, k % 2, 1 + half, :].rearrange("p (b s) -> p b s", b=B)
                        y = ps[:, k % 2, 2 - half, :].rearrange("p (b s) -> p b s", b=B)
                        cosine = rope[:, half, 0:KEEP].unsqueeze(1).to_broadcast([128, B, KEEP])
                        sine = rope[:, 2 + half, 0:KEEP].unsqueeze(1).to_broadcast([128, B, KEEP])
                        nc.vector.tensor_tensor(tc[:, k % 2, half], x, cosine, ALU.mult)
                        last = nc.vector.tensor_tensor(tsn[:, k % 2, half], y, sine, ALU.mult)
                    last.then_inc(s_rot, 1)

            @block.gpsimd
            def _(pool):
                for k in range(4):
                    pool.wait_ge(s_rot, k + 1)
                    for half in range(2):
                        last = nc.gpsimd.tensor_tensor(kst[:, :, 1 + half, k, :], tc[:, k % 2, half], tsn[:, k % 2, half], ALU.add)
                    last.then_inc(s_sum, 1)


UNITS = 24
SLOTS = UNITS
GROUP_UNITS = 6

KIND = ["hi", "hi", "lo", "hi", "hi", "lo"]
HEADS = [(0,), (1,), (0, 1), (2,), (3,), (2, 3)]

PLAN = {
    0: ["tok"], 1: ["s2_01"], 3: ["krot_0"], 4: ["trq"], 5: ["krot_1", "kn_01"], 6: ["v_00", "s2_23"], 7: ["v_10", "s2t_0"],
    8: ["v_01", "s2t_1"], 9: ["v_11", "y"], 10: ["kn_23"], 12: ["qrot_0"], 13: ["p2_01", "p2_23"], 14: ["qn_0", "qrot_1"],
    15: ["qn_1"], 16: ["krot_2"], 17: ["qrot_2"], 18: ["krot_3"], 19: ["qrot_3"], 20: ["qn_2"], 21: ["qn_3"], 22: ["trk"],
}
PV_SLOT = {14: 0, 17: 1, 22: 2, 4: 3}
GATE_SLOT = 11
LAG, P_RING = 3, 4
V_ORDER = ["v_00", "v_10", "v_01", "v_11"]
ROT_ORDER = [n for s in sorted(PLAN) for n in PLAN[s] if n[1:4] == "rot"]
OF_BATCH = {"s2_01", "s2_23", "s2t_0", "s2t_1", "p2_01", "p2_23", *V_ORDER}
OF_BEFORE = {"y"}


def uses(mode):
    all_ = [(s, n) for s in range(SLOTS) for n in PLAN.get(s, [])]
    of_after = [(s, n) for s, n in all_ if n not in OF_BATCH | OF_BEFORE]
    return {
        "first": of_after,
        "second": [(s, n) for s, n in all_ if n not in OF_BEFORE],
        "body": all_,
        "last": [(s, n) for s, n in all_ if n in OF_BATCH | OF_BEFORE],
        "drain": [(s, n) for s, n in all_ if n in OF_BEFORE],
    }[mode]


class Turn:

    def __init__(self, mode, b):
        self.mode, self.b = mode, b
        self.attends = mode in ("second", "body", "last")
        self.projects = mode in ("first", "second", "body")
        self.follows = mode in ("body", "last", "drain")
        self.pb = 0 if mode == "first" else b + 1
        self.order = {n: i for i, (_, n) in enumerate(uses(mode))}
        self.order_before = {n: i for i, (_, n) in enumerate(uses("first" if mode == "second" else "body" if mode != "drain" else "last"))}
        first, second, body, last = (len(uses(m)) for m in ("first", "second", "body", "last"))
        assert body % 2 == 0
        self.start = {"first": 0, "second": first, "body": first + second, "last": first + second,
                      "drain": first + second + last - body}[mode]
        self.starts = self.start if mode in ("first", "second") else self.start + (b - 1) * body

    def before(self):
        return Turn({"second": "first", "drain": "last"}.get(self.mode, "body"), self.b - 1)

    def tasks(self, s):
        return [n for n in PLAN.get(s, []) if n in self.order]

    def bank(self, n):
        return (self.start + self.order[n]) % 2

    def full(self, n):
        return self.starts + (self.order[n] + 1)

    def full_before(self, n):
        return self.starts - (len(self.order_before) - self.order_before[n] - 1)

    def last_in_bank(self, n):
        at = self.order[n] - 2
        if at >= 0:
            return next(m for m, i in self.order.items() if i == at), self
        if self.mode == "first":
            return None
        at += len(self.order_before)
        return next(m for m, i in self.order_before.items() if i == at), self.before()

    def unit(self, u, lag=0):
        u = u - lag + 1
        return max(u, 0) if self.mode == "second" else self.b * UNITS + u

    def stage(self, s, lag):
        if s >= lag:
            return (s - lag, self) if self.attends else None
        return (s - lag + UNITS, self.before()) if self.follows else None

    def values_group(self, s):
        if s not in PV_SLOT:
            return None
        k = PV_SLOT[s]
        if k < 3:
            return (k, self) if self.attends else None
        return (k, self.before()) if self.follows else None


def phase_attend0(nc, sem, io, g):
    resid, ident, ident_b = g["resid"], g["ident"], g["ident_b"]
    w_q, w_val = g["w_q"], g["w_val"]
    with ExitStack() as stack:
        ph = Phase(nc, stack, "at0")
        w_tok = ph.sb("w_tok", [C, QL + KVL + ROPE])
        w_k = ph.sb("w_k", [C, 3, 4, 128])
        w_out = ph.sb("w_out", [128, 4, C])
        mask = ph.sb("mask", [128, 512])
        mask_b = ph.sb("mask_b", [128, 512], BF16)
        rope_q = ph.sb("rope_q", [128, 2, 512])
        rope_k = ph.sb("rope_k", [128, 2, 512])
        rope_t = ph.sb("rope_t", [128, 2, 128])
        xT = ph.sb("xT", [C, T])
        xTv = ph.sb("xTv", [C, T])
        sq = ph.sb("sq", [128, 2, QL])
        ss = ph.sb("ss", [128, 4])
        sse = ph.sb("sse", [128, 4])
        rs = ph.sb("rs", [128, 4])
        rv = ph.sb("rv", [128, 3])
        halfneg = ph.sb("halfneg", [128, 4])
        rms_eps = ph.sb("rms_eps", [128, 4])
        eps = ph.sb("eps", [128, 4])
        gate_pb = ph.sb("gate_pb", [128, 3])
        gate_b = ph.sb("gate_b", [128, 1])
        latent_sq = ph.sb("latent_sq", [128, 2, KVL])
        nq = ph.sb("nq", [128, 2, QL])
        k1tok = ph.sb("k1tok", [128, 2, 128])
        krt = ph.sb("krt", [128, 2, 2, ROPE])
        nqT = ph.sb("nqT", [QL, T])
        k1 = ph.sb("k1", [128, T])
        val = ph.sb("val", [128, 2, 2, 512])
        qst = ph.sb("qst", [128, 4, 4, T])
        kst = ph.sb("kst", [128, 3, 4, T])
        qT = ph.sb("qT", [128, 4, 4, T])
        kT = ph.sb("kT", [D0, 4, 4, T])
        rc = ph.sb("rc", [128, 2, 512])
        rsn = ph.sb("rsn", [128, 2, 512])
        ksb = ph.sb("ksb", [D0, 4, 4, KEEP])
        vsd = ph.sb("vsd", [128, 4, 128])
        s2T = ph.sb("s2T", [128, 4, T])
        p2 = ph.sb("p2", [128, 2, 512])
        m2 = ph.sb("m2", [128, 2, 16])
        z2 = ph.sb("z2", [128, 2, 16])
        r2 = ph.sb("r2", [128, 2, 16])
        p2T = ph.sb("p2T", [128, 4, T])
        p = ph.sb("p", [128, P_RING, 512])
        nm = ph.sb("nm", [128, P_RING, 4])
        z = ph.sb("z", [128, P_RING, 4])
        rz = ph.sb("rz", [128, P_RING, 4])
        pT = ph.sb("pT", [128, 2, 4, 2, 384])
        oT = ph.sb("oT", [128, 4, T])
        ystats = ph.sb("ystats", [128, 2, 6])
        ymv = ph.sb("ymv", [128, 2, 2])
        yvar = ph.sb("yvar", [128, 2])
        yrstd = ph.sb("yrstd", [128, 2])
        y = ph.sb("y", [128, 2 * C])
        yn = ph.sb("yn", [128, 2, C])
        psS = ph.ps("psS", [128, 3, 512])
        psT = ph.ps("psT", [128, 2, 512])
        psO = ph.ps("psO", [128, 2, T])
        psM = ph.ps("psM", [128, 2, 512])

        def S(n):
            return sem("at0_" + n)

        mask_ready, xTv_loaded = S("mask_ready"), S("xTv_loaded")
        loaded, const, xT_loaded, sel_loaded, vsd_loaded = S("loaded"), S("const"), S("xT_loaded"), S("sel_loaded"), S("vsd_loaded")
        scores_full, max_ready, exp_ready, recip_ready, norm_ready, pT_full = (S(n) for n in (
            "scores_full", "max_ready", "exp_ready", "recip_ready", "norm_ready", "pT_full"))
        evac_even, evac_odd = S("evac_even"), S("evac_odd")
        o_full, o_ready = S("o_full"), S("o_ready")
        misc_full = S("misc_full")
        sq_ready, sse_ready, rs_ready, rv_ready, latents_ready, kr_mul, kr_ready = (S(n) for n in (
            "sq_ready", "sse_ready", "rs_ready", "rv_ready", "latents_ready", "kr_mul", "kr_ready"))
        gate_ready = S("gate_ready")
        nqT_ready, k1_ready, val_ready = S("nqT_ready"), S("k1_ready"), S("val_ready")
        rot_mul, q_rot, k_rot, q_plain, k_plain = S("rot_mul"), S("q_rot"), S("k_rot"), S("q_plain"), S("k_plain")
        qk_loaded = [S("qk_loaded0"), S("qk_loaded1")]
        s2T_ready, m2_ready, s2_ready, e2_ready, z2_ready, r2_ready, p2_ready, p2T_ready = (S(n) for n in (
            "s2T_ready", "m2_ready", "s2_ready", "e2_ready", "z2_ready", "r2_ready", "p2_ready", "p2T_ready"))
        ystats_ready, ymv_ready, yvar_ready, yrstd_ready, yn_ready, resid_ready = (S(n) for n in (
            "ystats_ready", "ymv_ready", "yvar_ready", "yrstd_ready", "yn_ready", "resid_ready"))
        OWN_DMAS = 28

        def turns(engine, body):
            body(Turn("first", 0))
            body(Turn("second", 0))
            with engine.Fori(1, B - 1) as b:
                body(Turn("body", b))
            body(Turn("last", B - 1))
            body(Turn("drain", B))

        def misc(n, t, eng):
            eng.wait_ge(misc_full, t.full(n))
            return psM[:, t.bank(n), :]

        def pT_unused(u, t):
            k = u // 6 - 1
            return max(k, 0) if t.mode == "second" else 4 * t.b + k

        def evacuate(copy, u):
            k, (j0, *more) = u // 6, HEADS[u % 6]
            bank = psT[:, u % 2, :]
            if KIND[u % 6] == "hi":
                return copy(pT[:, k % 2, j0, :, 128:384], bank.rearrange("p (a x) -> p a x", a=2))
            return copy(pT[:, k % 2, j0:j0 + 2, :, 0:128], bank.rearrange("p (j a x) -> p j a x", j=2, a=2))

        def emptied(n, t):
            k = int(n[-1]) if n[-1].isdigit() else 0
            return {
                "tok": lambda: (kr_mul, t.pb + 1), "trq": lambda: (nqT_ready, t.pb + 1), "trk": lambda: (k1_ready, t.pb + 1),
                "qrot": lambda: (rot_mul, 8 * t.pb + ROT_ORDER.index(n) + 1), "krot": lambda: (rot_mul, 8 * t.pb + ROT_ORDER.index(n) + 1),
                "qn": lambda: (q_plain, 4 * t.pb + k + 1), "kn": lambda: (k_plain, 2 * t.pb + k // 2 + 1),
                "v": lambda: (val_ready, 4 * t.b + V_ORDER.index(n) + 1),
                "s2": lambda: (s2T_ready, 2 * t.b + k // 2 + 1), "s2t": lambda: (s2_ready, 2 * t.b + k + 1),
                "p2": lambda: (p2T_ready, 2 * t.b + k // 2 + 1), "y": lambda: (ystats_ready, t.b),
            }[n.split("_")[0]]()

        def bank_emptied(n, t):
            before = t.last_in_bank(n)
            return [] if before is None else [emptied(*before)]

        with nc.Block() as block:
            @block.sync
            def _(sp):
                for dst, src in ((w_tok, "w_tok"), (w_k, "w_wink"), (w_out, "w_proj"), (mask, "c_mask")):
                    sp.dma_start(dst[:], io[src]).then_inc(loaded, 16)
                for dst, src in ((rope_q, "c_rope_q"), (rope_k, "c_rope_k")):
                    sp.dma_start(dst[:], io[src].rearrange("p (a t) -> p a t", a=2)).then_inc(loaded, 16)
                sp.dma_start(rope_t[:], io["c_rope_t"]).then_inc(loaded, 16)

                def body(t):
                    if t.attends:
                        sp.wait_ge(const, 3)
                        if t.follows:
                            sp.wait_ge(o_full, 4 * t.b)
                        for j in range(4):
                            sp.dma_start(vsd[32 * j:32 * j + 32, :, 32 * j:32 * j + 32],
                                         io["vs_dram"][ds(t.b, 1)].rearrange("o s (g h v) -> h (o s) g v", g=4, h=4)[j]
                                         ).then_inc(vsd_loaded, 16)
                    if t.projects:
                        if t.attends:
                            sp.wait_ge(misc_full, t.full("s2_23"))
                        sp.dma_start(ksb[:], io["ks_dram"][ds(t.pb, 1)].rearrange("o r j g s -> (o r) j g s")).then_inc(sel_loaded, 16)
                    for pair in range(2):
                        if not t.projects:
                            break
                        settled = count_in_register(sp, 4 * t.pb + 2 * pair + 2)
                        settle(sp, loaded)
                        sp.wait_ge(q_rot, settled)
                        sp.wait_ge(k_rot, 4 * t.pb + 2 * pair + 2)
                        sp.wait_ge(q_plain, 4 * t.pb + 2 * pair + 2)
                        settled = count_in_register(sp, 2 * t.pb + pair + 1)
                        settle(sp, loaded)
                        sp.wait_ge(k_plain, settled)
                        if t.attends:
                            sp.wait_ge(scores_full, t.unit(12 * pair + 11))
                            if pair == 1:
                                sp.wait_ge(misc_full, t.full("s2_23"))
                        groups = slice(2 * pair, 2 * pair + 2)
                        for j in range(4):
                            for part in range(4):
                                sp.dma_start(qT[32 * part:32 * part + 32, j, groups, :],
                                             qst[32 * j:32 * j + 32, part, groups, :]).then_inc(qk_loaded[pair], 16)
                            for part in range(3):
                                sp.dma_start(kT[32 * part:32 * part + 32, j, groups, :],
                                             kst[32 * j:32 * j + 32, part, groups, :]).then_inc(qk_loaded[pair], 16)
                turns(sp, body)

            @block.gpsimd
            def _(pool):
                nc.gpsimd.memset(eps[:], LN_EPS)
                nc.gpsimd.memset(rms_eps[:], RMS_EPS)
                nc.gpsimd.memset(halfneg[:], -0.5).then_inc(const, 1)
                nc.gpsimd.memset(k1tok[:, :, 0:NOPE], 0.0).then_inc(const, 1)
                nc.gpsimd.memset(vsd[:], 0.0).then_inc(const, 1)
                pool.wait_ge(const, 3)

                def body(t):
                    for s in range(SLOTS):
                        for n in t.tasks(s):
                            if n == "tok":
                                pool.wait_ge(sq_ready, t.pb + 1)
                                nc.gpsimd.tensor_tensor(sse[:], ss[:], rms_eps[:], ALU.add).then_inc(sse_ready, 1)
                                pool.wait_ge(sse_ready, t.pb + 1)
                                pool.wait_ge(rv_ready, t.pb)
                                nc.gpsimd.tensor_tensor(rs[:], sse[:], halfneg[:], ALU.pow).then_inc(rs_ready, 1)
                            if n[:4] in ("qrot", "krot"):
                                k = int(n[-1])
                                done = q_rot if n[0] == "q" else k_rot
                                dst = (qst if n[0] == "q" else kst)[:, 1:3, k, :]
                                turn = ROT_ORDER.index(n)
                                pool.wait_ge(rot_mul, 8 * t.pb + turn + 1)
                                if t.attends:
                                    pool.wait_ge(qk_loaded[k // 2], 16 * OWN_DMAS * t.pb)
                                nc.gpsimd.tensor_tensor(dst, rc[:, turn % 2, :].rearrange("p (a t) -> p a t", a=2),
                                                        rsn[:, turn % 2, :].rearrange("p (a t) -> p a t", a=2), ALU.add).then_inc(done, 1)
                            if n == "y":
                                pool.wait_ge(ymv_ready, t.b)
                                nc.gpsimd.tensor_tensor(yvar[:], ymv[:, :, 1], eps[:, 0:2], ALU.add).then_inc(yvar_ready, 1)
                                pool.wait_ge(yvar_ready, t.b)
                                nc.gpsimd.tensor_tensor(yrstd[:], yvar[:], halfneg[:, 0:2], ALU.pow).then_inc(yrstd_ready, 1)
                        if t.stage(s, 1):
                            u, of = t.stage(s, 1)
                            r = u % P_RING
                            pool.wait_ge(recip_ready, of.unit(u))
                            n_ = 2 if KIND[u % 6] == "hi" else 4
                            pv = p[:, r, :].rearrange("p (a k) -> p a k", a=n_)
                            nc.gpsimd.tensor_tensor(pv, pv, rz[:, r, 0:n_].unsqueeze(2).to_broadcast([128, n_, 512 // n_]),
                                                    ALU.mult).then_inc(norm_ready, 1)
                turns(pool, body)

            @block.vector
            def _(dve):
                dve.wait_ge(loaded, 16 * 7)
                nc.vector.tensor_copy(mask_b[:], mask[:]).then_inc(mask_ready, 1)
                dve.wait_ge(const, 3)

                def task(n, t):
                    if n == "tok":
                        bank = misc(n, t, dve)[:, 0:384].rearrange("p (a c) -> p a c", a=2)
                        kr = bank[:, :, QL + KVL:]
                        dve.wait_ge(latents_ready, t.pb + 1)
                        nc.vector.tensor_tensor(krt[:, 0], kr, rope_t[:, :, 0:ROPE], ALU.mult)
                        swapped = krt[:, 1].rearrange("p a (h f) -> p a h f", h=2)
                        for half in range(2):
                            last = nc.vector.tensor_tensor(swapped[:, :, half, :], kr[:, :, HALF * (1 - half):HALF * (2 - half)],
                                                           rope_t[:, :, ROPE + HALF * half:ROPE + HALF * half + HALF], ALU.mult)
                        last.then_inc(kr_mul, 1)
                        dve.wait_ge(kr_mul, t.pb + 1)
                        nc.vector.tensor_tensor(k1tok[:, :, NOPE:D0], krt[:, 0], krt[:, 1], ALU.add).then_inc(kr_ready, 1)
                    if n[:4] in ("qrot", "krot"):
                        k = int(n[-1])
                        turn = ROT_ORDER.index(n)
                        table = rope_q if n[0] == "q" else rope_k
                        bank = misc(n, t, dve)
                        two_before = ROT_ORDER[turn - 2]
                        dve.wait_ge(q_rot if two_before[0] == "q" else k_rot, 4 * (t.pb - (turn < 2)) + (int(two_before[-1]) + 1)
                                    if t.attends or turn >= 2 else 0)
                        nc.vector.tensor_tensor(rc[:, turn % 2, :], bank, table[:, 0, :], ALU.mult)
                        for half in range(2):
                            last = nc.vector.tensor_tensor(rsn[:, turn % 2, T * half:T * half + T],
                                                           psM[:, t.bank(n), T * (1 - half):T * (2 - half)],
                                                           table[:, 1, T * half:T * half + T], ALU.mult)
                        last.then_inc(rot_mul, 1)
                    if n == "trk":
                        bank = misc(n, t, dve)
                        if t.attends:
                            dve.wait_ge(scores_full, t.unit(UNITS - 1))
                        nc.vector.tensor_scalar(k1[:], bank[:, 0:T], g["kv_scale"][:], None, ALU.mult).then_inc(k1_ready, 1)
                    if n[:4] == "s2t_":
                        i = int(n[-1])
                        bank = misc(n, t, dve).rearrange("p (h s) -> p h s", s=KEEP)
                        nc.vector.reduce_max(m2[:, i, :], bank, AX.X).then_inc(m2_ready, 1)
                        dve.wait_ge(m2_ready, 2 * t.b + i + 1)
                        dve.wait_ge(p2T_ready, 2 * t.b)
                        nc.vector.tensor_tensor(p2[:, i, :].rearrange("p (h s) -> p h s", s=KEEP), bank,
                                                m2[:, i, :].unsqueeze(2).to_broadcast([128, 16, KEEP]), ALU.subtract).then_inc(s2_ready, 1)
                    if n == "y":
                        bank = misc(n, t, dve)
                        dve.wait_ge(yn_ready, t.b - 1)
                        nc.vector.tensor_copy(y[:], bank[:, 0:2 * C])
                        for i in range(2):
                            last = nc.vector.bn_stats(ystats[:, i, :], bank[:, C * i:C * i + C])
                        last.then_inc(ystats_ready, 1)
                        settled = count_in_register(dve, t.b)
                        settle(dve, loaded)
                        dve.wait_ge(ystats_ready, settled)
                        dve.wait_ge(yvar_ready, t.b - 1)
                        for i in range(2):
                            last = nc.vector.bn_aggr(ymv[:, i, :], ystats[:, i, :])
                        last.then_inc(ymv_ready, 1)

                def add_y(b):
                    dve.wait_ge(yrstd_ready, b + 1)
                    dve.wait_ge(ystats_ready, b + 1)
                    for i in range(2):
                        last = nc.vector.tensor_scalar(yn[:, i, :], y[:, C * i:C * i + C], ymv[:, i, 0:1], yrstd[:, i:i + 1],
                                                       ALU.subtract, ALU.mult)
                    last.then_inc(yn_ready, 1)
                    dve.wait_ge(yn_ready, b + 1)
                    rows = resid[:, ds(2 * b, 2), :]
                    nc.vector.tensor_tensor(rows, rows, yn[:], ALU.add).then_inc(resid_ready, 1)
                    dve.wait_ge(resid_ready, b + 1)

                def p2_probs(t):
                    dve.wait_ge(e2_ready, t.b + 1)
                    nc.vector.reduce_sum(z2[:].rearrange("p t h -> p (t h)"), p2[:].rearrange("p t (h s) -> p (t h) s", s=KEEP),
                                         AX.X).then_inc(z2_ready, 1)
                    dve.wait_ge(z2_ready, t.b + 1)
                    nc.vector.reciprocal(r2[:], z2[:])
                    nc.vector.tensor_copy(gate_b[:], g["gates"][:, ds(t.b, 1), 1]).then_inc(r2_ready, 1)
                    dve.wait_ge(r2_ready, 2 * t.b + 1)
                    nc.vector.tensor_scalar(r2[:], r2[:], gate_b[:], None, ALU.mult).then_inc(r2_ready, 1)

                def p2_scaled(t):
                    dve.wait_ge(r2_ready, 2 * t.b + 2)
                    pv = p2[:].rearrange("p t (h s) -> p (t h) s", s=KEEP)
                    nc.vector.tensor_tensor(pv, pv, r2[:].rearrange("p t h -> p (t h)").unsqueeze(2).to_broadcast([128, 32, KEEP]),
                                            ALU.mult).then_inc(p2_ready, 1)

                def body(t):
                    for s in range(SLOTS):
                        if t.projects and s == SLOTS - 1:
                            task("trk", t)
                        if t.attends and s < UNITS:
                            n_ = 2 if KIND[s % 6] == "hi" else 4
                            dve.wait_ge(scores_full, t.unit(s))
                            nc.vector.tensor_reduce(nm[:, s % P_RING, 0:n_], psS[:, s % 3, :].rearrange("p (a k) -> p a k", a=n_), AX.X,
                                                    ALU.max, negate=True).then_inc(max_ready, 1)
                        if t.projects and s == 2:
                            task("tok", t)
                        for n in t.tasks(s):
                            if n not in ("tok", "trk"):
                                task(n, t)
                        if t.projects and s == GATE_SLOT - 3:
                            dve.wait_ge(rv_ready, t.pb)
                            nc.vector.tensor_copy(gate_pb[:], g["gates"][:, ds(t.pb, 1), :].rearrange("p o a -> p (o a)")
                                                  ).then_inc(gate_ready, 1)
                        if t.stage(s, 1):
                            u, of = t.stage(s, 1)
                            r = u % P_RING
                            n_ = 2 if KIND[u % 6] == "hi" else 4
                            dve.wait_ge(exp_ready, of.unit(u))
                            nc.vector.reciprocal(rz[:, r, 0:n_], z[:, r, 0:n_]).then_inc(recip_ready, 1)
                        if s == 10 and t.attends:
                            p2_probs(t)
                        if s == 11 and t.attends:
                            p2_scaled(t)
                        if s == 12 and t.follows:
                            add_y(t.b - 1)
                        if t.stage(s, LAG):
                            u, of = t.stage(s, LAG)
                            if u % 2 == 0:
                                dve.wait_ge(pT_full, of.unit(u))
                                dve.wait_ge(o_full, pT_unused(u, of))
                                evacuate(nc.vector.tensor_copy, u).then_inc(evac_even, 1)

                turns(dve, body)

            @block.scalar
            def _(act):
                act.wait_ge(loaded, 16 * 7)
                act.wait_ge(const, 3)


                def task(n, t):
                    if n == "tok":
                        bank = misc(n, t, act)[:, 0:384].rearrange("p (a c) -> p a c", a=2)
                        act.wait_ge(sse_ready, t.pb)
                        for i in range(2):
                            nc.scalar.activation(sq[:, i, :], bank[:, i, 0:QL], ACT.Square, scale=QL ** -0.5, accum_out=ss[:, 2 * i:2 * i + 1])
                            last = nc.scalar.activation(latent_sq[:, i, :], bank[:, i, QL:QL + KVL], ACT.Square, scale=KVL ** -0.5,
                                                        accum_out=ss[:, 2 * i + 1:2 * i + 2])
                        last.then_inc(sq_ready, 1)
                    if n == "latents":
                        bank = psM[:, t.bank("tok"), 0:384].rearrange("p (a c) -> p a c", a=2)
                        act.wait_ge(rs_ready, t.pb + 1)
                        if t.attends:
                            act.wait_ge(misc_full, t.full_before("trk"))
                        for i in range(2):
                            nc.scalar.activation(nq[:, i, :], bank[:, i, 0:QL], ACT.Copy, scale=rs[:, 2 * i:2 * i + 1])
                            last = nc.scalar.activation(k1tok[:, i, D0:128], bank[:, i, QL:QL + KVL], ACT.Copy, scale=rs[:, 2 * i + 1:2 * i + 2])
                        last.then_inc(latents_ready, 1)
                    if n == "trq":
                        bank = misc(n, t, act)
                        nc.scalar.copy(nqT[:], bank[0:QL, 0:T]).then_inc(nqT_ready, 1)
                    if n[:2] == "qn":
                        k = int(n[-1])
                        bank = misc(n, t, act)
                        if t.attends:
                            act.wait_ge(qk_loaded[k // 2], 16 * OWN_DMAS * t.pb)
                        nc.scalar.activation(qst[:, 0::3, k, :], bank.rearrange("p (a t) -> p a t", a=2), ACT.Copy,
                                             scale=D0 ** -0.5).then_inc(q_plain, 1)
                    if n[:2] == "kn":
                        pair = int(n[-2]) // 2
                        bank = misc(n, t, act)
                        if t.attends:
                            act.wait_ge(qk_loaded[pair], 16 * OWN_DMAS * t.pb)
                        nc.scalar.copy(kst[:, 0, 2 * pair:2 * pair + 2, :], bank.rearrange("p (a t) -> p a t", a=2)).then_inc(k_plain, 1)
                    if n[:2] == "v_":
                        a, i = int(n[2]), int(n[3])
                        bank = misc(n, t, act)
                        k = V_ORDER.index(n)
                        if k == 0:
                            if t.follows:
                                act.wait_ge(o_full, 4 * t.b)
                            act.wait_ge(rv_ready, t.b + 1)
                        scale = rv[:, i:i + 1] if a == 0 else rv[:, 2:3]
                        nc.scalar.activation(val[:, a, i, :], bank, ACT.Copy, scale=scale).then_inc(val_ready, 1)
                    if n == "rv":
                            act.wait_ge(gate_ready, t.pb + 1)
                            if t.attends:
                                act.wait_ge(val_ready, 4 * t.b + 4)
                            nc.scalar.copy(rv[:, 2:3], gate_pb[:, 2:3])
                            for x in range(2):
                                last = nc.scalar.activation(rv[:, x:x + 1], rs[:, 2 * x + 1:2 * x + 2], ACT.Copy,
                                                            scale=gate_pb[:, 0:1])
                            last.then_inc(rv_ready, 1)
                    if n in ("s2_01", "s2_23"):
                        i = int(n[-2]) // 2
                        bank = misc(n, t, act)
                        nc.scalar.copy(s2T[:, 2 * i:2 * i + 2, :], bank.rearrange("p (a t) -> p a t", a=2)).then_inc(s2T_ready, 1)
                    if n in ("p2_01", "p2_23"):
                        i = int(n[-2]) // 2
                        bank = misc(n, t, act)
                        act.wait_ge(o_full, 4 * t.b)
                        nc.scalar.copy(p2T[:, 2 * i:2 * i + 2, :], bank.rearrange("p (a t) -> p a t", a=2)).then_inc(p2T_ready, 1)

                def body(t):
                    if t.projects:
                        if t.attends:
                            act.wait_ge(misc_full, t.full_before("kn_23"))
                            act.wait_ge(misc_full, t.full_before("krot_3"))
                        nc.scalar.copy(xT[:], g["xT_all"][:, ds(T * t.pb, T)]).then_inc(xT_loaded, 1)
                    for s in range(SLOTS):
                        if t.attends and s < UNITS:
                            r, bank = s % P_RING, psS[:, s % 3, :]
                            n_ = 2 if KIND[s % 6] == "hi" else 4
                            w = 512 // n_
                            act.wait_ge(max_ready, t.unit(s))
                            act.wait_ge(pT_full, t.unit(s, P_RING))
                            for i in range(n_):
                                last = nc.scalar.activation(p[:, r, w * i:w * i + w], bank[:, w * i:w * i + w], ACT.Exp,
                                                            bias=nm[:, r, i:i + 1], accum_out=z[:, r, i:i + 1])
                            last.then_inc(exp_ready, 1)
                        for n in t.tasks(s):
                            task(n, t)
                        if t.projects and s == 1:
                            task("latents", t)
                        if t.attends and s == 3:
                            if t.follows:
                                act.wait_ge(val_ready, 4 * t.b)
                            nc.scalar.copy(xTv[:], g["xT_all"][:, ds(T * t.b, T)]).then_inc(xTv_loaded, 1)
                        if t.projects and s == GATE_SLOT:
                            task("rv", t)
                        if t.attends and s == 9:
                            act.wait_ge(s2_ready, 2 * t.b + 2)
                            nc.scalar.activation(p2[:], p2[:], ACT.Exp).then_inc(e2_ready, 1)
                        if t.stage(s, LAG):
                            u, of = t.stage(s, LAG)
                            if u % 2 == 1:
                                act.wait_ge(pT_full, of.unit(u))
                                act.wait_ge(o_full, pT_unused(u, of))
                                evacuate(nc.scalar.copy, u).then_inc(evac_odd, 1)
                        if t.values_group(s):
                            k, of = t.values_group(s)
                            act.wait_ge(o_full, 4 * of.b + k + 1)
                            if k == 0 and t.follows:
                                act.wait_ge(misc_full, t.full("y"))
                            nc.scalar.copy(oT[:, k, :], psO[:, k % 2, :]).then_inc(o_ready, 1)

                turns(act, body)

            @block.tensor
            def _(pe):
                pe.wait_ge(loaded, 16 * 7)
                pe.wait_ge(const, 3)
                pe.wait_ge(mask_ready, 1)

                def mm(out, lhsT, rhs, start=True, stop=True):
                    return nc.tensor.matmul(out, lhsT, rhs, start=start, stop=stop, skip_group_check=True)

                def task(n, t):
                    bank = psM[:, t.bank(n), :]
                    for by, count in bank_emptied(n, t):
                        pe.wait_ge(by, count)
                    if n == "tok":
                        pe.wait_ge(xT_loaded, t.pb + 1)
                        for i in range(2):
                            last = mm(bank[:, 192 * i:192 * i + 192], xT[:, 128 * i:128 * i + 128], w_tok[:])
                    if n == "trq":
                        pe.wait_ge(latents_ready, t.pb + 1)
                        for i in range(2):
                            last = nc.tensor.transpose(bank[0:QL, 128 * i:128 * i + 128], nq[:, i, :], ident[:])
                    if n == "trk":
                        pe.wait_ge(kr_ready, t.pb + 1)
                        pe.wait_ge(latents_ready, t.pb + 1)
                        for i in range(2):
                            last = nc.tensor.transpose(bank[:, 128 * i:128 * i + 128], k1tok[:, i, :], ident[:])
                    if n[:4] == "qrot":
                        pe.wait_ge(nqT_ready, t.pb + 1)
                        for half in range(2):
                            last = mm(bank[:, T * half:T * half + T], w_q[:, 1 + half, int(n[-1]), :], nqT[:])
                    if n[:2] == "qn":
                        for i, part in enumerate((0, 3)):
                            last = mm(bank[:, T * i:T * i + T], w_q[:, part, int(n[-1]), :], nqT[:])
                    if n[:4] == "krot":
                        for half in range(2):
                            last = mm(bank[:, T * half:T * half + T], w_k[:, 1 + half, int(n[-1]), :], xT[:])
                    if n[:2] == "kn":
                        for i in range(2):
                            last = mm(bank[:, T * i:T * i + T], w_k[:, 0, int(n[-2]) + i, :], xT[:])
                    if n[:2] == "v_":
                        a, i = int(n[2]), int(n[3])
                        pe.wait_ge(xTv_loaded, t.b + 1)
                        last = mm(bank, xTv[:, 128 * i:128 * i + 128], w_val[:, a, :])
                    if n in ("s2_01", "s2_23"):
                        pe.wait_ge(qk_loaded[int(n[-2]) // 2], 16 * OWN_DMAS * (t.b + 1))
                        if n == "s2_01":
                            pe.wait_ge(sel_loaded, 16 * (t.b + 1))
                        for i in range(2):
                            for j in range(4):
                                last = mm(bank[32 * j:32 * j + 32, T * i:T * i + T], ksb[:, j, int(n[-2]) + i, :],
                                          qT[0:D0, j, int(n[-2]) + i, :])
                    if n[:4] == "s2t_":
                        i = int(n[-1])
                        pe.wait_ge(s2T_ready, 2 * t.b + 2)
                        for k in range(4):
                            last = nc.tensor.transpose(bank[:, 128 * k:128 * k + 128], s2T[:, k, 128 * i:128 * i + 128], ident[:])
                    if n in ("p2_01", "p2_23"):
                        pe.wait_ge(p2_ready, t.b + 1)
                        for x in range(2):
                            for i in range(2):
                                k = int(n[-2]) + x
                                last = nc.tensor.transpose(bank[:, T * x + 128 * i:T * x + 128 * i + 128],
                                                           p2[:, i, 128 * k:128 * k + 128], ident[:])
                    if n == "y":
                        pe.wait_ge(o_ready, 4 * t.b)
                        for i in range(2):
                            for k in range(4):
                                last = mm(bank[:, C * i:C * i + C], oT[:, k, 128 * i:128 * i + 128], w_out[:, k, :], k == 0, k == 3)
                    last.then_inc(misc_full, 1)

                def scores(u, t):
                    k, r = u // 6, u % 3
                    bank = psS[:, r, :]
                    if u == 0:
                        pe.wait_ge(k1_ready, t.b + 1)
                    if u % 12 == 0:
                        pe.wait_ge(qk_loaded[u // 12], 16 * OWN_DMAS * (t.b + 1))
                    pe.wait_ge(exp_ready, t.unit(u, 3))
                    if KIND[u % 6] == "hi":
                        (j,) = HEADS[u % 6]
                        mm(bank[:, 0:256], qT[:, j, k, 128:256], k1[:], True, False)
                        mm(bank[:, 256:512], qT[0:D0, j, k, 128:256], kT[:, j, k, :], False, False)
                        last = mm(bank.rearrange("p (a x) -> p a x", a=2)[:, :, 128:256], ident_b[:], mask_b[:, 0:256], False, True)
                    else:
                        for i, j in enumerate(HEADS[u % 6]):
                            mm(bank[:, 256 * i:256 * i + 128], qT[:, j, k, 0:128], k1[:, 0:128], i == 0, False)
                            mm(bank[:, 256 * i + 128:256 * i + 256], qT[0:D0, j, k, 0:128], kT[:, j, k, 0:128], False, False)
                        last = mm(bank, ident_b[:], mask_b[:], False, True)
                    last.then_inc(scores_full, 1)

                def transposes(u, t):
                    k, r = u // 6, u % P_RING
                    pe.wait_ge(norm_ready, t.unit(u))
                    pe.wait_ge(evac_even if u % 2 == 0 else evac_odd, t.b * (UNITS // 2) + u // 2)
                    for i in range(4):
                        last = nc.tensor.transpose(psT[:, u % 2, 128 * i:128 * i + 128], p[:, r, 128 * i:128 * i + 128], ident[:])
                    last.then_inc(pT_full, 1)

                def values(k, t):
                    pe.wait_ge(evac_even, t.b * (UNITS // 2) + 3 * k + 3)
                    pe.wait_ge(evac_odd, t.b * (UNITS // 2) + 3 * k + 3)
                    pe.wait_ge(val_ready, 4 * (t.b + 1))
                    pe.wait_ge(p2T_ready, 2 * (t.b + 1))
                    pe.wait_ge(vsd_loaded, 64 * (t.b + 1))
                    pe.wait_ge(o_ready, 4 * t.b + k)
                    out = psO[:, k % 2, :]
                    mm(out, vsd[:, k, :], p2T[:, k, :], True, False)
                    for a in range(2):
                        for tile in range(2):
                            for j in range(4):
                                cols = slice(0, 256) if tile == 0 else slice(256, 384)
                                last = mm(out[32 * j:32 * j + 32, 128 * tile:256], val[:, a, tile, 128 * k + 32 * j:128 * k + 32 * j + 32],
                                          pT[:, k % 2, j, a, cols], False, a == 1 and tile == 1)
                    last.then_inc(o_full, 1)

                def body(t):
                    for s in range(SLOTS):
                        if t.attends:
                            scores(s, t)
                        for n in t.tasks(s):
                            task(n, t)
                        if t.stage(s, LAG):
                            transposes(*t.stage(s, LAG))
                        if t.values_group(s):
                            values(*t.values_group(s))

                turns(pe, body)


E0, HID0, TOP0 = 32, 512, 8


def phase_choose(nc, sem, io, g):
    resid, ident = g["resid"], g["ident"]
    with ExitStack() as stack:
        ph = Phase(nc, stack, "cho")
        gate_w = ph.sb("gate_w", [C, E0])
        gate_b = ph.sb("gate_b", [128, 1])
        stats = ph.sb("stats", [128, 8, 6])
        mv = ph.sb("mv", [128, 8, 2])
        var = ph.sb("var", [128, 8])
        rstd = ph.sb("rstd", [128, 8])
        halfneg = ph.sb("halfneg", [128, 8])
        eps = ph.sb("eps", [128, 8])
        xn = ph.sb("xn", [128, 8, C])
        xTq = ph.sb("xTq", [C, 8, 128])
        logit = ph.sb("logit", [128, T])
        prob = ph.sb("prob", [128, T])
        rest = ph.sb("rest", [128, T])
        pick = ph.sb("pick", [128, T])
        nmax = ph.sb("nmax", [128, 1])
        z = ph.sb("z", [128, 1])
        rz = ph.sb("rz", [128, 1])
        top = ph.sb("top", [128, TOP0])
        pickT = ph.sb("pickT", [128, 2, 128])
        psT = ph.ps("psT", [128, 8, 128])
        psL = ph.ps("psL", [128, T])
        psP = ph.ps("psP", [128, 2, 128])
        psM = ph.ps("psM", [C, 4, E0])

        def S(n):
            return sem("cho_" + n)

        (loaded, const, s_stats, s_mv, s_var, s_rstd, s_xn, s_psT, s_xT, s_psL, s_logit, s_nmax, s_exp, s_rz, s_prob, s_top,
         s_rest, s_pick, s_psP, s_pickT, s_psM, s_merged, s_pick_kept) = (S(n) for n in (
             "loaded", "const", "stats", "mv", "var", "rstd", "xn", "psT", "xT", "psL", "logit", "nmax", "exp", "rz", "prob",
             "top", "rest", "pick", "psP", "pickT", "psM", "merged", "pick_kept"))
        with nc.Block() as block:
            @block.sync
            def _(sp):
                sp.dma_start(gate_w[:], io["gate0_w"]).then_inc(loaded, 16)
                sp.dma_start(gate_b[:], io["gate0_b"]).then_inc(loaded, 16)

            @block.gpsimd
            def _(pool):
                nc.gpsimd.memset(eps[:], LN_EPS)
                nc.gpsimd.memset(halfneg[:], -0.5).then_inc(const, 1)
                pool.wait_ge(const, 1)
                with pool.Fori(0, 4) as q:
                    pool.wait_ge(s_mv, q + 1)
                    nc.gpsimd.tensor_tensor(var[:], mv[:, :, 1], eps[:], ALU.add).then_inc(s_var, 1)
                    pool.wait_ge(s_var, q + 1)
                    nc.gpsimd.tensor_tensor(rstd[:], var[:], halfneg[:], ALU.pow).then_inc(s_rstd, 1)

            @block.vector
            def _(dve):
                dve.wait_ge(loaded, 16 * 2)
                with dve.Fori(0, 4) as q:
                    for i in range(8):
                        last = nc.vector.bn_stats(stats[:, i, :], resid[:, ds(8 * q + i, 1), :])
                    last.then_inc(s_stats, 1)
                    settled = count_in_register(dve, q + 1)
                    settle(dve, loaded)
                    dve.wait_ge(s_stats, settled)
                    for i in range(8):
                        last = nc.vector.bn_aggr(mv[:, i, :], stats[:, i, :])
                    last.then_inc(s_mv, 1)
                    dve.wait_ge(s_rstd, q + 1)
                    dve.wait_ge(s_psM, q)
                    for i in range(8):
                        last = nc.vector.tensor_scalar(xn[:, i, :], resid[:, ds(8 * q + i, 1), :].rearrange("p o c -> p (o c)"),
                                                       mv[:, i, 0:1], rstd[:, i:i + 1], ALU.subtract, ALU.mult)
                    last.then_inc(s_xn, 1)
                    dve.wait_ge(s_psL, q + 1)
                    nc.vector.tensor_scalar(logit[:], psL[:], gate_b[:], None, ALU.add).then_inc(s_logit, 1)
                    dve.wait_ge(s_logit, q + 1)
                    nc.vector.tensor_reduce(nmax[:], logit[:], AX.X, ALU.max, negate=True).then_inc(s_nmax, 1)
                    dve.wait_ge(s_exp, q + 1)
                    nc.vector.reciprocal(rz[:], z[:]).then_inc(s_rz, 1)
                    dve.wait_ge(s_rz, q + 1)
                    nc.vector.tensor_scalar(prob[:], prob[:], rz[:], None, ALU.mult).then_inc(s_prob, 1)
                    settled = count_in_register(dve, q + 1)
                    settle(dve, loaded)
                    dve.wait_ge(s_prob, settled)
                    nc.vector.max(top[:], prob[:]).then_inc(s_top, 1)
                    settled = count_in_register(dve, q + 1)
                    settle(dve, loaded)
                    dve.wait_ge(s_top, settled)
                    nc.vector.match_replace(out=rest[:], in_to_replace=top[:], in_values=prob[:], imm_value=0.0).then_inc(s_rest, 1)
                    dve.wait_ge(s_rest, q + 1)
                    dve.wait_ge(s_pickT, q)
                    nc.vector.tensor_tensor(pick[:], prob[:], rest[:], ALU.subtract).then_inc(s_pick, 1)
                    dve.wait_ge(s_pick, q + 1)
                    nc.vector.tensor_copy(g["pick"][:, ds(q, 1), :].rearrange("p o t -> p (o t)"), pick[:]).then_inc(s_pick_kept, 1)

            @block.scalar
            def _(act):
                with act.Fori(0, 4) as q:
                    for k in range(2):
                        act.wait_ge(s_psT, 2 * q + k + 1)
                        nc.scalar.copy(flat(xTq[:, 4 * k:4 * k + 4, :]), flat(psT[:, 4 * k:4 * k + 4, :])).then_inc(s_xT, 1)
                    act.wait_ge(s_nmax, q + 1)
                    nc.scalar.activation(prob[:], logit[:], ACT.Exp, bias=nmax[:], accum_out=z[:]).then_inc(s_exp, 1)
                    act.wait_ge(s_psP, q + 1)
                    nc.scalar.copy(flat(pickT[:]), flat(psP[:])).then_inc(s_pickT, 1)
                    act.wait_ge(s_psM, q + 1)
                    nc.scalar.copy(g["merged"][:, :, ds(4 * q, 4)].rearrange("c e b -> c b e"), psM[:]).then_inc(s_merged, 1)

            @block.tensor
            def _(pe):
                pe.wait_ge(loaded, 16 * 2)
                with pe.Fori(0, 4) as q:
                    pe.wait_ge(s_xn, q + 1)
                    for k in range(2):
                        for i in range(4 * k, 4 * k + 4):
                            last = nc.tensor.transpose(psT[:, i, :], xn[:, i, :], ident[:])
                        last.then_inc(s_psT, 1)
                    pe.wait_ge(s_xT, 2 * q + 2)
                    for i in range(4):
                        last = nc.tensor.matmul(psL[32 * i:32 * i + 32, :], gate_w[:], flat(xTq[:, 2 * i:2 * i + 2, :]), start=True, stop=True)
                    last.then_inc(s_psL, 1)
                    pe.wait_ge(s_pick, q + 1)
                    for t in range(2):
                        last = nc.tensor.transpose(psP[:, t, :], pick[:, 128 * t:128 * t + 128], ident[:])
                    last.then_inc(s_psP, 1)
                    pe.wait_ge(s_pickT, q + 1)
                    pe.wait_ge(s_merged, q)
                    for i in range(4):
                        for t in range(2):
                            last = nc.tensor.matmul(psM[:, i, :], xn[:, 2 * i + t, :], pickT[:, t, 32 * i:32 * i + 32],
                                                    start=(t == 0), stop=(t == 1))
                    last.then_inc(s_psM, 1)


def phase_experts(nc, sem, io, g):
    ident = g["ident"]
    STEPS = E0 // 4
    with ExitStack() as stack:
        ph = Phase(nc, stack, "exp")
        merged = ph.sb("merged", [C, 2, 4, B])
        w1 = ph.sb("w1", [128, 2, 4, HID0])
        w1b = ph.sb("w1b", [4, 2, HID0])
        w2 = ph.sb("w2", [128, 2, 4, 4, C])
        w2b = ph.sb("w2b", [4, 2, C])
        rows = ph.sb("rows", [4, 128])
        h = ph.sb("h", [128, 2, HID0])
        hT = ph.sb("hT", [128, 2, 4, 128])
        o = ph.sb("o", [128, 2, C])
        psH = ph.ps("psH", [128, 2, HID0])
        psT = ph.ps("psT", [128, 2, 4, 128])
        psO = ph.ps("psO", [128, 2, 512])

        def S(n):
            return sem("exp_" + n)

        rows_loaded, w1_loaded, w2_loaded = S("rows_loaded"), [S("w1_loaded0"), S("w1_loaded1")], [S("w2_loaded0"), S("w2_loaded1")]
        s_merged, s_psH, s_h, s_psT, s_hT, s_psO, s_o = (S(n) for n in ("merged", "psH", "h", "psT", "hT", "psO", "o"))
        o_stored = [S("o_stored0"), S("o_stored1")]
        with nc.Block() as block:
            @block.sync
            def _(sp):
                def load(step, x, wait):
                    if wait:
                        sp.wait_ge(s_psH, step - 1)
                    sp.dma_start(w1[:, x], io["w1"][ds(4 * step, 4), 0:C, :].rearrange("e c h -> c e h")).then_inc(w1_loaded[x], 16)
                    sp.dma_start(w1b[:, x, :], io["w1"][ds(4 * step, 4), C, :]).then_inc(w1_loaded[x], 16)
                    if wait:
                        sp.wait_ge(s_psO, step - 1)
                    sp.dma_start(w2[:, x], io["w2"][ds(4 * step, 4), 0:HID0, :].rearrange("e (p k) c -> p e k c", k=4)
                                 ).then_inc(w2_loaded[x], 16)
                    sp.dma_start(w2b[:, x, :], io["w2"][ds(4 * step, 4), HID0, :]).then_inc(w2_loaded[x], 16)

                sp.dma_start(rows[:], io["c_rows"]).then_inc(rows_loaded, 16)
                load(0, 0, False)
                load(1, 1, False)
                with sp.Fori(2, STEPS - 1, 2) as i:
                    load(i, 0, True)
                    load(i + 1, 1, True)

            @block.gpsimd
            def _(pool):
                with pool.Fori(0, STEPS - 1, 2) as i:
                    for x in range(2):
                        pool.wait_ge(s_o, i + x + 1)
                        for j in range(4):
                            pool.dma_start(io["o_dram"][:, ds(4 * (i + x) + j, 1), :].rearrange("b o c -> (b o) c"),
                                           o[32 * j:32 * j + B, x, :]).then_inc(o_stored[x], 16)
                for x in range(2):
                    pool.wait_ge(o_stored[x], 64 * (STEPS // 2))

            @block.scalar
            def _(act):
                with act.Fori(0, STEPS - 1, 2) as i:
                    for x in range(2):
                        act.wait_ge(s_psH, i + x + 1)
                        act.wait_ge(s_psT, i)
                        nc.scalar.activation(h[:, x, :], psH[:, x, :], ACT.Gelu).then_inc(s_h, 1)

            @block.vector
            def _(dve):
                with dve.Fori(0, STEPS - 1, 2) as i:
                    dve.wait_ge(s_psH, i)
                    for x in range(2):
                        nc.vector.tensor_copy(merged[:, x], g["merged"][:, ds(4 * (i + x), 4), :]).then_inc(s_merged, 1)
                    for x in range(2):
                        dve.wait_ge(s_psT, i + x + 1)
                        dve.wait_ge(s_psO, i)
                        nc.vector.tensor_copy(flat(hT[:, x]), flat(psT[:, x])).then_inc(s_hT, 1)
                        dve.wait_ge(s_psO, i + x + 1)
                        dve.wait_ge(o_stored[x], 32 * i)
                        nc.vector.tensor_copy(o[:, x, :], psO[:, x, 0:C]).then_inc(s_o, 1)

            @block.tensor
            def _(pe):
                pe.wait_ge(rows_loaded, 16)
                with pe.Fori(0, STEPS - 1, 2) as i:
                    for x in range(2):
                        pe.wait_ge(w1_loaded[x], 16 * i + 32)
                        pe.wait_ge(s_merged, i + x + 1)
                        pe.wait_ge(s_h, i)
                        nc.tensor.matmul(psH[:, x, :], rows[:], w1b[:, x, :], start=True, stop=False, skip_group_check=True)
                        for j in range(4):
                            last = nc.tensor.matmul(psH[32 * j:32 * j + B, x, :], merged[:, x, j, :], w1[:, x, j, :],
                                                    start=False, stop=True, skip_group_check=True)
                        last.then_inc(s_psH, 1)
                        pe.wait_ge(s_h, i + x + 1)
                        pe.wait_ge(s_hT, i)
                        for k in range(4):
                            last = nc.tensor.transpose(psT[:, x, k, :], h[:, x, k::4], ident[:])
                        last.then_inc(s_psT, 1)
                        pe.wait_ge(w2_loaded[x], 16 * i + 32)
                        pe.wait_ge(s_hT, i + x + 1)
                        pe.wait_ge(s_o, i)
                        nc.tensor.matmul(psO[:, x, 0:C], rows[:], w2b[:, x, :], start=True, stop=False, skip_group_check=True)
                        for k in range(4):
                            for j in range(4):
                                last = nc.tensor.matmul(psO[32 * j:32 * j + B, x, 0:C], hT[:, x, k, 32 * j:32 * j + B],
                                                        w2[:, x, j, k, :], start=False, stop=(k == 3), skip_group_check=True)
                        last.then_inc(s_psO, 1)


def phase_spread(nc, sem, io, g):
    resid, ident = g["resid"], g["ident"]
    with ExitStack() as stack:
        ph = Phase(nc, stack, "spr")
        o = ph.sb("o", [128, 4, 4, C])
        pick = ph.sb("pick", [128, T])
        stats = ph.sb("stats", [128, 2, 8, 6])
        mv = ph.sb("mv", [128, 2, 8, 2])
        var = ph.sb("var", [128, 2, 8])
        rstd = ph.sb("rstd", [128, 2, 8])
        halfneg = ph.sb("halfneg", [128, 8])
        eps = ph.sb("eps", [128, 8])
        yn = ph.sb("yn", [128, 8, C])
        xn = ph.sb("xn", [128, 8, C])
        ow = ph.sb("ow", [128, 4, C])
        psY = ph.ps("psY", [128, 2, 4, C])
        psT = ph.ps("psT", [128, 8, 128])

        def S(n):
            return sem("spr_" + n)

        (o_loaded, const, s_zero, s_pick, s_psY, s_stats, s_mv, s_var, s_rstd, s_yn, s_resid, s_xn, s_psT, s_xT) = (S(n) for n in (
            "o_loaded", "const", "zero", "pick", "psY", "stats", "mv", "var", "rstd", "yn", "resid", "xn", "psT", "xT"))
        with nc.Block() as block:
            @block.sync
            def _(sp):
                sp.wait_ge(s_zero, 1)
                for b in range(4):
                    sp.dma_start(o[32 * b:32 * b + 32, :, b, :],
                                 io["o_dram"].rearrange("(q b) e c -> b e q c", q=4)[b]).then_inc(o_loaded, 16)

            @block.gpsimd
            def _(pool):
                nc.gpsimd.memset(eps[:], LN_EPS)
                nc.gpsimd.memset(halfneg[:], -0.5).then_inc(const, 1)
                pool.wait_ge(const, 1)
                with pool.Fori(0, 4) as q:
                    for k in range(2):
                        pool.wait_ge(s_mv, 2 * q + k + 1)
                        nc.gpsimd.tensor_tensor(var[:, k], mv[:, k, :, 1], eps[:], ALU.add).then_inc(s_var, 1)
                        pool.wait_ge(s_var, 2 * q + k + 1)
                        nc.gpsimd.tensor_tensor(rstd[:, k], var[:, k], halfneg[:], ALU.pow).then_inc(s_rstd, 1)

            @block.vector
            def _(dve):
                nc.vector.memset(o[:], 0.0).then_inc(s_zero, 1)
                dve.wait_ge(o_loaded, 64)
                with dve.Fori(0, 4) as q:
                    dve.wait_ge(s_psY, q)
                    nc.vector.tensor_copy(pick[:], g["pick"][:, ds(q, 1), :].rearrange("p o t -> p (o t)"))
                    nc.vector.tensor_copy(ow[:], o[:, ds(q, 1)].rearrange("p o b c -> p (o b) c")).then_inc(s_pick, 1)
                    dve.wait_ge(s_psY, q + 1)
                    for i in range(8):
                        last = nc.vector.bn_stats(stats[:, 0, i, :], psY[:, i % 2, i // 2, :])
                    last.then_inc(s_stats, 1)
                    settled = count_in_register(dve, 2 * q + 1)
                    settle(dve, o_loaded)
                    dve.wait_ge(s_stats, settled)
                    for i in range(8):
                        last = nc.vector.bn_aggr(mv[:, 0, i, :], stats[:, 0, i, :])
                    last.then_inc(s_mv, 1)
                    dve.wait_ge(s_rstd, 2 * q + 1)
                    for i in range(8):
                        last = nc.vector.tensor_scalar(yn[:, i, :], psY[:, i % 2, i // 2, :], mv[:, 0, i, 0:1], rstd[:, 0, i:i + 1],
                                                       ALU.subtract, ALU.mult)
                    last.then_inc(s_yn, 1)
                    dve.wait_ge(s_yn, q + 1)
                    rows = resid[:, ds(8 * q, 8), :]
                    nc.vector.tensor_tensor(rows, rows, yn[:], ALU.add).then_inc(s_resid, 1)
                    settled = count_in_register(dve, q + 1)
                    settle(dve, o_loaded)
                    dve.wait_ge(s_resid, settled)
                    for i in range(8):
                        last = nc.vector.bn_stats(stats[:, 1, i, :], resid[:, ds(8 * q + i, 1), :])
                    last.then_inc(s_stats, 1)
                    settled = count_in_register(dve, 2 * q + 2)
                    settle(dve, o_loaded)
                    dve.wait_ge(s_stats, settled)
                    for i in range(8):
                        last = nc.vector.bn_aggr(mv[:, 1, i, :], stats[:, 1, i, :])
                    last.then_inc(s_mv, 1)
                    dve.wait_ge(s_rstd, 2 * q + 2)
                    dve.wait_ge(s_psT, 2 * q)
                    for i in range(8):
                        last = nc.vector.tensor_scalar(xn[:, i, :], resid[:, ds(8 * q + i, 1), :].rearrange("p o c -> p (o c)"),
                                                       mv[:, 1, i, 0:1], rstd[:, 1, i:i + 1], ALU.subtract, ALU.mult)
                    last.then_inc(s_xn, 1)

            @block.scalar
            def _(act):
                with act.Fori(0, 4) as q:
                    for k in range(2):
                        act.wait_ge(s_psT, 2 * q + k + 1)
                        nc.scalar.copy(g["xT_all"][:, ds(1024 * q + 512 * k, 512)], flat(psT[:, 4 * k:4 * k + 4, :])).then_inc(s_xT, 1)

            @block.tensor
            def _(pe):
                with pe.Fori(0, 4) as q:
                    pe.wait_ge(s_pick, q + 1)
                    pe.wait_ge(s_yn, q)
                    for t in range(2):
                        last = nc.tensor.matmul(psY[:, t], pick[:, 128 * t:128 * t + 128], flat(ow[:]), start=True, stop=True)
                    last.then_inc(s_psY, 1)
                    pe.wait_ge(s_xn, q + 1)
                    pe.wait_ge(s_xT, 2 * q)
                    for k in range(2):
                        for i in range(4 * k, 4 * k + 4):
                            last = nc.tensor.transpose(psT[:, i, :], xn[:, i, :], ident[:])
                        last.then_inc(s_psT, 1)


KV1, REP1, HD1, LAT1 = 2, 4, 128, 32
UNITS1, SLOTS1, USES1_FIRST, USES1 = 12, 16, 5, 6
KIND1 = ["hi", "hi", "lo"]
PLAN1 = {1: ["k_0"], 2: ["q_0"], 4: ["k_1"], 6: ["q_1"], 8: ["v"], 15: ["y"]}
ORDER1 = ["k_0", "q_0", "k_1", "q_1", "v", "y"]


class Turn1:

    def __init__(self, n, half, attends=True, projects=True):
        self.n, self.half, self.attends, self.projects = n, half, attends, projects
        self.pn = n + 1 if attends else 0
        self.phalf = 1 - half if attends else 0

    def tasks(self, s):
        return [t for t in PLAN1.get(s, []) if (self.attends if t == "y" else self.projects)]

    def bank(self, task):
        return ORDER1.index(task) % 2 if not self.attends else (USES1_FIRST + self.at(task)) % 2

    def at(self, task):
        return ORDER1.index(task) if self.projects else 0

    def full(self, task):
        if not self.attends:
            return self.at(task) + 1
        return self.n * USES1 + (USES1_FIRST + self.at(task) + 1)

    def unit(self, u, lag=0):
        return self.n * UNITS1 + max(u - lag + 1, 0)


def phase_attend1(nc, sem, io, g):
    resid, ident, ident_b = g["resid"], g["ident"], g["ident_b"]
    with ExitStack() as stack:
        ph = Phase(nc, stack, "at1")
        wqT = ph.sb("wqT", [HD1, 8, C])
        wkuT = ph.sb("wkuT", [HD1, LAT1])
        wvuT = ph.sb("wvuT", [HD1, LAT1])
        wo = ph.sb("wo", [HD1, 8, C])
        w_k = ph.sb("w_k", [C, KV1, 128])
        w_v = ph.sb("w_v", [C, KV1 * LAT1])
        w_qk = ph.sb("w_qk", [C, KV1, 128])
        w_vo = ph.sb("w_vo", [128, KV1, C])
        mask = ph.sb("mask", [128, 512])
        mask_b = ph.sb("mask_b", [128, 512], BF16)
        xT = ph.sb("xT", [C, 2, T])
        q = ph.sb("q", [128, 2, 2, KV1, T])
        k = ph.sb("k", [128, 2, 2, KV1, REP1, T])
        val = ph.sb("val", [128, 2, 2, 2, KV1 * LAT1])
        p = ph.sb("p", [128, 3, 512])
        nm = ph.sb("nm", [128, 3, 4])
        z = ph.sb("z", [128, 3, 4])
        rz = ph.sb("rz", [128, 3, 4])
        pT = ph.sb("pT", [128, 2, REP1, 384])
        oT = ph.sb("oT", [128, 4, T])
        halfneg = ph.sb("halfneg", [128, 4])
        eps = ph.sb("eps", [128, 4])
        stats = ph.sb("stats", [128, 4, 6])
        mv = ph.sb("mv", [128, 4, 2])
        var = ph.sb("var", [128, 4])
        rstd = ph.sb("rstd", [128, 4])
        yn = ph.sb("yn", [128, 4, C])
        psS = ph.ps("psS", [128, 3, 512])
        psT = ph.ps("psT", [128, 2, 512])
        psO = ph.ps("psO", [128, 512])
        psM = ph.ps("psM", [128, 2, 512])

        def S(n):
            return sem("at1_" + n)

        (loaded, const, k_zero, mask_ready, wprod, w_ready, xT_loaded, scores_full, max_ready, exp_ready, recip_ready, norm_ready,
         pT_full, evac_even, evac_odd, o_full, o_ready, misc_full, k_ready, q_ready, v_ready, s_stats, s_mv, s_var, s_rstd, s_yn,
         s_resid) = (S(n) for n in (
             "loaded", "const", "k_zero", "mask_ready", "wprod", "w_ready", "xT_loaded", "scores_full", "max_ready", "exp_ready",
             "recip_ready", "norm_ready", "pT_full", "evac_even", "evac_odd", "o_full", "o_ready", "misc_full", "k_ready",
             "q_ready", "v_ready", "stats", "mv", "var", "rstd", "yn", "resid"))
        N_TURNS = B // 2

        def turns(engine, body):
            body(Turn1(0, 0, attends=False))
            with engine.Fori(0, N_TURNS // 2 - 1) as i:
                body(Turn1(2 * i, 0))
                body(Turn1(2 * i + 1, 1))
            body(Turn1(N_TURNS - 2, 0))
            body(Turn1(N_TURNS - 1, 1, projects=False))

        def pT_unused(u, t):
            return 4 * t.n + max(u // 3 - 1, 0)

        def evacuate(copy, u):
            grp = u // 3
            bank = psT[:, u % 2, :]
            if KIND1[u % 3] == "hi":
                heads = slice(2 * (u % 3), 2 * (u % 3) + 2)
                return copy(pT[:, grp % 2, heads, 128:384], bank.rearrange("p (r x) -> p r x", r=2))
            return copy(pT[:, grp % 2, :, 0:128], bank.rearrange("p (r x) -> p r x", r=4))

        with nc.Block() as block:
            @block.sync
            def _(sp):
                for dst, src in ((wqT, "wq1T"), (wkuT, "wk_upT"), (wvuT, "wv_upT"), (wo, "wo1"), (w_k, "wk_down4"),
                                 (w_v, "wv_down"), (mask, "c_mask")):
                    sp.dma_start(dst[:], io[src]).then_inc(loaded, 16)

                def body(t):
                    if t.projects:
                        sp.wait_ge(misc_full, t.n * USES1 + USES1_FIRST if t.attends else 0)
                        sp.dma_start(flat(xT[:]), g["xT_all"][:, ds(2 * T * t.pn, 2 * T)]).then_inc(xT_loaded, 16)

                turns(sp, body)

            @block.gpsimd
            def _(pool):
                nc.gpsimd.memset(eps[:], LN_EPS)
                nc.gpsimd.memset(halfneg[:], -0.5).then_inc(const, 1)
                pool.wait_ge(const, 1)

                def body(t):
                    if not t.attends:
                        return
                    for u in range(UNITS1):
                        r, n_ = u % 3, 2 if KIND1[u % 3] == "hi" else 4
                        pool.wait_ge(recip_ready, t.unit(u))
                        pv = p[:, r, :].rearrange("p (a k) -> p a k", a=n_)
                        nc.gpsimd.tensor_tensor(pv, pv, rz[:, r, 0:n_].unsqueeze(2).to_broadcast([128, n_, 512 // n_]),
                                                ALU.mult).then_inc(norm_ready, 1)
                    pool.wait_ge(s_mv, t.n + 1)
                    nc.gpsimd.tensor_tensor(var[:], mv[:, :, 1], eps[:], ALU.add).then_inc(s_var, 1)
                    pool.wait_ge(s_var, t.n + 1)
                    nc.gpsimd.tensor_tensor(rstd[:], var[:], halfneg[:], ALU.pow).then_inc(s_rstd, 1)

                turns(pool, body)

            @block.vector
            def _(dve):
                nc.vector.memset(k[:].rearrange("p a b c d e -> p (a b c d e)"), 0.0).then_inc(k_zero, 1)
                dve.wait_ge(loaded, 16 * 7)
                nc.vector.tensor_copy(mask_b[:], mask[:]).then_inc(mask_ready, 1)
                dve.wait_ge(wprod, 1)
                nc.vector.tensor_scalar(flat(w_qk[:]), psM[:, 0, 0:256], float(HD1) ** -0.5, None, ALU.mult)
                nc.vector.tensor_copy(flat(w_vo[:]), psM[:, 1, 0:256]).then_inc(w_ready, 1)

                def body(t):
                    for s in range(SLOTS1):
                        if t.attends and s < UNITS1:
                            r, n_ = s % 3, 2 if KIND1[s % 3] == "hi" else 4
                            dve.wait_ge(scores_full, t.unit(s))
                            nc.vector.tensor_reduce(nm[:, r, 0:n_], psS[:, r, :].rearrange("p (a k) -> p a k", a=n_), AX.X,
                                                    ALU.max, negate=True).then_inc(max_ready, 1)
                        for n in t.tasks(s):
                            bank = psM[:, t.bank(n), :]
                            if n[0] == "q":
                                dve.wait_ge(misc_full, t.full(n))
                                nc.vector.tensor_copy(q[:, t.phalf, int(n[-1])], bank.rearrange("p (v t) -> p v t", v=KV1)).then_inc(q_ready, 1)
                            if n == "v":
                                dve.wait_ge(misc_full, t.full(n))
                                nc.vector.tensor_copy(val[:, t.phalf], bank[:, 0:256].rearrange("p (b t l) -> p b t l", b=2, t=2)).then_inc(v_ready, 1)
                            if n == "y":
                                dve.wait_ge(misc_full, t.full(n))
                                for i in range(4):
                                    last = nc.vector.bn_stats(stats[:, i, :], bank[:, C * i:C * i + C])
                                last.then_inc(s_stats, 1)
                                settled = count_in_register(dve, t.n + 1)
                                settle(dve, loaded)
                                dve.wait_ge(s_stats, settled)
                                for i in range(4):
                                    last = nc.vector.bn_aggr(mv[:, i, :], stats[:, i, :])
                                last.then_inc(s_mv, 1)
                                dve.wait_ge(s_rstd, t.n + 1)
                                for i in range(4):
                                    last = nc.vector.tensor_scalar(yn[:, i, :], bank[:, C * i:C * i + C], mv[:, i, 0:1],
                                                                   rstd[:, i:i + 1], ALU.subtract, ALU.mult)
                                last.then_inc(s_yn, 1)
                                dve.wait_ge(s_yn, t.n + 1)
                                rows = resid[:, ds(4 * t.n, 4), :]
                                nc.vector.tensor_tensor(rows, rows, yn[:], ALU.add).then_inc(s_resid, 1)
                                dve.wait_ge(s_resid, t.n + 1)
                        if t.attends:
                            if 1 <= s < UNITS1 + 1:
                                u = s - 1
                                r, n_ = u % 3, 2 if KIND1[u % 3] == "hi" else 4
                                dve.wait_ge(exp_ready, t.unit(u))
                                nc.vector.reciprocal(rz[:, r, 0:n_], z[:, r, 0:n_]).then_inc(recip_ready, 1)
                            if 2 <= s < UNITS1 + 2 and s % 2 == 0:
                                dve.wait_ge(pT_full, t.unit(s - 2))
                                dve.wait_ge(o_full, pT_unused(s - 2, t))
                                evacuate(nc.vector.tensor_copy, s - 2).then_inc(evac_even, 1)

                turns(dve, body)

            @block.scalar
            def _(act):
                act.wait_ge(k_zero, 1)

                def body(t):
                    for s in range(SLOTS1):
                        if t.attends and s < UNITS1:
                            r, n_ = s % 3, 2 if KIND1[s % 3] == "hi" else 4
                            w = 512 // n_
                            act.wait_ge(max_ready, t.unit(s))
                            act.wait_ge(pT_full, t.unit(s, 3))
                            for i in range(n_):
                                last = nc.scalar.activation(p[:, r, w * i:w * i + w], psS[:, r, w * i:w * i + w], ACT.Exp,
                                                            bias=nm[:, r, i:i + 1], accum_out=z[:, r, i:i + 1])
                            last.then_inc(exp_ready, 1)
                        for n in t.tasks(s):
                            if n[0] == "k":
                                act.wait_ge(misc_full, t.full(n))
                                for r in range(REP1):
                                    rows = slice(32 * r, 32 * r + 32)
                                    last = nc.scalar.copy(k[rows, t.phalf, int(n[-1]), :, r, :],
                                                          psM[rows, t.bank(n), :].rearrange("p (v t) -> p v t", v=KV1))
                                last.then_inc(k_ready, 1)
                        if t.attends:
                            if 2 <= s < UNITS1 + 2 and s % 2 == 1:
                                act.wait_ge(pT_full, t.unit(s - 2))
                                act.wait_ge(o_full, pT_unused(s - 2, t))
                                evacuate(nc.scalar.copy, s - 2).then_inc(evac_odd, 1)
                            if s >= 5 and s % 3 == 2:
                                grp = (s - 5) // 3
                                act.wait_ge(o_full, 4 * t.n + grp + 1)
                                if grp == 0:
                                    act.wait_ge(s_yn, t.n)
                                nc.scalar.copy(oT[:, grp, :], psO[:, 0:T]).then_inc(o_ready, 1)

                turns(act, body)

            @block.tensor
            def _(pe):
                pe.wait_ge(loaded, 16 * 7)
                pe.wait_ge(mask_ready, 1)
                pe.wait_ge(k_zero, 1)

                def mm(out, lhsT, rhs, start=True, stop=True):
                    return nc.tensor.matmul(out, lhsT, rhs, start=start, stop=stop, skip_group_check=True)

                for h in range(8):
                    v, r = h // REP1, h % REP1
                    mm(psM[:, 0, 32 * h:32 * h + 32], wqT[:, h, :], wkuT[:])
                    last = mm(psM[32 * r:32 * r + 32, 1, C * v:C * v + C], wvuT[:], wo[:, h, :])
                last.then_inc(wprod, 1)
                pe.wait_ge(w_ready, 1)

                def task(n, t):
                    bank = psM[:, t.bank(n), :]
                    i = int(n[-1]) if n[-1].isdigit() else 0
                    if n == "k_0" and t.attends:
                        pe.wait_ge(v_ready, t.pn)
                        pe.wait_ge(q_ready, 2 * t.pn)
                    if n == "q_0" and t.attends:
                        pe.wait_ge(s_yn, t.n)
                        pe.wait_ge(v_ready, t.pn)
                    if n == "k_1":
                        pe.wait_ge(k_ready, 2 * t.pn + 1)
                    if n == "q_1":
                        pe.wait_ge(q_ready, 2 * t.pn + 1)
                    if n == "v":
                        pe.wait_ge(k_ready, 2 * t.pn + 2)
                    if n == "y":
                        if t.projects:
                            pe.wait_ge(q_ready, 2 * t.pn + 2)
                        else:
                            pe.wait_ge(v_ready, t.pn)
                            pe.wait_ge(q_ready, 2 * t.pn)
                            pe.wait_ge(s_yn, t.n)
                        pe.wait_ge(o_ready, 4 * t.n + 4)
                    if n == "k_0":
                        pe.wait_ge(xT_loaded, 16 * (t.pn + 1))
                    if n[0] == "k":
                        for v in range(KV1):
                            last = mm(bank[:, T * v:T * v + T], w_k[:, v, :], xT[:, i, :])
                    if n[0] == "q":
                        for v in range(KV1):
                            last = mm(bank[:, T * v:T * v + T], w_qk[:, v, :], xT[:, i, :])
                    if n == "v":
                        for b in range(2):
                            for tile in range(2):
                                last = mm(bank[:, 64 * (2 * b + tile):64 * (2 * b + tile) + 64],
                                          xT[:, b, 128 * tile:128 * tile + 128], w_v[:])
                    if n == "y":
                        for b in range(2):
                            for tile in range(2):
                                at = C * (2 * b + tile)
                                for v in range(KV1):
                                    last = mm(bank[:, at:at + C], oT[:, 2 * b + v, 128 * tile:128 * tile + 128], w_vo[:, v, :], v == 0, v == 1)
                    last.then_inc(misc_full, 1)

                def scores(u, t):
                    grp = u // 3
                    b, v = grp // 2, grp % 2
                    bank = psS[:, u % 3, :]
                    if u == 0:
                        pe.wait_ge(k_ready, 2 * (t.n + 1))
                        pe.wait_ge(q_ready, 2 * (t.n + 1))
                    pe.wait_ge(exp_ready, t.unit(u, 3))
                    if KIND1[u % 3] == "hi":
                        heads = slice(2 * (u % 3), 2 * (u % 3) + 2)
                        mm(bank, q[:, t.half, b, v, 128:256], k[:, t.half, b, v, heads, :], True, False)
                        last = mm(bank.rearrange("p (a x) -> p a x", a=2)[:, :, 128:256], ident_b[:], mask_b[:, 0:256], False, True)
                    else:
                        mm(bank, q[:, t.half, b, v, 0:128], k[:, t.half, b, v, :, 0:128], True, False)
                        last = mm(bank, ident_b[:], mask_b[:], False, True)
                    last.then_inc(scores_full, 1)

                def transposes(u, t):
                    pe.wait_ge(norm_ready, t.unit(u))
                    pe.wait_ge(evac_even if u % 2 == 0 else evac_odd, t.n * (UNITS1 // 2) + u // 2)
                    for i in range(4):
                        last = nc.tensor.transpose(psT[:, u % 2, 128 * i:128 * i + 128], p[:, u % 3, 128 * i:128 * i + 128], ident[:])
                    last.then_inc(pT_full, 1)

                def values(grp, t):
                    b, v = grp // 2, grp % 2
                    done = 3 * grp + 3
                    pe.wait_ge(evac_even, t.n * (UNITS1 // 2) + (done + 1) // 2)
                    pe.wait_ge(evac_odd, t.n * (UNITS1 // 2) + done // 2)
                    pe.wait_ge(v_ready, t.n + 1)
                    pe.wait_ge(o_ready, 4 * t.n + grp)
                    for tile in range(2):
                        for r in range(REP1):
                            cols = slice(0, 256) if tile == 0 else slice(256, 384)
                            last = mm(psO[32 * r:32 * r + 32, 128 * tile:256], val[:, t.half, b, tile, 32 * v:32 * v + 32],
                                      pT[:, grp % 2, r, cols], tile == 0, tile == 1)
                    last.then_inc(o_full, 1)

                def body(t):
                    for s in range(SLOTS1):
                        if t.attends and s < UNITS1:
                            scores(s, t)
                        if t.attends and s >= 5 and s % 3 == 2:
                            values((s - 5) // 3, t)
                        for n in t.tasks(s):
                            task(n, t)
                        if t.attends and 2 <= s < UNITS1 + 2:
                            transposes(s - 2, t)

                turns(pe, body)


E1, TOP1, INTER1 = 8, 2, 128


def phase_route(nc, sem, io, g):
    resid, ident = g["resid"], g["ident"]
    with ExitStack() as stack:
        ph = Phase(nc, stack, "rou")
        stats = ph.sb("stats", [128, 8, 6])
        mv = ph.sb("mv", [128, 8, 2])
        var = ph.sb("var", [128, 8])
        rstd = ph.sb("rstd", [128, 8])
        halfneg = ph.sb("halfneg", [128, 8])
        eps = ph.sb("eps", [128, 8])
        xn = ph.sb("xn", [128, 8, C])
        xTq = ph.sb("xTq", [C, 8, 128])
        gate_w = ph.sb("gate_w", [C, E1])
        gate_b = ph.sb("gate_b", [128, E1])
        before = ph.sb("before", [128, E1, E1])
        prob = ph.sb("prob", [128, NT, E1])
        m = ph.sb("m", [128, NT])
        z = ph.sb("z", [128, NT])
        higher = ph.sb("higher", [128, NT * E1, E1])
        equal = ph.sb("equal", [128, NT * E1, E1])
        rank = ph.sb("rank", [128, NT * E1])
        psT = ph.ps("psT", [128, 8, 128])
        psR = ph.ps("psR", [128, NT, E1])
        psG = ph.ps("psG", [E1 + 1, 2, 512])

        def S(n):
            return sem("rou_" + n)

        (loaded, const, s_stats, s_mv, s_var, s_rstd, s_xn, s_psT, s_xT, s_psR, s_step, s_exp, s_weights, s_psG, s_wT,
         s_kept) = (S(n) for n in ("loaded", "const", "stats", "mv", "var", "rstd", "xn", "psT", "xT", "psR", "step", "exp",
                                   "weights", "psG", "wT", "kept"))
        with nc.Block() as block:
            @block.sync
            def _(sp):
                for dst, src in ((gate_w, "gate1_w"), (gate_b, "gate1_b"), (before, "c_before8")):
                    sp.dma_start(dst[:], io[src]).then_inc(loaded, 16)
                with sp.Fori(0, 4) as q:
                    sp.wait_ge(s_xT, 2 * q + 2)
                    sp.dma_start(g["xT_all"][:, ds(1024 * q, 1024)], flat(xTq[:])).then_inc(s_kept, 16)
                sp.wait_ge(s_kept, 16 * 4)

            @block.gpsimd
            def _(pool):
                nc.gpsimd.memset(eps[:], LN_EPS)
                nc.gpsimd.memset(halfneg[:], -0.5).then_inc(const, 1)
                nc.gpsimd.memset(g["w_tok"][:, :, E1:E1 + 1], 1.0).then_inc(const, 1)
                pool.wait_ge(const, 2)
                with pool.Fori(0, 4) as q:
                    pool.wait_ge(s_mv, q + 1)
                    nc.gpsimd.tensor_tensor(var[:], mv[:, :, 1], eps[:], ALU.add).then_inc(s_var, 1)
                    pool.wait_ge(s_var, q + 1)
                    nc.gpsimd.tensor_tensor(rstd[:], var[:], halfneg[:], ALU.pow).then_inc(s_rstd, 1)

            @block.vector
            def _(dve):
                dve.wait_ge(loaded, 16 * 3)
                with dve.Fori(0, 4) as q:
                    for i in range(8):
                        last = nc.vector.bn_stats(stats[:, i, :], resid[:, ds(8 * q + i, 1), :])
                    last.then_inc(s_stats, 1)
                    settled = count_in_register(dve, q + 1)
                    settle(dve, loaded)
                    dve.wait_ge(s_stats, settled)
                    for i in range(8):
                        last = nc.vector.bn_aggr(mv[:, i, :], stats[:, i, :])
                    last.then_inc(s_mv, 1)
                    dve.wait_ge(s_rstd, q + 1)
                    dve.wait_ge(s_psT, 2 * q)
                    for i in range(8):
                        last = nc.vector.tensor_scalar(xn[:, i, :], resid[:, ds(8 * q + i, 1), :].rearrange("p o c -> p (o c)"),
                                                       mv[:, i, 0:1], rstd[:, i:i + 1], ALU.subtract, ALU.mult)
                    last.then_inc(s_xn, 1)
                wide = [128, NT, E1]
                dve.wait_ge(s_psR, 4)
                nc.vector.tensor_tensor(prob[:], psR[:], gate_b[:].unsqueeze(1).to_broadcast(wide), ALU.add).then_inc(s_step, 1)
                dve.wait_ge(s_step, 1)
                nc.vector.reduce_max(m[:], prob[:], AX.X).then_inc(s_step, 1)
                dve.wait_ge(s_step, 2)
                nc.vector.tensor_tensor(prob[:], prob[:], m[:].unsqueeze(2).to_broadcast(wide), ALU.subtract).then_inc(s_step, 1)
                dve.wait_ge(s_exp, 1)
                nc.vector.reduce_sum(z[:], prob[:], AX.X).then_inc(s_step, 1)
                dve.wait_ge(s_step, 4)
                nc.vector.reciprocal(m[:], z[:]).then_inc(s_step, 1)
                dve.wait_ge(s_step, 5)
                nc.vector.tensor_tensor(prob[:], prob[:], m[:].unsqueeze(2).to_broadcast(wide), ALU.mult).then_inc(s_step, 1)
                dve.wait_ge(s_step, 6)
                high4 = higher[:].rearrange("p (t e) f -> p t e f", t=NT)
                eq4 = equal[:].rearrange("p (t e) f -> p t e f", t=NT)
                for e in range(E1):
                    mine = prob[:, :, e:e + 1].to_broadcast(wide)
                    nc.vector.tensor_tensor(high4[:, :, e, :], prob[:], mine, ALU.is_gt)
                    last = nc.vector.tensor_tensor(eq4[:, :, e, :], prob[:], mine, ALU.is_equal)
                last.then_inc(s_step, 1)
                dve.wait_ge(s_step, 7)
                for e in range(E1):
                    last = nc.vector.tensor_tensor(eq4[:, :, e, :], eq4[:, :, e, :], before[:, e:e + 1, :].to_broadcast(wide), ALU.mult)
                last.then_inc(s_step, 1)
                dve.wait_ge(s_step, 8)
                nc.vector.tensor_tensor(higher[:], higher[:], equal[:], ALU.add).then_inc(s_step, 1)
                dve.wait_ge(s_step, 9)
                nc.vector.reduce_sum(rank[:], higher[:], AX.X).then_inc(s_step, 1)
                dve.wait_ge(s_step, 10)
                nc.vector.tensor_scalar(rank[:], rank[:], TOP1 - 0.5, None, ALU.is_lt).then_inc(s_step, 1)
                dve.wait_ge(s_step, 11)
                nc.vector.tensor_tensor(g["w_tok"][:, :, 0:E1], prob[:], rank[:].rearrange("p (t e) -> p t e", e=E1), ALU.mult).then_inc(s_weights, 1)

            @block.scalar
            def _(act):
                with act.Fori(0, 4) as q:
                    act.wait_ge(s_kept, 16 * q)
                    act.wait_ge(s_psR, q)
                    for k in range(2):
                        act.wait_ge(s_psT, 2 * q + k + 1)
                        nc.scalar.copy(flat(xTq[:, 4 * k:4 * k + 4, :]), flat(psT[:, 4 * k:4 * k + 4, :])).then_inc(s_xT, 1)
                act.wait_ge(s_step, 3)
                nc.scalar.activation(prob[:], prob[:], ACT.Exp).then_inc(s_exp, 1)
                for k in range(8):
                    act.wait_ge(s_psG, k + 1)
                    nc.scalar.copy(g["w_tokT"][:, 512 * k:512 * k + 512], psG[:, k % 2, :]).then_inc(s_wT, 1)

            @block.tensor
            def _(pe):
                pe.wait_ge(loaded, 16 * 3)
                with pe.Fori(0, 4) as q:
                    pe.wait_ge(s_xn, q + 1)
                    pe.wait_ge(s_xT, 2 * q)
                    for k in range(2):
                        for i in range(4 * k, 4 * k + 4):
                            last = nc.tensor.transpose(psT[:, i, :], xn[:, i, :], ident[:])
                        last.then_inc(s_psT, 1)
                    pe.wait_ge(s_xT, 2 * q + 2)
                    for i in range(8):
                        last = nc.tensor.matmul(psR[:, ds(8 * q + i, 1), :].rearrange("p o e -> p (o e)"), xTq[:, i, :], gate_w[:],
                                                start=True, stop=True)
                    last.then_inc(s_psR, 1)
                pe.wait_ge(s_weights, 1)
                pe.wait_ge(const, 2)
                for k in range(8):
                    if k >= 2:
                        pe.wait_ge(s_wT, k - 1)
                    for i in range(4):
                        last = nc.tensor.transpose(psG[:, k % 2, 128 * i:128 * i + 128], g["w_tok"][:, 4 * k + i, :], ident[:])
                    last.then_inc(s_psG, 1)


SHARED1 = 256 // INTER1


def phase_moe(nc, sem, io, g):
    resid = g["resid"]
    N = E1 + SHARED1
    with ExitStack() as stack:
        ph = Phase(nc, stack, "moe")
        w1 = ph.sb("w1", [C, N, INTER1])
        w3 = ph.sb("w3", [C, N, INTER1])
        w2 = ph.sb("w2", [INTER1, N, C])
        b1 = ph.sb("b1", [INTER1, N])
        b3 = ph.sb("b3", [INTER1, N])
        b2 = ph.sb("b2", [E1 + 1, C])
        wT = ph.sb("wT", [E1 + 1, 512])
        s1 = ph.sb("s1", [INTER1, 2, 512])
        hT = ph.sb("hT", [INTER1, 2, 512])
        hs = ph.sb("hs", [INTER1, SHARED1, 512])
        acc = ph.sb("acc", [128, 2, 4, C])
        stats = ph.sb("stats", [128, 4, 6])
        mv = ph.sb("mv", [128, 4, 2])
        var = ph.sb("var", [128, 4])
        rstd = ph.sb("rstd", [128, 4])
        halfneg = ph.sb("halfneg", [128, 4])
        eps = ph.sb("eps", [128, 4])
        wrow = ph.sb("wrow", [128, 4, E1])
        y = ph.sb("y", [128, 4, C])
        out = ph.sb("out", [128, 4, C])
        ps1 = ph.ps("ps1", [INTER1, 2, 512])
        ps3 = ph.ps("ps3", [INTER1, 2, 512])
        psY = ph.ps("psY", [128, 3, 4, C])

        def S(n):
            return sem("moe_" + n)

        s_wrow = S("wrow")
        (loaded, const, wT_loaded, s_up, s_silu, s_h, s_down, s_acc, s_stats, s_mv, s_var, s_rstd, s_y, s_out, stored) = (S(n) for n in (
            "loaded", "const", "wT_loaded", "up", "silu", "h", "down", "acc", "stats", "mv", "var", "rstd", "y", "out", "stored"))
        TURNS = NT // 4
        D = E1 + 1
        with nc.Block() as block:
            @block.sync
            def _(sp):
                for dst, src in ((w1, "m_w1"), (w3, "m_w3"), (w2, "m_w2"), (b1, "m_b1"), (b3, "m_b3"), (b2, "m_b2")):
                    sp.dma_start(dst[:], io[src]).then_inc(loaded, 16)
                with sp.Fori(0, TURNS) as i:
                    sp.wait_ge(s_down, D * i)
                    sp.dma_start(wT[:], g["w_tokT"][:, ds(512 * i, 512)]).then_inc(wT_loaded, 16)
                    sp.wait_ge(s_out, i + 1)
                    sp.dma_start(io["out"][:, ds(4 * i, 4), :], out[:]).then_inc(stored, 16)
                sp.wait_ge(stored, 16 * TURNS)

            @block.gpsimd
            def _(pool):
                nc.gpsimd.memset(eps[:], LN_EPS)
                nc.gpsimd.memset(halfneg[:], -0.5).then_inc(const, 1)
                pool.wait_ge(const, 1)
                with pool.Fori(0, TURNS) as i:
                    pool.wait_ge(s_mv, i + 1)
                    nc.gpsimd.tensor_tensor(var[:], mv[:, :, 1], eps[:], ALU.add).then_inc(s_var, 1)
                    pool.wait_ge(s_var, i + 1)
                    nc.gpsimd.tensor_tensor(rstd[:], var[:], halfneg[:], ALU.pow).then_inc(s_rstd, 1)
                    pool.wait_ge(s_y, i + 1)
                    pool.wait_ge(stored, 16 * i)
                    nc.gpsimd.tensor_tensor(out[:], resid[:, ds(4 * i, 4), :], y[:], ALU.add).then_inc(s_out, 1)

            @block.scalar
            def _(act):
                act.wait_ge(loaded, 16 * 6)
                with act.Fori(0, TURNS) as i:
                    for n in range(N):
                        act.wait_ge(s_up, N * i + n + 1)
                        act.wait_ge(s_h, N * i + max(n - 1, 0))
                        nc.scalar.activation(s1[:, n % 2, :], ps1[:, n % 2, :], ACT.Silu, bias=b1[:, n:n + 1]).then_inc(s_silu, 1)

            @block.vector
            def _(dve):
                dve.wait_ge(loaded, 16 * 6)

                def accumulate(i, e):
                    dve.wait_ge(s_down, D * i + e + 1)
                    if e:
                        dve.wait_ge(s_acc, D * i + e)
                    for t in range(4):
                        down = psY[:, e % 3, t, :]
                        if e == 0:
                            last = nc.vector.tensor_scalar(acc[:, 0, t, :], down, wrow[:, t, 0:1], None, ALU.mult)
                        else:
                            last = nc.vector.scalar_tensor_tensor(acc[:, e % 2, t, :], down, wrow[:, t, e:e + 1],
                                                                  acc[:, 1 - e % 2, t, :], ALU.mult, ALU.add)
                    last.then_inc(s_acc, 1)

                with dve.Fori(0, TURNS) as i:
                    dve.wait_ge(s_acc, D * i)
                    nc.vector.tensor_copy(wrow[:], g["w_tok"][:, ds(4 * i, 4), 0:E1]).then_inc(s_wrow, 1)
                    dve.wait_ge(s_wrow, i + 1)
                    for n in range(N):
                        dve.wait_ge(s_silu, N * i + n + 1)
                        if n < SHARED1:
                            dve.wait_ge(s_down, D * i)
                            dst = hs[:, n, :]
                        else:
                            dve.wait_ge(s_down, D * i + max(n - SHARED1 - 1, 0))
                            dst = hT[:, n % 2, :]
                        nc.vector.scalar_tensor_tensor(dst, ps3[:, n % 2, :], b3[:, n:n + 1], s1[:, n % 2, :], ALU.add, ALU.mult).then_inc(s_h, 1)
                        if n > SHARED1:
                            accumulate(i, n - SHARED1 - 1)
                    accumulate(i, E1 - 1)
                    dve.wait_ge(s_down, D * i + D)
                    dve.wait_ge(s_acc, D * i + D - 1)
                    nc.vector.tensor_tensor(acc[:, 0], psY[:, E1 % 3], acc[:, 1], ALU.add).then_inc(s_acc, 1)
                    dve.wait_ge(s_acc, D * i + D)
                    for t in range(4):
                        last = nc.vector.bn_stats(stats[:, t, :], acc[:, 0, t, :])
                    last.then_inc(s_stats, 1)
                    settled = count_in_register(dve, i + 1)
                    settle(dve, loaded)
                    dve.wait_ge(s_stats, settled)
                    for t in range(4):
                        last = nc.vector.bn_aggr(mv[:, t, :], stats[:, t, :])
                    last.then_inc(s_mv, 1)
                    dve.wait_ge(s_rstd, i + 1)
                    dve.wait_ge(s_out, i)
                    for t in range(4):
                        last = nc.vector.tensor_scalar(y[:, t, :], acc[:, 0, t, :], mv[:, t, 0:1], rstd[:, t:t + 1],
                                                       ALU.subtract, ALU.mult)
                    last.then_inc(s_y, 1)
                    dve.wait_ge(s_y, i + 1)

            @block.tensor
            def _(pe):
                pe.wait_ge(loaded, 16 * 6)

                def mm(out, lhsT, rhs, start=True, stop=True):
                    return nc.tensor.matmul(out, lhsT, rhs, start=start, stop=stop, skip_group_check=True)

                with pe.Fori(0, TURNS) as i:
                    x = g["xT_all"][:, ds(512 * i, 512)]

                    def up(n):
                        pe.wait_ge(s_h, N * i + max(n - 1, 0))
                        mm(ps1[:, n % 2, :], w1[:, n, :], x)
                        mm(ps3[:, n % 2, :], w3[:, n, :], x).then_inc(s_up, 1)

                    def down(e):
                        pe.wait_ge(s_h, N * i + SHARED1 + e + 1)
                        pe.wait_ge(s_acc, D * i + max(e - 2, 0))
                        for t in range(4):
                            last = mm(psY[:, e % 3, t, :], hT[:, e % 2, 128 * t:128 * t + 128], w2[:, SHARED1 + e, :])
                        last.then_inc(s_down, 1)

                    for n in range(N):
                        up(n)
                        if n > SHARED1:
                            down(n - SHARED1 - 1)
                    down(E1 - 1)
                    pe.wait_ge(wT_loaded, 16 * i + 16)
                    pe.wait_ge(s_acc, D * i + E1 - 2)
                    for t in range(4):
                        cols = slice(128 * t, 128 * t + 128)
                        for n in range(SHARED1):
                            mm(psY[:, E1 % 3, t, :], hs[:, n, cols], w2[:, n, :], n == 0, False)
                        last = mm(psY[:, E1 % 3, t, :], wT[:, cols], b2[:], False, True)
                    last.then_inc(s_down, 1)


def build(nc, arrays):
    io = {}
    for name, a in arrays.items():
        io[name] = nc.dram_tensor(name, list(a.shape), F32, kind="ExternalInput").ap()
    io["ks_dram"] = nc.dram_tensor("ks_dram", [B, D0, 4, 4, KEEP], F32).ap()
    io["vs_dram"] = nc.dram_tensor("vs_dram", [B, KEEP, 512], F32).ap()
    io["o_dram"] = nc.dram_tensor("o_dram", [B, 32, C], F32).ap()
    io["out"] = nc.dram_tensor("out", [128, NT, C], F32, kind="ExternalOutput").ap()
    with ExitStack() as stack:
        def run(phase):
            held = []

            def sem(name):
                held.append(nc.alloc_semaphore(name))
                return held[-1]
            phase(nc, sem, io, g)
            nc.all_engine_barrier()
            nc.clear_and_free_semaphores(held)
            nc.all_engine_barrier()

        main = Phase(nc, stack, "main")
        g = {"resid": main.sb("resid", [128, NT, C]), "ident": main.sb("ident", [128, 128]),
             "ident_b": main.sb("ident_b", [128, 128], BF16), "xT_all": main.sb("xT_all", [C, B * T])}
        with ExitStack() as layer0:
            l0 = Phase(nc, layer0, "l0")
            g["w_q"] = l0.sb("w_q", [QL, 4, 4, 128])
            g["w_val"] = l0.sb("w_val", [C, 2, 512])
            g["kv_scale"] = l0.sb("kv_scale", [128, 1])
            g["sel"] = l0.sb("sel", [C, B, KEEP])
            g["gates"] = l0.sb("gates", [128, B, 3])
            run(phase_weights)
            run(phase_select)
            run(phase_sel_kv)
            run(phase_attend0)
        with ExitStack() as layer0:
            l0 = Phase(nc, layer0, "l0f")
            g["pick"] = l0.sb("pick", [128, 4, T])
            g["merged"] = l0.sb("merged", [C, E0, B])
            run(phase_choose)
            run(phase_experts)
            run(phase_spread)
        run(phase_attend1)
        g["w_tok"] = main.sb("w_tok", [128, NT, E1 + 1])
        g["w_tokT"] = main.sb("w_tokT", [E1 + 1, B * T])
        run(phase_route)
        run(phase_moe)


def lay_out(i):
    c = np.ascontiguousarray
    a = dict(causal_constants())
    a["x"] = c(i["L0_attn_x"].reshape(NT, 128, C).transpose(1, 0, 2))
    nope, rope = i["L0_attn_w_dq_nope"], i["L0_attn_w_dq_rope"].reshape(QL, H0, 2, HALF)
    a["w_q"] = c(np.stack([nope, rope[:, :, 0].reshape(QL, -1), rope[:, :, 1].reshape(QL, -1)], 1).reshape(QL, 3, 4, 128))
    a["w_dq_nopeT"] = c(nope.T.reshape(4, 128, QL).transpose(1, 0, 2))
    dk = i["L0_attn_w_dk_nope"].reshape(KVL, 4, 4, NOPE)
    diag = np.zeros((4, NOPE, 4, 4, KVL), np.float32)
    for j in range(4):
        diag[j, :, :, j, :] = dk[:, :, j, :].transpose(2, 1, 0)
    a["w_dk_diag"] = diag.reshape(128, 4, 128)
    a["w_ckvT"] = c(i["L0_attn_w_ckv"].T)
    a["w_dv"] = i["L0_attn_w_dv"]
    a["g_q"] = i["L0_attn_g_qnorm"].reshape(QL, 1)
    a["g_kv"] = i["L0_attn_g_kvnorm"].reshape(KVL, 1)
    a["w_winv"] = i["L0_attn_w_winv"]
    a["w_imp"] = c(np.broadcast_to(i["L0_attn_w_imp"], (C, 128)))
    a["w_gate"] = i["L0_attn_w_gate"]
    for n in ("wink", "selk"):
        w = i[f"L0_attn_w_{n}"].reshape(C, H0, 3, 32)
        a[f"w_{n}"] = c(w.transpose(0, 2, 1, 3).reshape(C, 3, 4, 128))
    a["w_selv"] = i["L0_attn_w_selv"]
    a["w_tok"] = np.concatenate([i["L0_attn_w_cq"], i["L0_attn_w_ckv"], i["L0_attn_w_krope"]], 1)
    a["w_proj"] = c(i["L0_attn_w_proj"].reshape(4, 128, C).transpose(1, 0, 2))
    a["gate0_w"] = c(i["L0_ffn_gate_w"].T)
    a["gate0_b"] = c(np.broadcast_to(i["L0_ffn_gate_b"], (4, 32))).reshape(128, 1)
    a["w1"], a["w2"] = i["L0_ffn_w1"], i["L0_ffn_w2"]
    a["wq1T"] = c(i["L1_attn_wq"].reshape(C, 8, HD1).transpose(2, 1, 0))
    a["wk_upT"], a["wv_upT"] = c(i["L1_attn_wk_up"].T), c(i["L1_attn_wv_up"].T)
    a["wo1"] = c(i["L1_attn_wo"].reshape(8, HD1, C).transpose(1, 0, 2))
    a["wk_down4"] = c(np.broadcast_to(i["L1_attn_wk_down"].reshape(C, KV1, 1, LAT1), (C, KV1, 4, LAT1))).reshape(C, KV1, 128)
    a["wv_down"] = i["L1_attn_wv_down"]
    a["gate1_w"] = c(i["L1_ffn_gate_w"].T)
    a["gate1_b"] = c(np.broadcast_to(i["L1_ffn_gate_b"], (128, E1)))
    shared = {k: i[f"L1_ffn_ws{k}"].reshape(SHARED1, INTER1, C) for k in (1, 3)}
    for k in (1, 3):
        a[f"m_w{k}"] = c(np.concatenate([shared[k], i[f"L1_ffn_w{k}"]]).transpose(2, 0, 1))
        a[f"m_b{k}"] = c(np.concatenate([i[f"L1_ffn_bs{k}"].reshape(SHARED1, INTER1), i[f"L1_ffn_b{k}"]]).T)
    ws2 = i["L1_ffn_ws2"].reshape(C, SHARED1, INTER1).transpose(2, 1, 0)
    a["m_w2"] = c(np.concatenate([ws2, i["L1_ffn_w2"].transpose(2, 0, 1)], 1))
    a["m_b2"] = np.concatenate([i["L1_ffn_b2"], i["L1_ffn_bs2"][None]])
    return {k: c(v) for k, v in a.items()}


def kernel(**inputs):
    import concourse.bacc as bacc
    from concourse.bass_utils import run_bass_kernel_spmd

    nc = bacc.Bacc("TRN2", target_bir_lowering=False, num_devices=1)
    arrays = lay_out({name: np.asarray(a) for name, a in inputs.items()})
    build(nc, arrays)
    out = run_bass_kernel_spmd(nc, [arrays], core_ids=[0]).results[0]["out"]
    return np.ascontiguousarray(out.transpose(1, 0, 2)).reshape(B, T, C)
```

```python
from contextlib import ExitStack

import numpy as np
import concourse.bass as bass
from concourse import mybir
from concourse.alu_op_type import AluOpType as ALU

F32, BF16 = mybir.dt.float32, mybir.dt.bfloat16
ACT, AX = mybir.ActivationFunctionType, mybir.AxisListType
ds = bass.ds

B, T, C = 16, 256, 128
NT = B * T // 128
LN_EPS, RMS_EPS = 1e-5, 1e-6
H0, NOPE, ROPE, V0, KEEP = 16, 32, 64, 32, 32
HALF = ROPE // 2
QL, KVL = 96, 32
D0 = NOPE + ROPE
NEG = -1e30


def causal_constants():
    p = np.arange(128)
    ident = np.eye(128, dtype=np.float32)
    above = (p[None, :] > p[:, None])
    mask = np.tile(np.where(above, NEG, 0.0).astype(np.float32), (1, 4))
    s = np.arange(T)
    before = np.stack([(s[None, :] < (p[:, None] + 128 * t)) for t in range(2)], 1).astype(np.float32)
    upper = (p[:, None] < p[None, :]).astype(np.float32)
    iota = np.tile(np.arange(KEEP, dtype=np.float32), (128, 1))
    f = (1.0 / np.float32(10000.0) ** (np.arange(0, ROPE, 2, dtype=np.float32) / np.float32(ROPE))).astype(np.float32)
    a = np.outer(np.arange(T, dtype=np.float32), f).astype(np.float32)
    cos, sin = np.cos(a).astype(np.float32), np.sin(a).astype(np.float32)
    cT, sT = np.tile(cos.T, (4, 1)), np.tile(sin.T, (4, 1))
    rope_k = np.concatenate([cT, cT, -sT, sT], 1)
    rope_q = (rope_k * np.float32(D0 ** -0.5)).astype(np.float32)
    tok = np.concatenate([cos, cos, -sin, sin], 1).reshape(2, 128, 4 * HALF).transpose(1, 0, 2)
    rope_t = (tok / np.float32(H0)).astype(np.float32)
    return {
        "c_ident": ident,
        "c_rows": np.repeat(np.eye(4, dtype=np.float32), 32, 1) * (p % 32 < B), "c_mask": mask, "c_before": before, "c_upper": upper, "c_iota": iota,
        "c_rope_k": rope_k.astype(np.float32), "c_rope_q": rope_q, "c_rope_t": rope_t,
    }


class Phase:

    def __init__(self, nc, stack, name):
        self.nc, self.stack, self.name = nc, stack, name

    def sb(self, name, shape, dt=F32):
        return self.stack.enter_context(self.nc.sbuf_tensor(f"{self.name}_{name}", shape, dt))

    def ps(self, name, shape, dt=F32):
        return self.stack.enter_context(self.nc.psum_tensor(f"{self.name}_{name}", shape, dt))


def count_in_register(engine, count):
    register = engine.alloc_register()
    engine.reg_mov(register, count)
    return register


class Early:

    def __init__(self, nc, phase, arrays):
        self.phase, self.arrays = phase, arrays
        self.at = {n: phase.sb(n, shape) for n, (shape, _) in arrays.items()}
        self.loaded = nc.alloc_semaphore(phase.name + "_loaded")
        self.all = 16 * len(arrays)

    def load(self, sp, io):
        for n, (shape, src) in self.arrays.items():
            src = io[src]
            if len(shape) > len(src.shape):
                src = src.rearrange("p (a t) -> p a t", a=shape[1])
            sp.dma_start(self.at[n][:], src).then_inc(self.loaded, 16)


def settle(engine, passed):
    engine.wait_ge(passed, 1)


def flat(ap):
    return ap.rearrange("p a b -> p (a b)")


def phase_weights(nc, sem, io, g):
    with ExitStack() as stack:
        ph = Phase(nc, stack, "wts")
        wqT = ph.sb("wqT", [128, 4, QL])
        wkd = ph.sb("wkd", [128, 4, 128])
        ckvT = ph.sb("ckvT", [KVL, C])
        wdv = ph.sb("wdv", [KVL, 512])
        gq = ph.sb("gq", [QL, 1])
        gkv = ph.sb("gkv", [KVL, 1])
        ps = ph.ps("ps", [128, 2, 512])
        loaded, resident = sem("wts_loaded"), sem("wts_resident")
        scaled, dv_scaled, prod, done = sem("wts_scaled"), sem("wts_dv_scaled"), sem("wts_prod"), sem("wts_done")
        with nc.Block() as block:
            @block.sync
            def _(sp):
                for dst, src in ((wqT, "w_dq_nopeT"), (wkd, "w_dk_diag"), (ckvT, "w_ckvT"), (wdv, "w_dv"),
                                 (gq, "g_q"), (gkv, "g_kv")):
                    sp.dma_start(dst[:], io[src]).then_inc(loaded, 16)
                for dst, src in ((g["resid"], "x"), (g["w_q"][:, 0:3], "w_q"), (g["w_val"][:, 1, :], "w_winv"),
                                 (g["ident"], "c_ident")):
                    sp.dma_start(dst[:] if src in ("x", "c_ident") else dst, io[src]).then_inc(resident, 16)
                sp.dma_start(g["kv_scale"][96:128, :], io["g_kv"]).then_inc(resident, 16)
                for later in ("sel_early", "skv", "at0", "cho", "rou"):
                    g[later].load(sp, io)
                sp.wait_ge(resident, 16 * 5)

            @block.gpsimd
            def _(pool):
                nc.gpsimd.memset(g["kv_scale"][0:96, :], 1.0).then_inc(scaled, 1)

            @block.vector
            def _(dve):
                dve.wait_ge(loaded, 16 * 6)
                nc.vector.tensor_scalar(wdv[:], wdv[:], gkv[:], None, ALU.mult).then_inc(dv_scaled, 1)
                dve.wait_ge(resident, 16 * 5)
                dve.wait_ge(prod, 2)
                nc.vector.tensor_scalar(g["w_q"][:, 3].rearrange("p g m -> p (g m)"), ps[0:QL, 0, :], gq[:], None,
                                        ALU.mult).then_inc(done, 1)
                wq3 = g["w_q"][:, 0:3].rearrange("p a g m -> p (a g m)")
                nc.vector.tensor_scalar(wq3, wq3, gq[:], None, ALU.mult).then_inc(done, 1)
                nc.vector.tensor_copy(g["w_val"][:, 0, :], ps[:, 1, :]).then_inc(done, 1)
                dve.wait_ge(done, 3)
                nc.vector.tensor_copy(g["ident_b"][:], g["ident"][:]).then_inc(done, 1)

            @block.tensor
            def _(pe):
                pe.wait_ge(loaded, 16 * 6)
                for k in range(4):
                    last = nc.tensor.matmul(ps[0:QL, 0, 128 * k:128 * k + 128], wqT[:, k, :], wkd[:, k, :],
                                            start=True, stop=True)
                last.then_inc(prod, 1)
                pe.wait_ge(dv_scaled, 1)
                nc.tensor.matmul(ps[:, 1, :], ckvT[:], wdv[:], start=True, stop=True).then_inc(prod, 1)


def phase_select(nc, sem, io, g):
    resid, ident = g["resid"], g["ident"]
    with ExitStack() as stack:
        ph = Phase(nc, stack, "sel")
        stats = ph.sb("stats", [128, 4, 6])
        mv = ph.sb("mv", [128, 4, 2])
        var = ph.sb("var", [128, 4])
        rstd = ph.sb("rstd", [128, 4])
        halfneg = ph.sb("halfneg", [128, 4])
        eps = ph.sb("eps", [128, 4])
        xn = ph.sb("xn", [128, 2, 4, C])
        w_imp = g["sel_early"].at["w_imp"]
        before = g["sel_early"].at["before"]
        upper = g["sel_early"].at["upper"]
        upper_b = ph.sb("upper_b", [128, 128], BF16)
        ones_b = ph.sb("ones_b", [128, 128], BF16)
        iota = g["sel_early"].at["iota"]
        score = ph.sb("score", [128, 4])
        junk = ph.sb("junk", [128, 2, T])
        rank_gt = ph.sb("rank_gt", [128, 4])
        rank_eq = ph.sb("rank_eq", [128, 4])
        rank = ph.sb("rank", [128, 4])
        kept = ph.sb("kept", [128, 4])
        kept_b = ph.sb("kept_b", [128, 4], BF16)
        place = ph.sb("place", [128, 4])
        onehot = ph.sb("onehot", [128, 4, KEEP + 1])
        psT = ph.ps("psT", [128, 2, 4, 128])
        psS = ph.ps("psS", [128, 2, 2, T])
        psP = ph.ps("psP", [128, 512])
        psX = ph.ps("psX", [128, 2, 512])
        psG = ph.ps("psG", [128, 512])
        token_sum = ph.sb("token_sum", [C, B])
        g16 = ph.sb("g16", [16, 3])
        gmax = ph.sb("gmax", [16, 1])
        gsum = ph.sb("gsum", [16, 1])
        grec = ph.sb("grec", [16, 1])
        gdiag = ph.sb("gdiag", [16, 16, 3])
        w_gate = g["sel_early"].at["w_gate"]
        ones16 = ph.sb("ones16", [16, 128])
        loaded = g["sel_early"].loaded
        const, upper_ready = sem("sel_const"), sem("sel_upper_ready")
        s_stats, s_mv, s_var, s_rstd, s_xn = (sem("sel_" + n) for n in ("stats", "mv", "var", "rstd", "xn"))
        s_psT, s_xT, s_psS = (sem("sel_" + n) for n in ("psT", "xT", "psS"))
        s_score, s_counted, s_rank, s_kept, s_keptb = (sem("sel_" + n) for n in ("score", "counted", "rank", "kept", "keptb"))
        s_psP, s_place, s_onehot, s_psX, s_sel = (sem("sel_" + n) for n in ("psP", "place", "onehot", "psX", "sel"))
        s_gate = sem("sel_gate")
        STEPS = B // 2

        with nc.Block() as block:
            @block.gpsimd
            def _(pool):
                nc.gpsimd.memset(eps[:], LN_EPS)
                nc.gpsimd.memset(halfneg[:], -0.5).then_inc(const, 1)
                nc.gpsimd.memset(ones_b[:], 1.0).then_inc(const, 1)
                nc.gpsimd.memset(ones16[:], 1.0).then_inc(const, 1)
                nc.gpsimd.memset(onehot[:, :, KEEP:KEEP + 1], 1.0).then_inc(const, 1)
                pool.wait_ge(const, 4)
                with pool.Fori(0, STEPS) as n:
                    pool.wait_ge(s_mv, n + 1)
                    nc.gpsimd.tensor_tensor(var[:], mv[:, :, 1], eps[:], ALU.add).then_inc(s_var, 1)
                    pool.wait_ge(s_var, n + 1)
                    nc.gpsimd.tensor_tensor(rstd[:], var[:], halfneg[:], ALU.pow).then_inc(s_rstd, 1)

            @block.vector
            def _(dve):
                dve.wait_ge(loaded, 16 * 5)
                nc.vector.tensor_copy(upper_b[:], upper[:]).then_inc(upper_ready, 1)

                def moments(n):
                    for i in range(4):
                        last = nc.vector.bn_stats(stats[:, i, :], resid[:, ds(4 * n + i, 1), :])
                    last.then_inc(s_stats, 1)
                    settled = count_in_register(dve, n + 1)
                    settle(dve, loaded)
                    dve.wait_ge(s_stats, settled)
                    dve.wait_ge(s_rstd, n)
                    for i in range(4):
                        last = nc.vector.bn_aggr(mv[:, i, :], stats[:, i, :])
                    last.then_inc(s_mv, 1)

                def normalize(n, half):
                    dve.wait_ge(s_rstd, n + 1)
                    for i in range(4):
                        last = nc.vector.tensor_scalar(xn[:, half, i, :], resid[:, ds(4 * n + i, 1), :].rearrange("p o c -> p (o c)"),
                                                       mv[:, i, 0:1], rstd[:, i:i + 1], ALU.subtract, ALU.mult)
                    last.then_inc(s_xn, 1)

                def choose(n, half, ahead):
                    if ahead:
                        moments(n + 1)
                    dve.wait_ge(s_psS, n + 1)
                    for i in range(4):
                        last = nc.vector.scalar_tensor_tensor(junk[:, i % 2, 0:128], psS[:, half, i // 2, 128 * (i % 2):128 * (i % 2) + 128],
                                                              1.0, ident[:], ALU.mult, ALU.mult, accum_out=score[:, i:i + 1])
                        last.then_inc(s_score, 1)
                        dve.wait_ge(s_score, 12 * n + i + 1)
                    dve.wait_ge(s_psX, n)
                    if ahead:
                        normalize(n + 1, 1 - half)
                    for i in range(4):
                        nc.vector.tensor_scalar(junk[:, 0, :], psS[:, half, i // 2, :], score[:, i:i + 1], 0.0, ALU.is_gt, ALU.add,
                                                accum_out=rank_gt[:, i:i + 1]).then_inc(s_score, 1)
                        nc.vector.scalar_tensor_tensor(junk[:, 1, :], psS[:, half, i // 2, :], score[:, i:i + 1],
                                                       before[:, i % 2, :], ALU.is_equal, ALU.mult,
                                                       accum_out=rank_eq[:, i:i + 1]).then_inc(s_score, 1)
                        dve.wait_ge(s_score, 12 * n + 4 + 2 * i + 2)
                    nc.vector.tensor_tensor(rank[:], rank_gt[:], rank_eq[:], ALU.add).then_inc(s_rank, 1)
                    dve.wait_ge(s_rank, n + 1)
                    nc.vector.tensor_scalar(kept[:], rank[:], KEEP - 0.5, None, ALU.is_lt).then_inc(s_kept, 1)
                    dve.wait_ge(s_kept, n + 1)
                    nc.vector.tensor_copy(kept_b[:], kept[:]).then_inc(s_keptb, 1)
                    dve.wait_ge(s_psP, n + 1)
                    nc.vector.tensor_copy(place[:], psP[:, 0:4]).then_inc(s_place, 1)
                    dve.wait_ge(s_place, n + 1)
                    for i in range(4):
                        last = nc.vector.tensor_scalar(onehot[:, i, 0:KEEP], iota[:], place[:, i:i + 1], kept[:, i:i + 1],
                                                       ALU.is_equal, ALU.mult)
                    last.then_inc(s_onehot, 1)

                moments(0)
                normalize(0, 0)
                with dve.Fori(0, STEPS - 3, 2) as n:
                    choose(n, 0, True)
                    choose(n + 1, 1, True)
                choose(STEPS - 2, 0, True)
                choose(STEPS - 1, 1, False)
                dve.wait_ge(s_psX, STEPS + 1)
                nc.vector.reduce_max(gmax[:], psG[0:16, 0:3], AX.X).then_inc(s_gate, 1)
                dve.wait_ge(s_gate, 1)
                nc.vector.tensor_scalar(g16[:], psG[0:16, 0:3], gmax[:], 1.0 / T, ALU.subtract, ALU.mult).then_inc(s_gate, 1)
                dve.wait_ge(s_gate, 3)
                nc.vector.reciprocal(grec[:], gsum[:]).then_inc(s_gate, 1)
                dve.wait_ge(s_gate, 4)
                nc.vector.tensor_scalar(g16[:], g16[:], grec[:], None, ALU.mult).then_inc(s_gate, 1)
                dve.wait_ge(s_gate, 5)
                for a in range(3):
                    last = nc.vector.tensor_scalar(gdiag[:, :, a], ident[0:16, 0:16], g16[:, a:a + 1], None, ALU.mult)
                last.then_inc(s_gate, 1)
                dve.wait_ge(s_psX, STEPS + 2)
                nc.vector.tensor_copy(g["gates"][:].rearrange("p b a -> p (b a)"), psG[:, 0:3 * B]).then_inc(s_gate, 1)

            @block.scalar
            def _(act):
                def transposed(n, half):
                    act.wait_ge(s_psT, n + 1)
                    nc.scalar.copy(g["xT_all"][:, ds(512 * n, 512)], flat(psT[:, half])).then_inc(s_xT, 1)

                def gathered(n, half):
                    act.wait_ge(s_psX, n + 1)
                    rows = psX[:, half, 0:2 * (KEEP + 1)].rearrange("p (b k) -> p b k", b=2)
                    nc.scalar.copy(g["sel"][:, ds(2 * n, 2), :], rows[:, :, 0:KEEP])
                    nc.scalar.copy(token_sum[:, ds(2 * n, 2)], rows[:, :, KEEP]).then_inc(s_sel, 1)

                transposed(0, 0)
                with act.Fori(0, STEPS - 3, 2) as n:
                    transposed(n + 1, 1)
                    gathered(n, 0)
                    transposed(n + 2, 0)
                    gathered(n + 1, 1)
                transposed(STEPS - 1, 1)
                gathered(STEPS - 2, 0)
                gathered(STEPS - 1, 1)
                act.wait_ge(s_gate, 2)
                nc.scalar.activation(g16[:], g16[:], ACT.Exp, accum_out=gsum[:]).then_inc(s_gate, 1)

            @block.tensor
            def _(pe):
                pe.wait_ge(loaded, 16 * 5)
                pe.wait_ge(const, 4)
                pe.wait_ge(upper_ready, 1)

                def front(n, half):
                    pe.wait_ge(s_xn, n + 1)
                    for i in range(4):
                        last = nc.tensor.transpose(psT[:, half, i, :], xn[:, half, i, :], ident[:])
                    last.then_inc(s_psT, 1)
                    pe.wait_ge(s_xT, n + 1)
                    nc.tensor.matmul(psS[:, half].rearrange("p b t -> p (b t)"), w_imp[:], g["xT_all"][:, ds(512 * n, 512)],
                                     start=True, stop=True).then_inc(s_psS, 1)

                def back(n, half, ahead):
                    if ahead:
                        front(n + 1, 1 - half)
                    pe.wait_ge(s_keptb, n + 1)
                    nc.tensor.matmul(psP[:, 0:4], upper_b[:], kept_b[:], start=True, stop=False, skip_group_check=True)
                    nc.tensor.matmul(psP[:, 1:4:2], ones_b[:], kept_b[:, 0::2], start=False, stop=True,
                                     skip_group_check=True).then_inc(s_psP, 1)
                    pe.wait_ge(s_onehot, n + 1)
                    for i in range(4):
                        at = (KEEP + 1) * (i // 2)
                        last = nc.tensor.matmul(psX[:, half, at:at + KEEP + 1], xn[:, half, i, :], onehot[:, i, :],
                                                start=(i % 2 == 0), stop=(i % 2 == 1), skip_group_check=True)
                    last.then_inc(s_psX, 1)

                front(0, 0)
                with pe.Fori(0, STEPS - 3, 2) as n:
                    back(n, 0, True)
                    back(n + 1, 1, True)
                back(STEPS - 2, 0, True)
                back(STEPS - 1, 1, False)
                pe.wait_ge(s_sel, STEPS)
                nc.tensor.matmul(psG[0:16, 0:3], token_sum[:], w_gate[:], start=True, stop=True).then_inc(s_psX, 1)
                pe.wait_ge(s_gate, 6)
                nc.tensor.matmul(psG[:, 0:3 * B], ones16[:], gdiag[:].rearrange("p b a -> p (b a)"), start=True, stop=True).then_inc(s_psX, 1)


def phase_sel_kv(nc, sem, io, g):
    with ExitStack() as stack:
        ph = Phase(nc, stack, "skv")
        w_k = g["skv"].at["w_k"]
        w_v = g["skv"].at["w_v"]
        rope = g["skv"].at["rope"]
        kst = ph.sb("kst", [128, B, 3, 4, KEEP])
        vst = ph.sb("vst", [128, 4, 512])
        tc = ph.sb("tc", [128, 2, 2, B, KEEP])
        tsn = ph.sb("tsn", [128, 2, 2, B, KEEP])
        ps = ph.ps("ps", [128, 2, 3, 512])
        psv = ph.ps("psv", [128, 2, 512])
        loaded = g["skv"].loaded
        s_ps, s_nope, s_rot, s_sum, s_psv, s_v, s_out = (sem("skv_" + n) for n in ("ps", "nope", "rot", "sum", "psv", "v", "out"))
        with nc.Block() as block:
            @block.sync
            def _(sp):
                def keys(part):
                    for j in range(4):
                        sp.dma_start(io["ks_dram"][:, 32 * part:32 * part + 32, j].rearrange("b r g s -> r b g s"),
                                     kst[32 * j:32 * j + 32, :, part]).then_inc(s_out, 16)

                sp.wait_ge(s_nope, 4)
                keys(0)
                sp.wait_ge(s_v, 4)
                sp.dma_start(io["vs_dram"].rearrange("(q a) s n -> (a s) q n", q=4), vst[:]).then_inc(s_out, 16)
                sp.wait_ge(s_sum, 4)
                keys(1)
                keys(2)
                sp.wait_ge(s_out, 16 * 13)

            @block.tensor
            def _(pe):
                pe.wait_ge(loaded, 16 * 3)
                keys = g["sel"]
                for k in range(4):
                    if k >= 2:
                        pe.wait_ge(s_nope, k - 1)
                        pe.wait_ge(s_rot, k - 1)
                    for part in range(3):
                        last = nc.tensor.matmul(ps[:, k % 2, part, :], w_k[:, part, k, :], flat(keys[:]), start=True, stop=True)
                    last.then_inc(s_ps, 1)
                for k in range(4):
                    if k >= 2:
                        pe.wait_ge(s_v, k - 1)
                    nc.tensor.matmul(psv[:, k % 2, :], flat(keys[:, 4 * k:4 * k + 4, :]), w_v[:], start=True, stop=True).then_inc(s_psv, 1)

            @block.scalar
            def _(act):
                for k in range(4):
                    act.wait_ge(s_ps, k + 1)
                    nc.scalar.copy(kst[:, :, 0, k, :], ps[:, k % 2, 0, :].rearrange("p (b s) -> p b s", b=B)).then_inc(s_nope, 1)
                for k in range(4):
                    act.wait_ge(s_psv, k + 1)
                    nc.scalar.copy(vst[:, k, :], psv[:, k % 2, :]).then_inc(s_v, 1)

            @block.vector
            def _(dve):
                dve.wait_ge(loaded, 16 * 3)
                for k in range(4):
                    dve.wait_ge(s_ps, k + 1)
                    if k >= 2:
                        dve.wait_ge(s_sum, k - 1)
                    for half in range(2):
                        x = ps[:, k % 2, 1 + half, :].rearrange("p (b s) -> p b s", b=B)
                        y = ps[:, k % 2, 2 - half, :].rearrange("p (b s) -> p b s", b=B)
                        cosine = rope[:, half, 0:KEEP].unsqueeze(1).to_broadcast([128, B, KEEP])
                        sine = rope[:, 2 + half, 0:KEEP].unsqueeze(1).to_broadcast([128, B, KEEP])
                        nc.vector.tensor_tensor(tc[:, k % 2, half], x, cosine, ALU.mult)
                        last = nc.vector.tensor_tensor(tsn[:, k % 2, half], y, sine, ALU.mult)
                    last.then_inc(s_rot, 1)

            @block.gpsimd
            def _(pool):
                for k in range(4):
                    pool.wait_ge(s_rot, k + 1)
                    for half in range(2):
                        last = nc.gpsimd.tensor_tensor(kst[:, :, 1 + half, k, :], tc[:, k % 2, half], tsn[:, k % 2, half], ALU.add)
                    last.then_inc(s_sum, 1)


UNITS = 24
SLOTS = UNITS
GROUP_UNITS = 6

KIND = ["hi", "hi", "lo", "hi", "hi", "lo"]
HEADS = [(0,), (1,), (0, 1), (2,), (3,), (2, 3)]

PLAN = {
    0: ["tok"], 1: ["s2_01"], 3: ["krot_0"], 4: ["trq"], 5: ["krot_1", "kn_01"], 6: ["v_00", "kn_23"], 7: ["v_10", "s2_23"],
    8: ["v_01", "s2t_0"], 9: ["v_11", "s2t_1"], 10: ["y", "qrot_0"], 13: ["p2_01"], 14: ["p2_23", "qrot_1"], 15: ["qn_0"],
    16: ["qn_1", "krot_2"], 17: ["qrot_2"], 18: ["krot_3"], 19: ["qrot_3"], 20: ["qn_2"], 21: ["qn_3"], 22: ["trk"],
}
GATE_SLOT = 11
LAG, P_RING = 3, 4
V_ORDER = ["v_00", "v_10", "v_01", "v_11"]
ROT_ORDER = [n for s in sorted(PLAN) for n in PLAN[s] if n[1:4] == "rot"]
class Turn:

    UNITS, PLAN = UNITS, PLAN
    OF_BATCH = {"s2_01", "s2_23", "s2t_0", "s2t_1", "p2_01", "p2_23", *V_ORDER}
    OF_BEFORE = {"y"}
    VALUES = {15: (0, 0), 17: (1, 0), 22: (2, 0), 4: (3, 1)}

    @classmethod
    def uses(cls, mode):
        all_ = [n for s in sorted(cls.PLAN) for n in cls.PLAN[s]]
        of_batch = [n for n in all_ if n in cls.OF_BATCH]
        return {
            "first": [n for n in all_ if n not in cls.OF_BATCH | cls.OF_BEFORE],
            "second": [n for n in all_ if n not in cls.OF_BEFORE],
            "body": all_,
            "last": [n for n in all_ if n in cls.OF_BATCH | cls.OF_BEFORE],
            "drain": [n for n in all_ if n in cls.OF_BEFORE],
        }[mode]

    def __init__(self, mode, b, half=0):
        self.mode, self.b, self.half = mode, b, half
        self.attends = mode in ("second", "body", "last")
        self.projects = mode in ("first", "second", "body")
        self.follows = mode in ("body", "last", "drain")
        self.pb = 0 if mode == "first" else b + 1
        self.phalf = 0 if mode == "first" else 1 - half
        self.order = {n: i for i, n in enumerate(self.uses(mode))}
        self.order_before = {n: i for i, n in enumerate(self.uses({"second": "first", "drain": "last"}.get(mode, "body")))}
        first, second, body, last = (len(self.uses(m)) for m in ("first", "second", "body", "last"))
        assert body % 2 == 0
        self.start = {"first": 0, "second": first, "body": first + second, "last": first + second,
                      "drain": first + second + last - body}[mode]
        self.starts = self.start if mode in ("first", "second") else self.start + (b - 1) * body

    def before(self):
        return type(self)({"second": "first", "drain": "last"}.get(self.mode, "body"), self.b - 1, 1 - self.half)

    def tasks(self, s):
        return [n for n in self.PLAN.get(s, []) if n in self.order]

    def bank(self, n):
        return (self.start + self.order[n]) % 2

    def full(self, n):
        return self.starts + (self.order[n] + 1)

    def full_before(self, n):
        return self.starts - (len(self.order_before) - self.order_before[n] - 1)

    def last_in_bank(self, n):
        at = self.order[n] - 2
        if at >= 0:
            return next(m for m, i in self.order.items() if i == at), self
        if self.mode == "first":
            return None
        at += len(self.order_before)
        if at >= 0:
            return next(m for m, i in self.order_before.items() if i == at), self.before()
        before = self.before()
        at += len(before.order_before)
        return next(m for m, i in before.order_before.items() if i == at), before.before()

    def unit(self, u, lag=0):
        u = u - lag + 1
        return max(u, 0) if self.mode == "second" else self.b * self.UNITS + u

    def stage(self, s, lag):
        if s >= lag:
            return (s - lag, self) if self.attends else None
        return (s - lag + self.UNITS, self.before()) if self.follows else None

    def values_group(self, s):
        if s not in self.VALUES:
            return None
        k, later = self.VALUES[s]
        if later:
            return (k, self.before()) if self.follows else None
        return (k, self) if self.attends else None


def phase_attend0(nc, sem, io, g):
    resid, ident, ident_b = g["resid"], g["ident"], g["ident_b"]
    w_q, w_val = g["w_q"], g["w_val"]
    with ExitStack() as stack:
        ph = Phase(nc, stack, "at0")
        w_tok = g["at0"].at["w_tok"]
        w_k = g["at0"].at["w_k"]
        w_out = g["at0"].at["w_out"]
        mask = g["at0"].at["mask"]
        mask_b = ph.sb("mask_b", [128, 512], BF16)
        rope_q = g["at0"].at["rope_q"]
        rope_k = g["at0"].at["rope_k"]
        rope_t = g["at0"].at["rope_t"]
        xT = ph.sb("xT", [C, T])
        xTv = ph.sb("xTv", [C, T])
        sq = ph.sb("sq", [128, 2, QL])
        ss = ph.sb("ss", [128, 4])
        sse = ph.sb("sse", [128, 4])
        rs = ph.sb("rs", [128, 4])
        rv = ph.sb("rv", [128, 3])
        halfneg = ph.sb("halfneg", [128, 4])
        rms_eps = ph.sb("rms_eps", [128, 4])
        eps = ph.sb("eps", [128, 4])
        gate_pb = ph.sb("gate_pb", [128, 3])
        gate_b = ph.sb("gate_b", [128, 1])
        latent_sq = ph.sb("latent_sq", [128, 2, KVL])
        nq = ph.sb("nq", [128, 2, QL])
        k1tok = ph.sb("k1tok", [128, 2, 128])
        krt = ph.sb("krt", [128, 2, 2, ROPE])
        nqT = ph.sb("nqT", [QL, T])
        k1 = ph.sb("k1", [128, T])
        val = ph.sb("val", [128, 2, 2, 512])
        qst = ph.sb("qst", [128, 4, 4, T])
        kst = ph.sb("kst", [128, 3, 4, T])
        qT = ph.sb("qT", [128, 4, 4, T])
        kT = ph.sb("kT", [D0, 4, 4, T])
        rc = ph.sb("rc", [128, 2, 512])
        rsn = ph.sb("rsn", [128, 2, 512])
        ksb = ph.sb("ksb", [D0, 4, 4, KEEP])
        vsd = ph.sb("vsd", [128, 4, 128])
        s2T = ph.sb("s2T", [128, 4, T])
        p2 = ph.sb("p2", [128, 2, 512])
        m2 = ph.sb("m2", [128, 2, 16])
        z2 = ph.sb("z2", [128, 2, 16])
        r2 = ph.sb("r2", [128, 2, 16])
        p2T = ph.sb("p2T", [128, 4, T])
        p = ph.sb("p", [128, P_RING, 512])
        nm = ph.sb("nm", [128, P_RING, 4])
        z = ph.sb("z", [128, P_RING, 4])
        rz = ph.sb("rz", [128, P_RING, 4])
        pT = ph.sb("pT", [128, 2, 4, 2, 384])
        oT = ph.sb("oT", [128, 4, T])
        ystats = ph.sb("ystats", [128, 2, 6])
        ymv = ph.sb("ymv", [128, 2, 2])
        yvar = ph.sb("yvar", [128, 2])
        yrstd = ph.sb("yrstd", [128, 2])
        y = ph.sb("y", [128, 2 * C])
        yn = ph.sb("yn", [128, 2, C])
        psS = ph.ps("psS", [128, 3, 512])
        psT = ph.ps("psT", [128, 2, 512])
        psO = ph.ps("psO", [128, 2, T])
        psM = ph.ps("psM", [128, 2, 512])

        def S(n):
            return sem("at0_" + n)

        mask_ready, xTv_loaded = S("mask_ready"), S("xTv_loaded")
        loaded = g["at0"].loaded
        const, xT_loaded, sel_loaded, vsd_loaded = S("const"), S("xT_loaded"), S("sel_loaded"), S("vsd_loaded")
        scores_full, max_ready, exp_ready, recip_ready, norm_ready, pT_full = (S(n) for n in (
            "scores_full", "max_ready", "exp_ready", "recip_ready", "norm_ready", "pT_full"))
        evac_even, evac_odd = S("evac_even"), S("evac_odd")
        o_full, o_ready = S("o_full"), S("o_ready")
        misc_full = S("misc_full")
        sq_ready, sse_ready, rs_ready, rv_ready, latents_ready, kr_mul, kr_ready = (S(n) for n in (
            "sq_ready", "sse_ready", "rs_ready", "rv_ready", "latents_ready", "kr_mul", "kr_ready"))
        gate_ready = S("gate_ready")
        nqT_ready, k1_ready, val_ready = S("nqT_ready"), S("k1_ready"), S("val_ready")
        rot_mul, q_rot, k_rot, q_plain, k_plain = S("rot_mul"), S("q_rot"), S("k_rot"), S("q_plain"), S("k_plain")
        qk_loaded = [S("qk_loaded0"), S("qk_loaded1")]
        s2T_ready, m2_ready, s2_ready, e2_ready, z2_ready, r2_ready, p2_ready, p2T_ready = (S(n) for n in (
            "s2T_ready", "m2_ready", "s2_ready", "e2_ready", "z2_ready", "r2_ready", "p2_ready", "p2T_ready"))
        ystats_ready, ymv_ready, yvar_ready, yrstd_ready, yn_ready, resid_ready = (S(n) for n in (
            "ystats_ready", "ymv_ready", "yvar_ready", "yrstd_ready", "yn_ready", "resid_ready"))
        OWN_DMAS = 28

        def turns(engine, body):
            body(Turn("first", 0))
            body(Turn("second", 0))
            with engine.Fori(1, B - 1) as b:
                body(Turn("body", b))
            body(Turn("last", B - 1))
            body(Turn("drain", B))

        def misc(n, t, eng):
            eng.wait_ge(misc_full, t.full(n))
            return psM[:, t.bank(n), :]

        def pT_unused(u, t):
            k = u // 6 - 1
            return max(k, 0) if t.mode == "second" else 4 * t.b + k

        def evacuate(copy, u):
            k, (j0, *more) = u // 6, HEADS[u % 6]
            bank = psT[:, u % 2, :]
            if KIND[u % 6] == "hi":
                return copy(pT[:, k % 2, j0, :, 128:384], bank.rearrange("p (a x) -> p a x", a=2))
            return copy(pT[:, k % 2, j0:j0 + 2, :, 0:128], bank.rearrange("p (j a x) -> p j a x", j=2, a=2))

        def emptied(n, t):
            k = int(n[-1]) if n[-1].isdigit() else 0
            return {
                "tok": lambda: (kr_mul, t.pb + 1), "trq": lambda: (nqT_ready, t.pb + 1), "trk": lambda: (k1_ready, t.pb + 1),
                "qrot": lambda: (rot_mul, 8 * t.pb + ROT_ORDER.index(n) + 1), "krot": lambda: (rot_mul, 8 * t.pb + ROT_ORDER.index(n) + 1),
                "qn": lambda: (q_plain, 4 * t.pb + k + 1), "kn": lambda: (k_plain, 2 * t.pb + k // 2 + 1),
                "v": lambda: (val_ready, 4 * t.b + V_ORDER.index(n) + 1),
                "s2": lambda: (s2T_ready, 2 * t.b + k // 2 + 1), "s2t": lambda: (s2_ready, 2 * t.b + k + 1),
                "p2": lambda: (p2T_ready, 2 * t.b + k // 2 + 1), "y": lambda: (ystats_ready, t.b),
            }[n.split("_")[0]]()

        def bank_emptied(n, t):
            before = t.last_in_bank(n)
            return [] if before is None else [emptied(*before)]

        with nc.Block() as block:
            @block.sync
            def _(sp):

                def body(t):
                    if t.attends:
                        sp.wait_ge(const, 3)
                        if t.follows:
                            sp.wait_ge(o_full, 4 * t.b)
                        for j in range(4):
                            sp.dma_start(vsd[32 * j:32 * j + 32, :, 32 * j:32 * j + 32],
                                         io["vs_dram"][ds(t.b, 1)].rearrange("o s (g h v) -> h (o s) g v", g=4, h=4)[j]
                                         ).then_inc(vsd_loaded, 16)
                    if t.projects:
                        if t.attends:
                            sp.wait_ge(misc_full, t.full("s2_23"))
                        sp.dma_start(ksb[:], io["ks_dram"][ds(t.pb, 1)].rearrange("o r j g s -> (o r) j g s")).then_inc(sel_loaded, 16)
                    for pair in range(2):
                        if not t.projects:
                            break
                        settled = count_in_register(sp, 4 * t.pb + 2 * pair + 2)
                        settle(sp, loaded)
                        sp.wait_ge(q_rot, settled)
                        sp.wait_ge(k_rot, 4 * t.pb + 2 * pair + 2)
                        sp.wait_ge(q_plain, 4 * t.pb + 2 * pair + 2)
                        settled = count_in_register(sp, 2 * t.pb + pair + 1)
                        settle(sp, loaded)
                        sp.wait_ge(k_plain, settled)
                        if t.attends:
                            sp.wait_ge(scores_full, t.unit(12 * pair + 11))
                            if pair == 1:
                                sp.wait_ge(misc_full, t.full("s2_23"))
                        groups = slice(2 * pair, 2 * pair + 2)
                        for j in range(4):
                            for part in range(4):
                                sp.dma_start(qT[32 * part:32 * part + 32, j, groups, :],
                                             qst[32 * j:32 * j + 32, part, groups, :]).then_inc(qk_loaded[pair], 16)
                            for part in range(3):
                                sp.dma_start(kT[32 * part:32 * part + 32, j, groups, :],
                                             kst[32 * j:32 * j + 32, part, groups, :]).then_inc(qk_loaded[pair], 16)
                turns(sp, body)

            @block.gpsimd
            def _(pool):
                nc.gpsimd.memset(eps[:], LN_EPS)
                nc.gpsimd.memset(rms_eps[:], RMS_EPS)
                nc.gpsimd.memset(halfneg[:], -0.5).then_inc(const, 1)
                nc.gpsimd.memset(k1tok[:, :, 0:NOPE], 0.0).then_inc(const, 1)
                nc.gpsimd.memset(vsd[:], 0.0).then_inc(const, 1)
                pool.wait_ge(const, 3)

                def body(t):
                    for s in range(SLOTS):
                        for n in t.tasks(s):
                            if n == "tok":
                                pool.wait_ge(sq_ready, t.pb + 1)
                                nc.gpsimd.tensor_tensor(sse[:], ss[:], rms_eps[:], ALU.add).then_inc(sse_ready, 1)
                                pool.wait_ge(sse_ready, t.pb + 1)
                                pool.wait_ge(rv_ready, t.pb)
                                nc.gpsimd.tensor_tensor(rs[:], sse[:], halfneg[:], ALU.pow).then_inc(rs_ready, 1)
                            if n[:4] in ("qrot", "krot"):
                                k = int(n[-1])
                                done = q_rot if n[0] == "q" else k_rot
                                dst = (qst if n[0] == "q" else kst)[:, 1:3, k, :]
                                turn = ROT_ORDER.index(n)
                                pool.wait_ge(rot_mul, 8 * t.pb + turn + 1)
                                if t.attends:
                                    pool.wait_ge(qk_loaded[k // 2], 16 * OWN_DMAS * t.pb)
                                nc.gpsimd.tensor_tensor(dst, rc[:, turn % 2, :].rearrange("p (a t) -> p a t", a=2),
                                                        rsn[:, turn % 2, :].rearrange("p (a t) -> p a t", a=2), ALU.add).then_inc(done, 1)
                            if n == "y":
                                pool.wait_ge(ymv_ready, t.b)
                                nc.gpsimd.tensor_tensor(yvar[:], ymv[:, :, 1], eps[:, 0:2], ALU.add).then_inc(yvar_ready, 1)
                                pool.wait_ge(yvar_ready, t.b)
                                nc.gpsimd.tensor_tensor(yrstd[:], yvar[:], halfneg[:, 0:2], ALU.pow).then_inc(yrstd_ready, 1)
                        if t.stage(s, 1):
                            u, of = t.stage(s, 1)
                            r = u % P_RING
                            pool.wait_ge(recip_ready, of.unit(u))
                            n_ = 2 if KIND[u % 6] == "hi" else 4
                            pv = p[:, r, :].rearrange("p (a k) -> p a k", a=n_)
                            nc.gpsimd.tensor_tensor(pv, pv, rz[:, r, 0:n_].unsqueeze(2).to_broadcast([128, n_, 512 // n_]),
                                                    ALU.mult).then_inc(norm_ready, 1)
                turns(pool, body)

            @block.vector
            def _(dve):
                dve.wait_ge(loaded, 16 * 7)
                nc.vector.tensor_copy(mask_b[:], mask[:]).then_inc(mask_ready, 1)
                dve.wait_ge(const, 3)

                def task(n, t):
                    if n == "tok":
                        bank = misc(n, t, dve)[:, 0:384].rearrange("p (a c) -> p a c", a=2)
                        kr = bank[:, :, QL + KVL:]
                        dve.wait_ge(latents_ready, t.pb + 1)
                        nc.vector.tensor_tensor(krt[:, 0], kr, rope_t[:, :, 0:ROPE], ALU.mult)
                        swapped = krt[:, 1].rearrange("p a (h f) -> p a h f", h=2)
                        for half in range(2):
                            last = nc.vector.tensor_tensor(swapped[:, :, half, :], kr[:, :, HALF * (1 - half):HALF * (2 - half)],
                                                           rope_t[:, :, ROPE + HALF * half:ROPE + HALF * half + HALF], ALU.mult)
                        last.then_inc(kr_mul, 1)
                        dve.wait_ge(kr_mul, t.pb + 1)
                        nc.vector.tensor_tensor(k1tok[:, :, NOPE:D0], krt[:, 0], krt[:, 1], ALU.add).then_inc(kr_ready, 1)
                    if n[:4] in ("qrot", "krot"):
                        k = int(n[-1])
                        turn = ROT_ORDER.index(n)
                        table = rope_q if n[0] == "q" else rope_k
                        bank = misc(n, t, dve)
                        two_before = ROT_ORDER[turn - 2]
                        dve.wait_ge(q_rot if two_before[0] == "q" else k_rot, 4 * (t.pb - (turn < 2)) + (int(two_before[-1]) + 1)
                                    if t.attends or turn >= 2 else 0)
                        nc.vector.tensor_tensor(rc[:, turn % 2, :], bank, table[:, 0, :], ALU.mult)
                        for half in range(2):
                            last = nc.vector.tensor_tensor(rsn[:, turn % 2, T * half:T * half + T],
                                                           psM[:, t.bank(n), T * (1 - half):T * (2 - half)],
                                                           table[:, 1, T * half:T * half + T], ALU.mult)
                        last.then_inc(rot_mul, 1)
                    if n == "trk":
                        bank = misc(n, t, dve)
                        if t.attends:
                            dve.wait_ge(scores_full, t.unit(UNITS - 1))
                        nc.vector.tensor_scalar(k1[:], bank[:, 0:T], g["kv_scale"][:], None, ALU.mult).then_inc(k1_ready, 1)
                    if n[:4] == "s2t_":
                        i = int(n[-1])
                        bank = misc(n, t, dve).rearrange("p (h s) -> p h s", s=KEEP)
                        nc.vector.reduce_max(m2[:, i, :], bank, AX.X).then_inc(m2_ready, 1)
                        dve.wait_ge(m2_ready, 2 * t.b + i + 1)
                        dve.wait_ge(p2T_ready, 2 * t.b)
                        nc.vector.tensor_tensor(p2[:, i, :].rearrange("p (h s) -> p h s", s=KEEP), bank,
                                                m2[:, i, :].unsqueeze(2).to_broadcast([128, 16, KEEP]), ALU.subtract).then_inc(s2_ready, 1)
                    if n == "y":
                        bank = misc(n, t, dve)
                        dve.wait_ge(yn_ready, t.b - 1)
                        nc.vector.tensor_copy(y[:], bank[:, 0:2 * C])
                        for i in range(2):
                            last = nc.vector.bn_stats(ystats[:, i, :], bank[:, C * i:C * i + C])
                        last.then_inc(ystats_ready, 1)
                        settled = count_in_register(dve, t.b)
                        settle(dve, loaded)
                        dve.wait_ge(ystats_ready, settled)
                        dve.wait_ge(yvar_ready, t.b - 1)
                        for i in range(2):
                            last = nc.vector.bn_aggr(ymv[:, i, :], ystats[:, i, :])
                        last.then_inc(ymv_ready, 1)

                def add_y(b):
                    dve.wait_ge(yrstd_ready, b + 1)
                    dve.wait_ge(ystats_ready, b + 1)
                    for i in range(2):
                        last = nc.vector.tensor_scalar(yn[:, i, :], y[:, C * i:C * i + C], ymv[:, i, 0:1], yrstd[:, i:i + 1],
                                                       ALU.subtract, ALU.mult)
                    last.then_inc(yn_ready, 1)
                    dve.wait_ge(yn_ready, b + 1)
                    rows = resid[:, ds(2 * b, 2), :]
                    nc.vector.tensor_tensor(rows, rows, yn[:], ALU.add).then_inc(resid_ready, 1)
                    dve.wait_ge(resid_ready, b + 1)

                def p2_probs(t):
                    dve.wait_ge(e2_ready, t.b + 1)
                    nc.vector.reduce_sum(z2[:].rearrange("p t h -> p (t h)"), p2[:].rearrange("p t (h s) -> p (t h) s", s=KEEP),
                                         AX.X).then_inc(z2_ready, 1)
                    dve.wait_ge(z2_ready, t.b + 1)
                    nc.vector.reciprocal(r2[:], z2[:])
                    nc.vector.tensor_copy(gate_b[:], g["gates"][:, ds(t.b, 1), 1]).then_inc(r2_ready, 1)
                    dve.wait_ge(r2_ready, 2 * t.b + 1)
                    nc.vector.tensor_scalar(r2[:], r2[:], gate_b[:], None, ALU.mult).then_inc(r2_ready, 1)

                def p2_scaled(t):
                    dve.wait_ge(r2_ready, 2 * t.b + 2)
                    pv = p2[:].rearrange("p t (h s) -> p (t h) s", s=KEEP)
                    nc.vector.tensor_tensor(pv, pv, r2[:].rearrange("p t h -> p (t h)").unsqueeze(2).to_broadcast([128, 32, KEEP]),
                                            ALU.mult).then_inc(p2_ready, 1)

                def body(t):
                    if t.projects:
                        if t.attends:
                            dve.wait_ge(misc_full, t.full_before("kn_23"))
                            dve.wait_ge(misc_full, t.full_before("krot_3"))
                        nc.vector.tensor_copy(xT[:], g["xT_all"][:, ds(T * t.pb, T)]).then_inc(xT_loaded, 1)
                    for s in range(SLOTS):
                        if t.projects and s == SLOTS - 1:
                            task("trk", t)
                        if t.stage(s, 1):
                            u, of = t.stage(s, 1)
                            r = u % P_RING
                            n_ = 2 if KIND[u % 6] == "hi" else 4
                            dve.wait_ge(exp_ready, of.unit(u))
                            nc.vector.reciprocal(rz[:, r, 0:n_], z[:, r, 0:n_]).then_inc(recip_ready, 1)
                        if t.attends and s < UNITS:
                            n_ = 2 if KIND[s % 6] == "hi" else 4
                            dve.wait_ge(scores_full, t.unit(s))
                            nc.vector.tensor_reduce(nm[:, s % P_RING, 0:n_], psS[:, s % 3, :].rearrange("p (a k) -> p a k", a=n_), AX.X,
                                                    ALU.max, negate=True).then_inc(max_ready, 1)
                        if t.projects and s == 2:
                            task("tok", t)
                        for n in t.tasks(s):
                            if n not in ("tok", "trk"):
                                task(n, t)
                        if t.projects and s == GATE_SLOT - 3:
                            dve.wait_ge(rv_ready, t.pb)
                            nc.vector.tensor_copy(gate_pb[:], g["gates"][:, ds(t.pb, 1), :].rearrange("p o a -> p (o a)")
                                                  ).then_inc(gate_ready, 1)
                        if s == 11 and t.attends:
                            p2_probs(t)
                        if s == 12 and t.attends:
                            p2_scaled(t)
                        if s == 13 and t.follows:
                            add_y(t.b - 1)
                        if t.stage(s, LAG):
                            u, of = t.stage(s, LAG)
                            if u % 2 == 0:
                                dve.wait_ge(pT_full, of.unit(u))
                                dve.wait_ge(o_full, pT_unused(u, of))
                                evacuate(nc.vector.tensor_copy, u).then_inc(evac_even, 1)

                turns(dve, body)

            @block.scalar
            def _(act):
                act.wait_ge(loaded, 16 * 7)
                act.wait_ge(const, 3)

                def task(n, t):
                    if n == "tok":
                        bank = misc(n, t, act)[:, 0:384].rearrange("p (a c) -> p a c", a=2)
                        act.wait_ge(sse_ready, t.pb)
                        for i in range(2):
                            nc.scalar.activation(sq[:, i, :], bank[:, i, 0:QL], ACT.Square, scale=QL ** -0.5, accum_out=ss[:, 2 * i:2 * i + 1])
                            last = nc.scalar.activation(latent_sq[:, i, :], bank[:, i, QL:QL + KVL], ACT.Square, scale=KVL ** -0.5,
                                                        accum_out=ss[:, 2 * i + 1:2 * i + 2])
                        last.then_inc(sq_ready, 1)
                    if n == "latents":
                        bank = psM[:, t.bank("tok"), 0:384].rearrange("p (a c) -> p a c", a=2)
                        act.wait_ge(rs_ready, t.pb + 1)
                        if t.attends:
                            act.wait_ge(misc_full, t.full_before("trk"))
                        for i in range(2):
                            nc.scalar.activation(nq[:, i, :], bank[:, i, 0:QL], ACT.Copy, scale=rs[:, 2 * i:2 * i + 1])
                            last = nc.scalar.activation(k1tok[:, i, D0:128], bank[:, i, QL:QL + KVL], ACT.Copy, scale=rs[:, 2 * i + 1:2 * i + 2])
                        last.then_inc(latents_ready, 1)
                    if n == "trq":
                        bank = misc(n, t, act)
                        nc.scalar.copy(nqT[:], bank[0:QL, 0:T]).then_inc(nqT_ready, 1)
                    if n[:2] == "qn":
                        k = int(n[-1])
                        bank = misc(n, t, act)
                        if t.attends:
                            act.wait_ge(qk_loaded[k // 2], 16 * OWN_DMAS * t.pb)
                        nc.scalar.activation(qst[:, 0::3, k, :], bank.rearrange("p (a t) -> p a t", a=2), ACT.Copy,
                                             scale=D0 ** -0.5).then_inc(q_plain, 1)
                    if n[:2] == "kn":
                        pair = int(n[-2]) // 2
                        bank = misc(n, t, act)
                        if t.attends:
                            act.wait_ge(qk_loaded[pair], 16 * OWN_DMAS * t.pb)
                        nc.scalar.copy(kst[:, 0, 2 * pair:2 * pair + 2, :], bank.rearrange("p (a t) -> p a t", a=2)).then_inc(k_plain, 1)
                    if n[:2] == "v_":
                        a, i = int(n[2]), int(n[3])
                        bank = misc(n, t, act)
                        k = V_ORDER.index(n)
                        if k == 0:
                            if t.follows:
                                act.wait_ge(o_full, 4 * t.b)
                            act.wait_ge(rv_ready, t.b + 1)
                        scale = rv[:, i:i + 1] if a == 0 else rv[:, 2:3]
                        nc.scalar.activation(val[:, a, i, :], bank, ACT.Copy, scale=scale).then_inc(val_ready, 1)
                    if n == "rv":
                            act.wait_ge(gate_ready, t.pb + 1)
                            if t.attends:
                                act.wait_ge(val_ready, 4 * t.b + 4)
                            nc.scalar.copy(rv[:, 2:3], gate_pb[:, 2:3])
                            for x in range(2):
                                last = nc.scalar.activation(rv[:, x:x + 1], rs[:, 2 * x + 1:2 * x + 2], ACT.Copy,
                                                            scale=gate_pb[:, 0:1])
                            last.then_inc(rv_ready, 1)
                    if n in ("s2_01", "s2_23"):
                        i = int(n[-2]) // 2
                        bank = misc(n, t, act)
                        nc.scalar.copy(s2T[:, 2 * i:2 * i + 2, :], bank.rearrange("p (a t) -> p a t", a=2)).then_inc(s2T_ready, 1)
                    if n in ("p2_01", "p2_23"):
                        i = int(n[-2]) // 2
                        bank = misc(n, t, act)
                        act.wait_ge(o_full, 4 * t.b)
                        nc.scalar.copy(p2T[:, 2 * i:2 * i + 2, :], bank.rearrange("p (a t) -> p a t", a=2)).then_inc(p2T_ready, 1)

                def body(t):
                    for s in range(SLOTS):
                        if t.attends and s < UNITS:
                            r, bank = s % P_RING, psS[:, s % 3, :]
                            n_ = 2 if KIND[s % 6] == "hi" else 4
                            w = 512 // n_
                            act.wait_ge(max_ready, t.unit(s))
                            act.wait_ge(pT_full, t.unit(s, P_RING))
                            for i in range(n_):
                                last = nc.scalar.activation(p[:, r, w * i:w * i + w], bank[:, w * i:w * i + w], ACT.Exp,
                                                            bias=nm[:, r, i:i + 1], accum_out=z[:, r, i:i + 1])
                            last.then_inc(exp_ready, 1)
                        for n in t.tasks(s):
                            task(n, t)
                        if t.projects and s == 1:
                            task("latents", t)
                        if t.attends and s == 3:
                            if t.follows:
                                act.wait_ge(val_ready, 4 * t.b)
                            nc.scalar.copy(xTv[:], g["xT_all"][:, ds(T * t.b, T)]).then_inc(xTv_loaded, 1)
                        if t.projects and s == GATE_SLOT:
                            task("rv", t)
                        if t.attends and s == 10:
                            act.wait_ge(s2_ready, 2 * t.b + 2)
                            nc.scalar.activation(p2[:], p2[:], ACT.Exp).then_inc(e2_ready, 1)
                        if t.stage(s, LAG):
                            u, of = t.stage(s, LAG)
                            if u % 2 == 1:
                                act.wait_ge(pT_full, of.unit(u))
                                act.wait_ge(o_full, pT_unused(u, of))
                                evacuate(nc.scalar.copy, u).then_inc(evac_odd, 1)
                        if t.values_group(s):
                            k, of = t.values_group(s)
                            act.wait_ge(o_full, 4 * of.b + k + 1)
                            if k == 0 and t.follows:
                                act.wait_ge(misc_full, t.full("y"))
                            nc.scalar.copy(oT[:, k, :], psO[:, k % 2, :]).then_inc(o_ready, 1)

                turns(act, body)

            @block.tensor
            def _(pe):
                pe.wait_ge(loaded, 16 * 7)
                pe.wait_ge(const, 3)
                pe.wait_ge(mask_ready, 1)

                def mm(out, lhsT, rhs, start=True, stop=True):
                    return nc.tensor.matmul(out, lhsT, rhs, start=start, stop=stop, skip_group_check=True)

                def task(n, t):
                    bank = psM[:, t.bank(n), :]
                    for by, count in bank_emptied(n, t):
                        pe.wait_ge(by, count)
                    if n == "tok":
                        pe.wait_ge(xT_loaded, t.pb + 1)
                        for i in range(2):
                            last = mm(bank[:, 192 * i:192 * i + 192], xT[:, 128 * i:128 * i + 128], w_tok[:])
                    if n == "trq":
                        pe.wait_ge(latents_ready, t.pb + 1)
                        for i in range(2):
                            last = nc.tensor.transpose(bank[0:QL, 128 * i:128 * i + 128], nq[:, i, :], ident[:])
                    if n == "trk":
                        pe.wait_ge(kr_ready, t.pb + 1)
                        pe.wait_ge(latents_ready, t.pb + 1)
                        for i in range(2):
                            last = nc.tensor.transpose(bank[:, 128 * i:128 * i + 128], k1tok[:, i, :], ident[:])
                    if n[:4] == "qrot":
                        pe.wait_ge(nqT_ready, t.pb + 1)
                        for half in range(2):
                            last = mm(bank[:, T * half:T * half + T], w_q[:, 1 + half, int(n[-1]), :], nqT[:])
                    if n[:2] == "qn":
                        for i, part in enumerate((0, 3)):
                            last = mm(bank[:, T * i:T * i + T], w_q[:, part, int(n[-1]), :], nqT[:])
                    if n[:4] == "krot":
                        for half in range(2):
                            last = mm(bank[:, T * half:T * half + T], w_k[:, 1 + half, int(n[-1]), :], xT[:])
                    if n[:2] == "kn":
                        for i in range(2):
                            last = mm(bank[:, T * i:T * i + T], w_k[:, 0, int(n[-2]) + i, :], xT[:])
                    if n[:2] == "v_":
                        a, i = int(n[2]), int(n[3])
                        pe.wait_ge(xTv_loaded, t.b + 1)
                        last = mm(bank, xTv[:, 128 * i:128 * i + 128], w_val[:, a, :])
                    if n in ("s2_01", "s2_23"):
                        pe.wait_ge(qk_loaded[int(n[-2]) // 2], 16 * OWN_DMAS * (t.b + 1))
                        if n == "s2_01":
                            pe.wait_ge(sel_loaded, 16 * (t.b + 1))
                        for i in range(2):
                            for j in range(4):
                                last = mm(bank[32 * j:32 * j + 32, T * i:T * i + T], ksb[:, j, int(n[-2]) + i, :],
                                          qT[0:D0, j, int(n[-2]) + i, :])
                    if n[:4] == "s2t_":
                        i = int(n[-1])
                        pe.wait_ge(s2T_ready, 2 * t.b + 2)
                        for k in range(4):
                            last = nc.tensor.transpose(bank[:, 128 * k:128 * k + 128], s2T[:, k, 128 * i:128 * i + 128], ident[:])
                    if n in ("p2_01", "p2_23"):
                        pe.wait_ge(p2_ready, t.b + 1)
                        for x in range(2):
                            for i in range(2):
                                k = int(n[-2]) + x
                                last = nc.tensor.transpose(bank[:, T * x + 128 * i:T * x + 128 * i + 128],
                                                           p2[:, i, 128 * k:128 * k + 128], ident[:])
                    if n == "y":
                        pe.wait_ge(o_ready, 4 * t.b)
                        for i in range(2):
                            for k in range(4):
                                last = mm(bank[:, C * i:C * i + C], oT[:, k, 128 * i:128 * i + 128], w_out[:, k, :], k == 0, k == 3)
                    last.then_inc(misc_full, 1)

                def scores(u, t):
                    k, r = u // 6, u % 3
                    bank = psS[:, r, :]
                    if u == 0:
                        pe.wait_ge(k1_ready, t.b + 1)
                    if u % 12 == 0:
                        pe.wait_ge(qk_loaded[u // 12], 16 * OWN_DMAS * (t.b + 1))
                    pe.wait_ge(exp_ready, t.unit(u, 3))
                    if KIND[u % 6] == "hi":
                        (j,) = HEADS[u % 6]
                        mm(bank[:, 0:256], qT[:, j, k, 128:256], k1[:], True, False)
                        mm(bank[:, 256:512], qT[0:D0, j, k, 128:256], kT[:, j, k, :], False, False)
                        last = mm(bank.rearrange("p (a x) -> p a x", a=2)[:, :, 128:256], ident_b[:], mask_b[:, 0:256], False, True)
                    else:
                        for i, j in enumerate(HEADS[u % 6]):
                            mm(bank[:, 256 * i:256 * i + 128], qT[:, j, k, 0:128], k1[:, 0:128], i == 0, False)
                            mm(bank[:, 256 * i + 128:256 * i + 256], qT[0:D0, j, k, 0:128], kT[:, j, k, 0:128], False, False)
                        last = mm(bank, ident_b[:], mask_b[:], False, True)
                    last.then_inc(scores_full, 1)

                def transposes(u, t):
                    k, r = u // 6, u % P_RING
                    pe.wait_ge(norm_ready, t.unit(u))
                    pe.wait_ge(evac_even if u % 2 == 0 else evac_odd, t.b * (UNITS // 2) + u // 2)
                    for i in range(4):
                        last = nc.tensor.transpose(psT[:, u % 2, 128 * i:128 * i + 128], p[:, r, 128 * i:128 * i + 128], ident[:])
                    last.then_inc(pT_full, 1)

                def values(k, t):
                    pe.wait_ge(evac_even, t.b * (UNITS // 2) + 3 * k + 3)
                    pe.wait_ge(evac_odd, t.b * (UNITS // 2) + 3 * k + 3)
                    pe.wait_ge(val_ready, 4 * (t.b + 1))
                    pe.wait_ge(p2T_ready, 2 * (t.b + 1))
                    pe.wait_ge(vsd_loaded, 64 * (t.b + 1))
                    pe.wait_ge(o_ready, 4 * t.b + k)
                    out = psO[:, k % 2, :]
                    mm(out, vsd[:, k, :], p2T[:, k, :], True, False)
                    for a in range(2):
                        for tile in range(2):
                            for j in range(4):
                                cols = slice(0, 256) if tile == 0 else slice(256, 384)
                                last = mm(out[32 * j:32 * j + 32, 128 * tile:256], val[:, a, tile, 128 * k + 32 * j:128 * k + 32 * j + 32],
                                          pT[:, k % 2, j, a, cols], False, a == 1 and tile == 1)
                    last.then_inc(o_full, 1)

                def body(t):
                    for s in range(SLOTS):
                        if t.attends:
                            scores(s, t)
                        for n in t.tasks(s):
                            task(n, t)
                        if t.stage(s, LAG):
                            transposes(*t.stage(s, LAG))
                        if t.values_group(s):
                            values(*t.values_group(s))

                turns(pe, body)


E0, HID0, TOP0 = 32, 512, 8


def phase_choose(nc, sem, io, g):
    resid, ident = g["resid"], g["ident"]
    with ExitStack() as stack:
        ph = Phase(nc, stack, "cho")
        gate_w = g["cho"].at["gate_w"]
        gate_b = g["cho"].at["gate_b"]
        stats = ph.sb("stats", [128, 8, 6])
        mv = ph.sb("mv", [128, 8, 2])
        var = ph.sb("var", [128, 8])
        rstd = ph.sb("rstd", [128, 8])
        halfneg = ph.sb("halfneg", [128, 8])
        eps = ph.sb("eps", [128, 8])
        xn = ph.sb("xn", [128, 8, C])
        xTq = ph.sb("xTq", [C, 8, 128])
        logit = ph.sb("logit", [128, T])
        prob = ph.sb("prob", [128, T])
        rest = ph.sb("rest", [128, T])
        pick = ph.sb("pick", [128, T])
        nmax = ph.sb("nmax", [128, 1])
        z = ph.sb("z", [128, 1])
        rz = ph.sb("rz", [128, 1])
        top = ph.sb("top", [128, TOP0])
        pickT = ph.sb("pickT", [128, 2, 128])
        psT = ph.ps("psT", [128, 8, 128])
        psL = ph.ps("psL", [128, T])
        psP = ph.ps("psP", [128, 2, 128])
        psM = ph.ps("psM", [C, 4, E0])

        def S(n):
            return sem("cho_" + n)

        (const, s_stats, s_mv, s_var, s_rstd, s_xn, s_psT, s_xT, s_psL, s_logit, s_nmax, s_exp, s_rz, s_prob, s_top,
         s_rest, s_pick, s_psP, s_pickT, s_psM, s_merged, s_pick_kept) = (S(n) for n in (
             "const", "stats", "mv", "var", "rstd", "xn", "psT", "xT", "psL", "logit", "nmax", "exp", "rz", "prob",
             "top", "rest", "pick", "psP", "pickT", "psM", "merged", "pick_kept"))
        loaded = g["cho"].loaded
        with nc.Block() as block:
            @block.sync
            def _(sp):
                sp.dma_start(g["exp_rows"][:], io["c_rows"]).then_inc(g["exp_rows_loaded"], 16)
                for x in range(2):
                    load_w1(sp, io, g, x, x)
                    load_w2(sp, io, g, x, x)

            @block.gpsimd
            def _(pool):
                nc.gpsimd.memset(eps[:], LN_EPS)
                nc.gpsimd.memset(halfneg[:], -0.5).then_inc(const, 1)
                pool.wait_ge(const, 1)
                with pool.Fori(0, 4) as q:
                    pool.wait_ge(s_mv, q + 1)
                    nc.gpsimd.tensor_tensor(var[:], mv[:, :, 1], eps[:], ALU.add).then_inc(s_var, 1)
                    pool.wait_ge(s_var, q + 1)
                    nc.gpsimd.tensor_tensor(rstd[:], var[:], halfneg[:], ALU.pow).then_inc(s_rstd, 1)

            @block.vector
            def _(dve):
                dve.wait_ge(loaded, 16 * 2)
                def moments(q):
                    for i in range(8):
                        last = nc.vector.bn_stats(stats[:, i, :], resid[:, ds(8 * q + i, 1), :])
                    last.then_inc(s_stats, 1)
                    settled = count_in_register(dve, q + 1)
                    settle(dve, loaded)
                    dve.wait_ge(s_stats, settled)
                    for i in range(8):
                        last = nc.vector.bn_aggr(mv[:, i, :], stats[:, i, :])
                    last.then_inc(s_mv, 1)

                def body(q, ahead):
                    dve.wait_ge(s_rstd, q + 1)
                    dve.wait_ge(s_psM, q)
                    for i in range(8):
                        last = nc.vector.tensor_scalar(xn[:, i, :], resid[:, ds(8 * q + i, 1), :].rearrange("p o c -> p (o c)"),
                                                       mv[:, i, 0:1], rstd[:, i:i + 1], ALU.subtract, ALU.mult)
                    last.then_inc(s_xn, 1)
                    if ahead:
                        moments(q + 1)
                    dve.wait_ge(s_psL, q + 1)
                    nc.vector.tensor_scalar(logit[:], psL[:], gate_b[:], None, ALU.add).then_inc(s_logit, 1)
                    dve.wait_ge(s_logit, q + 1)
                    nc.vector.tensor_reduce(nmax[:], logit[:], AX.X, ALU.max, negate=True).then_inc(s_nmax, 1)
                    dve.wait_ge(s_exp, q + 1)
                    nc.vector.reciprocal(rz[:], z[:]).then_inc(s_rz, 1)
                    dve.wait_ge(s_rz, q + 1)
                    nc.vector.tensor_scalar(prob[:], prob[:], rz[:], None, ALU.mult).then_inc(s_prob, 1)
                    settled = count_in_register(dve, q + 1)
                    settle(dve, loaded)
                    dve.wait_ge(s_prob, settled)
                    nc.vector.max(top[:], prob[:]).then_inc(s_top, 1)
                    settled = count_in_register(dve, q + 1)
                    settle(dve, loaded)
                    dve.wait_ge(s_top, settled)
                    nc.vector.match_replace(out=rest[:], in_to_replace=top[:], in_values=prob[:], imm_value=0.0).then_inc(s_rest, 1)
                    dve.wait_ge(s_rest, q + 1)
                    dve.wait_ge(s_pickT, q)
                    nc.vector.tensor_tensor(pick[:], prob[:], rest[:], ALU.subtract).then_inc(s_pick, 1)
                    dve.wait_ge(s_pick, q + 1)
                    nc.vector.tensor_copy(g["pick"][:, ds(q, 1), :].rearrange("p o t -> p (o t)"), pick[:]).then_inc(s_pick_kept, 1)

                moments(0)
                with dve.Fori(0, 3) as q:
                    body(q, True)
                body(3, False)

            @block.scalar
            def _(act):
                with act.Fori(0, 4) as q:
                    for k in range(2):
                        act.wait_ge(s_psT, 2 * q + k + 1)
                        nc.scalar.copy(flat(xTq[:, 4 * k:4 * k + 4, :]), flat(psT[:, 4 * k:4 * k + 4, :])).then_inc(s_xT, 1)
                    act.wait_ge(s_nmax, q + 1)
                    nc.scalar.activation(prob[:], logit[:], ACT.Exp, bias=nmax[:], accum_out=z[:]).then_inc(s_exp, 1)
                    act.wait_ge(s_psP, q + 1)
                    nc.scalar.copy(flat(pickT[:]), flat(psP[:])).then_inc(s_pickT, 1)
                    act.wait_ge(s_psM, q + 1)
                    nc.scalar.copy(g["merged"][:, :, ds(4 * q, 4)].rearrange("c e b -> c b e"), psM[:]).then_inc(s_merged, 1)

            @block.tensor
            def _(pe):
                pe.wait_ge(loaded, 16 * 2)
                with pe.Fori(0, 4) as q:
                    pe.wait_ge(s_xn, q + 1)
                    for k in range(2):
                        for i in range(4 * k, 4 * k + 4):
                            last = nc.tensor.transpose(psT[:, i, :], xn[:, i, :], ident[:])
                        last.then_inc(s_psT, 1)
                    pe.wait_ge(s_xT, 2 * q + 2)
                    for i in range(4):
                        last = nc.tensor.matmul(psL[32 * i:32 * i + 32, :], gate_w[:], flat(xTq[:, 2 * i:2 * i + 2, :]), start=True, stop=True)
                    last.then_inc(s_psL, 1)
                    pe.wait_ge(s_pick, q + 1)
                    for t in range(2):
                        last = nc.tensor.transpose(psP[:, t, :], pick[:, 128 * t:128 * t + 128], ident[:])
                    last.then_inc(s_psP, 1)
                    pe.wait_ge(s_pickT, q + 1)
                    pe.wait_ge(s_merged, q)
                    for i in range(4):
                        for t in range(2):
                            last = nc.tensor.matmul(psM[:, i, :], xn[:, 2 * i + t, :], pickT[:, t, 32 * i:32 * i + 32],
                                                    start=(t == 0), stop=(t == 1))
                    last.then_inc(s_psM, 1)


def load_w1(sp, io, g, step, x):
    sp.dma_start(g["exp_w1"][:, x], io["w1"][ds(4 * step, 4), 0:C, :].rearrange("e c h -> c e h")).then_inc(g["exp_w1_loaded"][x], 16)
    sp.dma_start(g["exp_w1b"][:, x, :], io["w1"][ds(4 * step, 4), C, :]).then_inc(g["exp_w1_loaded"][x], 16)


def load_w2(sp, io, g, step, x):
    sp.dma_start(g["exp_w2"][:, x], io["w2"][ds(4 * step, 4), 0:HID0, :].rearrange("e (p k) c -> p e k c", k=4)
                 ).then_inc(g["exp_w2_loaded"][x], 16)
    sp.dma_start(g["exp_w2b"][:, x, :], io["w2"][ds(4 * step, 4), HID0, :]).then_inc(g["exp_w2_loaded"][x], 16)


def phase_experts(nc, sem, io, g):
    ident = g["ident"]
    STEPS = E0 // 4
    with ExitStack() as stack:
        ph = Phase(nc, stack, "exp")
        merged = ph.sb("merged", [C, 2, 4, B])
        w1, w1b, w2, w2b, rows = (g["exp_" + n] for n in ("w1", "w1b", "w2", "w2b", "rows"))
        h = ph.sb("h", [128, 2, HID0])
        hT = ph.sb("hT", [128, 2, 4, 128])
        o = ph.sb("o", [128, 2, C])
        psH = ph.ps("psH", [128, 2, HID0])
        psT = ph.ps("psT", [128, 2, 4, 128])
        psO = ph.ps("psO", [128, 2, 512])

        def S(n):
            return sem("exp_" + n)

        w1_loaded, w2_loaded = g["exp_w1_loaded"], g["exp_w2_loaded"]
        s_merged, s_psH, s_h, s_psT, s_hT, s_psO, s_o = (S(n) for n in ("merged", "psH", "h", "psT", "hT", "psO", "o"))
        o_stored = [S("o_stored0"), S("o_stored1")]
        with nc.Block() as block:
            @block.sync
            def _(sp):
                def load(step, x):
                    sp.wait_ge(s_psH, step - 1)
                    load_w1(sp, io, g, step, x)
                    sp.wait_ge(s_psO, step - 1)
                    load_w2(sp, io, g, step, x)

                with sp.Fori(2, STEPS - 1, 2) as i:
                    load(i, 0)
                    load(i + 1, 1)

            @block.gpsimd
            def _(pool):
                with pool.Fori(0, STEPS - 1, 2) as i:
                    for x in range(2):
                        pool.wait_ge(s_o, i + x + 1)
                        for j in range(4):
                            pool.dma_start(io["o_dram"][:, ds(4 * (i + x) + j, 1), :].rearrange("b o c -> (b o) c"),
                                           o[32 * j:32 * j + B, x, :]).then_inc(o_stored[x], 16)
                for x in range(2):
                    pool.wait_ge(o_stored[x], 64 * (STEPS // 2))

            @block.scalar
            def _(act):
                with act.Fori(0, STEPS - 1, 2) as i:
                    for x in range(2):
                        act.wait_ge(s_psH, i + x + 1)
                        act.wait_ge(s_psT, i)
                        nc.scalar.activation(h[:, x, :], psH[:, x, :], ACT.Gelu).then_inc(s_h, 1)

            @block.vector
            def _(dve):
                def merged_rows(n, x):
                    dve.wait_ge(s_psH, n - 1)
                    nc.vector.tensor_copy(merged[:, x], g["merged"][:, ds(4 * n, 4), :]).then_inc(s_merged, 1)

                def rest(n, x):
                    dve.wait_ge(s_psT, n + 1)
                    nc.vector.tensor_copy(flat(hT[:, x]), flat(psT[:, x])).then_inc(s_hT, 1)
                    dve.wait_ge(s_psO, n + 1)
                    dve.wait_ge(o_stored[x], 32 * (n - x))
                    nc.vector.tensor_copy(o[:, x, :], psO[:, x, 0:C]).then_inc(s_o, 1)

                for x in range(2):
                    nc.vector.tensor_copy(merged[:, x], g["merged"][:, 4 * x:4 * x + 4, :]).then_inc(s_merged, 1)
                rest(0, 0)
                with dve.Fori(1, STEPS - 2, 2) as n:
                    merged_rows(n + 1, 0)
                    rest(n, 1)
                    merged_rows(n + 2, 1)
                    rest(n + 1, 0)
                rest(STEPS - 1, 1)

            @block.tensor
            def _(pe):
                pe.wait_ge(g["exp_rows_loaded"], 16)

                def hidden(n, x, first=False):
                    pe.wait_ge(w1_loaded[x], 16 * (n - x) + 32)
                    pe.wait_ge(s_merged, n + 1)
                    if not first:
                        pe.wait_ge(s_h, n - 1)
                    nc.tensor.matmul(psH[:, x, :], rows[:], w1b[:, x, :], start=True, stop=False, skip_group_check=True)
                    for j in range(4):
                        last = nc.tensor.matmul(psH[32 * j:32 * j + B, x, :], merged[:, x, j, :], w1[:, x, j, :],
                                                start=False, stop=True, skip_group_check=True)
                    last.then_inc(s_psH, 1)

                def transposed(n, x, first=False):
                    pe.wait_ge(s_h, n + 1)
                    if not first:
                        pe.wait_ge(s_hT, n - 1)
                    for k in range(4):
                        last = nc.tensor.transpose(psT[:, x, k, :], h[:, x, k::4], ident[:])
                    last.then_inc(s_psT, 1)

                def output(n, x, first=False):
                    pe.wait_ge(w2_loaded[x], 16 * (n - x) + 32)
                    pe.wait_ge(s_hT, n + 1)
                    if not first:
                        pe.wait_ge(s_o, n - 1)
                    nc.tensor.matmul(psO[:, x, 0:C], rows[:], w2b[:, x, :], start=True, stop=False, skip_group_check=True)
                    for k in range(4):
                        for j in range(4):
                            last = nc.tensor.matmul(psO[32 * j:32 * j + B, x, 0:C], hT[:, x, k, 32 * j:32 * j + B],
                                                    w2[:, x, j, k, :], start=False, stop=(k == 3), skip_group_check=True)
                    last.then_inc(s_psO, 1)

                hidden(0, 0, first=True)
                transposed(0, 0, first=True)
                hidden(1, 1, first=True)
                output(0, 0, first=True)
                with pe.Fori(1, STEPS - 2, 2) as n:
                    transposed(n, 1)
                    hidden(n + 1, 0)
                    output(n, 1)
                    transposed(n + 1, 0)
                    hidden(n + 2, 1)
                    output(n + 1, 0)
                transposed(STEPS - 1, 1)
                output(STEPS - 1, 1)


def phase_spread(nc, sem, io, g):
    resid, ident = g["resid"], g["ident"]
    with ExitStack() as stack:
        ph = Phase(nc, stack, "spr")
        o = ph.sb("o", [128, 4, 4, C])
        pick = ph.sb("pick", [128, T])
        stats = ph.sb("stats", [128, 2, 4, 6])
        mv = ph.sb("mv", [128, 2, 4, 2])
        var = ph.sb("var", [128, 2, 4])
        rstd = ph.sb("rstd", [128, 2, 4])
        halfneg = ph.sb("halfneg", [128, 4])
        eps = ph.sb("eps", [128, 4])
        yn = ph.sb("yn", [128, 4, C])
        xn = ph.sb("xn", [128, 2, 4, C])
        ow = ph.sb("ow", [128, 2, 2, C])
        psY = ph.ps("psY", [128, 2, 512])
        psT = ph.ps("psT", [128, 2, 4, 128])

        def S(n):
            return sem("spr_" + n)

        (o_loaded, const, s_zero, s_pick, s_psY, s_yn, s_resid, s_xn, s_psT, s_xT) = (S(n) for n in (
            "o_loaded", "const", "zero", "pick", "psY", "yn", "resid", "xn", "psT", "xT"))
        s_stats, s_mv, s_var, s_rstd = ([S(n + "_out"), S(n + "_res")] for n in ("stats", "mv", "var", "rstd"))
        STEPS = B // 2
        with nc.Block() as block:
            @block.sync
            def _(sp):
                sp.wait_ge(s_zero, 1)
                for b in range(4):
                    sp.dma_start(o[32 * b:32 * b + 32, :, b, :],
                                 io["o_dram"].rearrange("(q b) e c -> b e q c", q=4)[b]).then_inc(o_loaded, 16)
                for later in ("at1", "moe"):
                    g[later].load(sp, io)

            @block.gpsimd
            def _(pool):
                nc.gpsimd.memset(eps[:], LN_EPS)
                nc.gpsimd.memset(halfneg[:], -0.5).then_inc(const, 1)
                pool.wait_ge(const, 1)

                def spread(k, n):
                    pool.wait_ge(s_mv[k], n + 1)
                    nc.gpsimd.tensor_tensor(var[:, k], mv[:, k, :, 1], eps[:], ALU.add).then_inc(s_var[k], 1)
                    pool.wait_ge(s_var[k], n + 1)
                    nc.gpsimd.tensor_tensor(rstd[:, k], var[:, k], halfneg[:], ALU.pow).then_inc(s_rstd[k], 1)

                spread(0, 0)
                with pool.Fori(0, STEPS - 1) as n:
                    spread(1, n)
                    spread(0, n + 1)
                spread(1, STEPS - 1)

            @block.vector
            def _(dve):
                nc.vector.memset(o[:], 0.0).then_inc(s_zero, 1)
                dve.wait_ge(o_loaded, 64)

                def moments(k, n, rows):
                    for i in range(4):
                        last = nc.vector.bn_stats(stats[:, k, i, :], rows(i))
                    last.then_inc(s_stats[k], 1)
                    settled = count_in_register(dve, n + 1)
                    settle(dve, o_loaded)
                    dve.wait_ge(s_stats[k], settled)
                    for i in range(4):
                        last = nc.vector.bn_aggr(mv[:, k, i, :], stats[:, k, i, :])
                    last.then_inc(s_mv[k], 1)

                def operands(q, x):
                    if x == 0:
                        dve.wait_ge(s_psY, 2 * q)
                        nc.vector.tensor_copy(pick[:], g["pick"][:, ds(q, 1), :].rearrange("p o t -> p (o t)"))
                    nc.vector.tensor_copy(ow[:, x], o[:, ds(q, 1), 2 * x:2 * x + 2].rearrange("p o b c -> p (o b) c")).then_inc(s_pick, 1)

                def out_row(x, i):
                    at = C * (2 * (i % 2) + i // 2)
                    return psY[:, x, at:at + C]

                def outputs(n, x):
                    dve.wait_ge(s_psY, n + 1)
                    moments(0, n, lambda i: out_row(x, i))

                def add(n, x):
                    dve.wait_ge(s_rstd[0], n + 1)
                    for i in range(4):
                        last = nc.vector.tensor_scalar(yn[:, i, :], out_row(x, i), mv[:, 0, i, 0:1], rstd[:, 0, i:i + 1],
                                                       ALU.subtract, ALU.mult)
                    last.then_inc(s_yn, 1)
                    dve.wait_ge(s_yn, n + 1)
                    rows = resid[:, ds(4 * n, 4), :]
                    nc.vector.tensor_tensor(rows, rows, yn[:], ALU.add).then_inc(s_resid, 1)
                    settled = count_in_register(dve, n + 1)
                    settle(dve, o_loaded)
                    dve.wait_ge(s_resid, settled)
                    moments(1, n, lambda i: resid[:, ds(4 * n + i, 1), :])

                def normalize(n, x, early=False):
                    dve.wait_ge(s_rstd[1], n + 1)
                    if not early:
                        dve.wait_ge(s_psT, n - 1)
                    for i in range(4):
                        last = nc.vector.tensor_scalar(xn[:, x, i, :], resid[:, ds(4 * n + i, 1), :].rearrange("p o c -> p (o c)"),
                                                       mv[:, 1, i, 0:1], rstd[:, 1, i:i + 1], ALU.subtract, ALU.mult)
                    last.then_inc(s_xn, 1)

                operands(0, 0)
                operands(0, 1)
                outputs(0, 0)
                add(0, 0)
                outputs(1, 1)
                normalize(0, 0, early=True)
                with dve.Fori(0, 3) as q:
                    add(2 * q + 1, 1)
                    operands(q + 1, 0)
                    operands(q + 1, 1)
                    outputs(2 * q + 2, 0)
                    normalize(2 * q + 1, 1)
                    add(2 * q + 2, 0)
                    outputs(2 * q + 3, 1)
                    normalize(2 * q + 2, 0)
                add(7, 1)
                normalize(7, 1)

            @block.scalar
            def _(act):
                with act.Fori(0, STEPS - 1, 2) as n:
                    for x in range(2):
                        act.wait_ge(s_psT, n + x + 1)
                        nc.scalar.copy(g["xT_all"][:, ds(512 * (n + x), 512)], flat(psT[:, x])).then_inc(s_xT, 1)

            @block.tensor
            def _(pe):
                def outputs(n, x, early=False):
                    pe.wait_ge(s_pick, n + 1)
                    if not early:
                        pe.wait_ge(s_yn, n - 1)
                    for t in range(2):
                        last = nc.tensor.matmul(psY[:, x, 2 * C * t:2 * C * t + 2 * C], pick[:, 128 * t:128 * t + 128], flat(ow[:, x]),
                                                start=True, stop=True, skip_group_check=True)
                    last.then_inc(s_psY, 1)

                def transposes(n, x, early=False):
                    pe.wait_ge(s_xn, n + 1)
                    if not early:
                        pe.wait_ge(s_xT, n - 1)
                    for i in range(4):
                        last = nc.tensor.transpose(psT[:, x, i, :], xn[:, x, i, :], ident[:])
                    last.then_inc(s_psT, 1)

                outputs(0, 0, early=True)
                outputs(1, 1, early=True)
                transposes(0, 0, early=True)
                with pe.Fori(1, STEPS - 2, 2) as n:
                    outputs(n + 1, 0)
                    transposes(n, 1)
                    outputs(n + 2, 1)
                    transposes(n + 1, 0)
                transposes(STEPS - 1, 1)


KV1, REP1, HD1, LAT1 = 2, 4, 128, 32
UNITS1 = 12
KIND1 = ["hi", "hi", "lo"]


class Turn1(Turn):

    UNITS, PLAN = UNITS1, {1: ["k_0"], 3: ["q_0"], 5: ["k_1"], 6: ["y"], 9: ["q_1"], 11: ["v"]}
    OF_BATCH = set()
    VALUES = {7: (0, 0), 10: (1, 0), 1: (2, 1), 4: (3, 1)}


def phase_attend1(nc, sem, io, g):
    resid, ident, ident_b = g["resid"], g["ident"], g["ident_b"]
    with ExitStack() as stack:
        ph = Phase(nc, stack, "at1")
        wqT = g["at1"].at["wqT"]
        wkuT = g["at1"].at["wkuT"]
        wvuT = g["at1"].at["wvuT"]
        wo = g["at1"].at["wo"]
        w_k = g["at1"].at["w_k"]
        w_v = g["at1"].at["w_v"]
        w_qk = ph.sb("w_qk", [C, KV1, 128])
        w_vo = ph.sb("w_vo", [128, KV1, C])
        mask = g["at1"].at["mask"]
        mask_b = ph.sb("mask_b", [128, 512], BF16)
        xT = ph.sb("xT", [C, 2, T])
        q = ph.sb("q", [128, 2, 2, KV1, T])
        k = ph.sb("k", [128, 2, 2, KV1, REP1, T])
        val = ph.sb("val", [128, 2, 2, 2, KV1 * LAT1])
        p = ph.sb("p", [128, P_RING, 512])
        nm = ph.sb("nm", [128, P_RING, 4])
        z = ph.sb("z", [128, P_RING, 4])
        rz = ph.sb("rz", [128, P_RING, 4])
        pT = ph.sb("pT", [128, 2, REP1, 384])
        oT = ph.sb("oT", [128, 4, T])
        halfneg = ph.sb("halfneg", [128, 4])
        eps = ph.sb("eps", [128, 4])
        stats = ph.sb("stats", [128, 4, 6])
        mv = ph.sb("mv", [128, 4, 2])
        var = ph.sb("var", [128, 4])
        rstd = ph.sb("rstd", [128, 4])
        y = ph.sb("y", [128, 4, C])
        yn = ph.sb("yn", [128, 4, C])
        stats_r = ph.sb("stats_r", [128, 4, 6])
        mv_r = ph.sb("mv_r", [128, 4, 2])
        var_r = ph.sb("var_r", [128, 4])
        rstd_r = ph.sb("rstd_r", [128, 4])
        psS = ph.ps("psS", [128, 3, 512])
        psT = ph.ps("psT", [128, 2, 512])
        psO = ph.ps("psO", [128, 512])
        psM = ph.ps("psM", [128, 2, 512])

        def S(n):
            return sem("at1_" + n)

        (const, k_zero, mask_ready, wprod, w_ready, xT_loaded, scores_full, max_ready, exp_ready, recip_ready, norm_ready,
         pT_full, evac_even, evac_odd, o_full, o_ready, misc_full, k_ready, q_ready, v_ready, s_stats, s_mv, s_var, s_rstd, s_yn,
         s_resid) = (S(n) for n in (
             "const", "k_zero", "mask_ready", "wprod", "w_ready", "xT_loaded", "scores_full", "max_ready", "exp_ready",
             "recip_ready", "norm_ready", "pT_full", "evac_even", "evac_odd", "o_full", "o_ready", "misc_full", "k_ready",
             "q_ready", "v_ready", "stats", "mv", "var", "rstd", "yn", "resid"))
        r_stats, r_mv, r_var, r_rstd, r_xn = (S("r_" + n) for n in ("stats", "mv", "var", "rstd", "xn"))
        N_TURNS = B // 2
        ADD, MOMENTS, POWER, NORMALIZE = 8, 9, 9, 11

        def turns(engine, body):
            body(Turn1("first", 0))
            body(Turn1("second", 0, 0))
            with engine.Fori(0, N_TURNS // 2 - 1) as i:
                body(Turn1("body", 2 * i + 1, 1))
                body(Turn1("body", 2 * i + 2, 0))
            body(Turn1("last", N_TURNS - 1, 1))
            body(Turn1("drain", N_TURNS, 0))

        def pT_unused(u, t):
            grp = u // 3 - 1
            return max(grp, 0) if t.mode == "second" else 4 * t.b + grp

        def emptied(n, t):
            i = int(n[-1]) if n[-1].isdigit() else 0
            return {"k": (k_ready, 2 * t.pb + i + 1), "q": (q_ready, 2 * t.pb + i + 1), "v": (v_ready, t.pb + 1),
                    "y": (s_stats, t.b)}[n[0]]

        def evacuate(copy, u):
            grp = u // 3
            bank = psT[:, u % 2, :]
            if KIND1[u % 3] == "hi":
                heads = slice(2 * (u % 3), 2 * (u % 3) + 2)
                return copy(pT[:, grp % 2, heads, 128:384], bank.rearrange("p (r x) -> p r x", r=2))
            return copy(pT[:, grp % 2, :, 0:128], bank.rearrange("p (r x) -> p r x", r=4))

        loaded = g["at1"].loaded
        with nc.Block() as block:
            @block.sync
            def _(sp):

                def body(t):
                    if t.projects:
                        if t.attends:
                            sp.wait_ge(misc_full, t.full_before("v"))
                        sp.dma_start(flat(xT[:]), g["xT_all"][:, ds(2 * T * t.pb, 2 * T)]).then_inc(xT_loaded, 16)

                turns(sp, body)

            @block.gpsimd
            def _(pool):
                nc.gpsimd.memset(eps[:], LN_EPS)
                nc.gpsimd.memset(halfneg[:], -0.5).then_inc(const, 1)
                pool.wait_ge(const, 1)

                def body(t):
                    for s in range(UNITS1):
                        if t.stage(s, 1):
                            u, of = t.stage(s, 1)
                            r, n_ = u % P_RING, 2 if KIND1[u % 3] == "hi" else 4
                            pool.wait_ge(recip_ready, of.unit(u))
                            pv = p[:, r, :].rearrange("p (a k) -> p a k", a=n_)
                            nc.gpsimd.tensor_tensor(pv, pv, rz[:, r, 0:n_].unsqueeze(2).to_broadcast([128, n_, 512 // n_]),
                                                    ALU.mult).then_inc(norm_ready, 1)
                        if "y" in t.tasks(s):
                            pool.wait_ge(s_mv, t.b)
                            nc.gpsimd.tensor_tensor(var[:], mv[:, :, 1], eps[:], ALU.add).then_inc(s_var, 1)
                            pool.wait_ge(s_var, t.b)
                            nc.gpsimd.tensor_tensor(rstd[:], var[:], halfneg[:], ALU.pow).then_inc(s_rstd, 1)
                        if s == POWER and t.follows:
                            pool.wait_ge(r_mv, t.b)
                            nc.gpsimd.tensor_tensor(var_r[:], mv_r[:, :, 1], eps[:], ALU.add).then_inc(r_var, 1)
                            pool.wait_ge(r_var, t.b)
                            nc.gpsimd.tensor_tensor(rstd_r[:], var_r[:], halfneg[:], ALU.pow).then_inc(r_rstd, 1)

                turns(pool, body)

            @block.vector
            def _(dve):
                nc.vector.memset(k[:].rearrange("p a b c d e -> p (a b c d e)"), 0.0).then_inc(k_zero, 1)
                dve.wait_ge(loaded, 16 * 7)
                nc.vector.tensor_copy(mask_b[:], mask[:]).then_inc(mask_ready, 1)
                dve.wait_ge(wprod, 1)
                nc.vector.tensor_scalar(flat(w_qk[:]), psM[:, 0, 0:256], float(HD1) ** -0.5, None, ALU.mult)
                nc.vector.tensor_copy(flat(w_vo[:]), psM[:, 1, 0:256]).then_inc(w_ready, 1)

                def add_y(b):
                    dve.wait_ge(s_rstd, b + 1)
                    for i in range(4):
                        last = nc.vector.tensor_scalar(yn[:, i, :], y[:, i, :], mv[:, i, 0:1], rstd[:, i:i + 1],
                                                       ALU.subtract, ALU.mult)
                    last.then_inc(s_yn, 1)
                    dve.wait_ge(s_yn, b + 1)
                    rows = resid[:, ds(4 * b, 4), :]
                    nc.vector.tensor_tensor(rows, rows, yn[:], ALU.add).then_inc(s_resid, 1)

                def moments(b):
                    settled = count_in_register(dve, b + 1)
                    settle(dve, loaded)
                    dve.wait_ge(s_resid, settled)
                    for i in range(4):
                        last = nc.vector.bn_stats(stats_r[:, i, :], resid[:, ds(4 * b + i, 1), :])
                    last.then_inc(r_stats, 1)
                    settled = count_in_register(dve, b + 1)
                    settle(dve, loaded)
                    dve.wait_ge(r_stats, settled)
                    for i in range(4):
                        last = nc.vector.bn_aggr(mv_r[:, i, :], stats_r[:, i, :])
                    last.then_inc(r_mv, 1)

                def normalize(b):
                    dve.wait_ge(r_rstd, b + 1)
                    for i in range(4):
                        last = nc.vector.tensor_scalar(g["xn"][:, ds(4 * b + i, 1), :].rearrange("p o c -> p (o c)"),
                                                       resid[:, ds(4 * b + i, 1), :].rearrange("p o c -> p (o c)"),
                                                       mv_r[:, i, 0:1], rstd_r[:, i:i + 1], ALU.subtract, ALU.mult)
                    last.then_inc(r_xn, 1)

                def body(t):
                    for s in range(UNITS1):
                        if t.attends:
                            n_ = 2 if KIND1[s % 3] == "hi" else 4
                            dve.wait_ge(scores_full, t.unit(s))
                            nc.vector.tensor_reduce(nm[:, s % P_RING, 0:n_], psS[:, s % 3, :].rearrange("p (a k) -> p a k", a=n_),
                                                    AX.X, ALU.max, negate=True).then_inc(max_ready, 1)
                        for n in t.tasks(s):
                            bank = psM[:, t.bank(n), :]
                            if n[0] == "q":
                                dve.wait_ge(misc_full, t.full(n))
                                nc.vector.tensor_copy(q[:, t.phalf, int(n[-1])], bank.rearrange("p (v t) -> p v t", v=KV1)).then_inc(q_ready, 1)
                            if n == "v":
                                dve.wait_ge(misc_full, t.full(n))
                                if t.follows:
                                    dve.wait_ge(o_full, 4 * t.b)
                                nc.vector.tensor_copy(val[:, t.phalf], bank[:, 0:256].rearrange("p (b t l) -> p b t l", b=2, t=2)).then_inc(v_ready, 1)
                            if n == "y":
                                dve.wait_ge(misc_full, t.full(n))
                                dve.wait_ge(s_yn, t.b - 1)
                                nc.vector.tensor_copy(flat(y[:]), bank)
                                for i in range(4):
                                    last = nc.vector.bn_stats(stats[:, i, :], bank[:, C * i:C * i + C])
                                last.then_inc(s_stats, 1)
                                settled = count_in_register(dve, t.b)
                                settle(dve, loaded)
                                dve.wait_ge(s_stats, settled)
                                for i in range(4):
                                    last = nc.vector.bn_aggr(mv[:, i, :], stats[:, i, :])
                                last.then_inc(s_mv, 1)
                        if t.stage(s, 1):
                            u, of = t.stage(s, 1)
                            r, n_ = u % P_RING, 2 if KIND1[u % 3] == "hi" else 4
                            dve.wait_ge(exp_ready, of.unit(u))
                            nc.vector.reciprocal(rz[:, r, 0:n_], z[:, r, 0:n_]).then_inc(recip_ready, 1)
                        if t.stage(s, LAG):
                            u, of = t.stage(s, LAG)
                            if u % 2 == 0:
                                dve.wait_ge(pT_full, of.unit(u))
                                dve.wait_ge(o_full, pT_unused(u, of))
                                evacuate(nc.vector.tensor_copy, u).then_inc(evac_even, 1)
                        if s == ADD and t.follows:
                            add_y(t.b - 1)
                        if s == MOMENTS and t.follows:
                            moments(t.b - 1)
                        if s == NORMALIZE and t.follows:
                            normalize(t.b - 1)

                turns(dve, body)

            @block.scalar
            def _(act):
                act.wait_ge(k_zero, 1)

                def body(t):
                    for s in range(UNITS1):
                        if t.attends:
                            r, n_ = s % P_RING, 2 if KIND1[s % 3] == "hi" else 4
                            w = 512 // n_
                            act.wait_ge(max_ready, t.unit(s))
                            act.wait_ge(pT_full, t.unit(s, P_RING))
                            for i in range(n_):
                                last = nc.scalar.activation(p[:, r, w * i:w * i + w], psS[:, s % 3, w * i:w * i + w], ACT.Exp,
                                                            bias=nm[:, r, i:i + 1], accum_out=z[:, r, i:i + 1])
                            last.then_inc(exp_ready, 1)
                        for n in t.tasks(s):
                            if n[0] == "k":
                                act.wait_ge(misc_full, t.full(n))
                                for r in range(REP1):
                                    rows = slice(32 * r, 32 * r + 32)
                                    last = nc.scalar.copy(k[rows, t.phalf, int(n[-1]), :, r, :],
                                                          psM[rows, t.bank(n), :].rearrange("p (v t) -> p v t", v=KV1))
                                last.then_inc(k_ready, 1)
                        if t.stage(s, LAG):
                            u, of = t.stage(s, LAG)
                            if u % 2 == 1:
                                act.wait_ge(pT_full, of.unit(u))
                                act.wait_ge(o_full, pT_unused(u, of))
                                evacuate(nc.scalar.copy, u).then_inc(evac_odd, 1)
                        if t.values_group(s):
                            grp, of = t.values_group(s)
                            act.wait_ge(o_full, 4 * of.b + grp + 1)
                            if grp == 0 and t.follows:
                                act.wait_ge(misc_full, t.full("y"))
                            nc.scalar.copy(oT[:, grp, :], psO[:, 0:T]).then_inc(o_ready, 1)

                turns(act, body)

            @block.tensor
            def _(pe):
                pe.wait_ge(loaded, 16 * 7)
                pe.wait_ge(mask_ready, 1)
                pe.wait_ge(k_zero, 1)

                def mm(out, lhsT, rhs, start=True, stop=True):
                    return nc.tensor.matmul(out, lhsT, rhs, start=start, stop=stop, skip_group_check=True)

                for h in range(8):
                    v, r = h // REP1, h % REP1
                    mm(psM[:, 0, 32 * h:32 * h + 32], wqT[:, h, :], wkuT[:])
                    last = mm(psM[32 * r:32 * r + 32, 1, C * v:C * v + C], wvuT[:], wo[:, h, :])
                last.then_inc(wprod, 1)
                pe.wait_ge(w_ready, 1)

                def task(n, t):
                    bank = psM[:, t.bank(n), :]
                    i = int(n[-1]) if n[-1].isdigit() else 0
                    filled_before = t.last_in_bank(n)
                    if filled_before is not None:
                        by, count = emptied(*filled_before)
                        pe.wait_ge(by, count)
                    if n == "y":
                        pe.wait_ge(o_ready, 4 * t.b)
                    if n == "k_0":
                        pe.wait_ge(xT_loaded, 16 * (t.pb + 1))
                    if n[0] == "k":
                        for v in range(KV1):
                            last = mm(bank[:, T * v:T * v + T], w_k[:, v, :], xT[:, i, :])
                    if n[0] == "q":
                        for v in range(KV1):
                            last = mm(bank[:, T * v:T * v + T], w_qk[:, v, :], xT[:, i, :])
                    if n == "v":
                        for b in range(2):
                            for tile in range(2):
                                last = mm(bank[:, 64 * (2 * b + tile):64 * (2 * b + tile) + 64],
                                          xT[:, b, 128 * tile:128 * tile + 128], w_v[:])
                    if n == "y":
                        for b in range(2):
                            for tile in range(2):
                                at = C * (2 * b + tile)
                                for v in range(KV1):
                                    last = mm(bank[:, at:at + C], oT[:, 2 * b + v, 128 * tile:128 * tile + 128], w_vo[:, v, :], v == 0, v == 1)
                    last.then_inc(misc_full, 1)

                def scores(u, t):
                    grp = u // 3
                    b, v = grp // 2, grp % 2
                    bank = psS[:, u % 3, :]
                    if u == 0:
                        pe.wait_ge(k_ready, 2 * (t.b + 1))
                        pe.wait_ge(q_ready, 2 * (t.b + 1))
                    pe.wait_ge(exp_ready, t.unit(u, 3))
                    if KIND1[u % 3] == "hi":
                        heads = slice(2 * (u % 3), 2 * (u % 3) + 2)
                        mm(bank, q[:, t.half, b, v, 128:256], k[:, t.half, b, v, heads, :], True, False)
                        last = mm(bank.rearrange("p (a x) -> p a x", a=2)[:, :, 128:256], ident_b[:], mask_b[:, 0:256], False, True)
                    else:
                        mm(bank, q[:, t.half, b, v, 0:128], k[:, t.half, b, v, :, 0:128], True, False)
                        last = mm(bank, ident_b[:], mask_b[:], False, True)
                    last.then_inc(scores_full, 1)

                def transposes(u, t):
                    pe.wait_ge(norm_ready, t.unit(u))
                    pe.wait_ge(evac_even if u % 2 == 0 else evac_odd, t.b * (UNITS1 // 2) + u // 2)
                    for i in range(4):
                        last = nc.tensor.transpose(psT[:, u % 2, 128 * i:128 * i + 128], p[:, u % P_RING, 128 * i:128 * i + 128], ident[:])
                    last.then_inc(pT_full, 1)

                def values(grp, t):
                    b, v = grp // 2, grp % 2
                    done = 3 * grp + 3
                    pe.wait_ge(evac_even, t.b * (UNITS1 // 2) + (done + 1) // 2)
                    pe.wait_ge(evac_odd, t.b * (UNITS1 // 2) + done // 2)
                    pe.wait_ge(v_ready, t.b + 1)
                    pe.wait_ge(o_ready, 4 * t.b + grp)
                    for tile in range(2):
                        for r in range(REP1):
                            cols = slice(0, 256) if tile == 0 else slice(256, 384)
                            last = mm(psO[32 * r:32 * r + 32, 128 * tile:256], val[:, t.half, b, tile, 32 * v:32 * v + 32],
                                      pT[:, grp % 2, r, cols], tile == 0, tile == 1)
                    last.then_inc(o_full, 1)

                def body(t):
                    for s in range(UNITS1):
                        if t.attends:
                            scores(s, t)
                        for n in t.tasks(s):
                            task(n, t)
                        if t.values_group(s):
                            values(*t.values_group(s))
                        if t.stage(s, LAG):
                            transposes(*t.stage(s, LAG))

                turns(pe, body)


E1, TOP1, INTER1 = 8, 2, 128


def phase_route(nc, sem, io, g):
    ident = g["ident"]
    with ExitStack() as stack:
        ph = Phase(nc, stack, "rou")
        gate_b = g["rou"].at["gate_b"]
        prob = ph.sb("prob", [128, NT, E1])
        m = ph.sb("m", [128, NT])
        z = ph.sb("z", [128, NT])
        top = ph.sb("top", [128, NT, E1])
        rest = ph.sb("rest", [128, NT, E1])
        psT = ph.ps("psT", [C, 4, 512])
        psR = ph.ps("psR", [128, NT, E1])
        psG = ph.ps("psG", [E1 + 1, 2, 512])
        gate_w = g["rou"].at["gate_w"]
        s_psT, s_xT_even, s_xT_odd, s_psR = (sem("rou_" + n) for n in ("psT", "xT_even", "xT_odd", "psR"))
        const, s_step, s_exp, s_weights, s_psG, s_wT = (sem("rou_" + n) for n in ("const", "step", "exp", "weights", "psG", "wT"))
        with nc.Block() as block:
            @block.gpsimd
            def _(pool):
                nc.gpsimd.memset(g["w_tok"][:, :, E1:E1 + 1], 1.0).then_inc(const, 1)

            @block.vector
            def _(dve):
                wide = [128, NT, E1]
                dve.wait_ge(g["rou"].loaded, g["rou"].all)
                for k in range(1, 8, 2):
                    dve.wait_ge(s_psT, k + 1)
                    nc.vector.tensor_copy(g["xT_all"][:, 512 * k:512 * k + 512], psT[:, k % 4, :]).then_inc(s_xT_odd, 1)
                dve.wait_ge(s_psR, 8)
                nc.vector.tensor_tensor(prob[:], psR[:], gate_b[:].unsqueeze(1).to_broadcast(wide), ALU.add).then_inc(s_step, 1)
                dve.wait_ge(s_step, 1)
                nc.vector.reduce_max(m[:], prob[:], AX.X).then_inc(s_step, 1)
                dve.wait_ge(s_step, 2)
                nc.vector.tensor_tensor(prob[:], prob[:], m[:].unsqueeze(2).to_broadcast(wide), ALU.subtract).then_inc(s_step, 1)
                dve.wait_ge(s_exp, 1)
                nc.vector.reduce_sum(z[:], prob[:], AX.X).then_inc(s_step, 1)
                dve.wait_ge(s_step, 4)
                nc.vector.reciprocal(m[:], z[:]).then_inc(s_step, 1)
                dve.wait_ge(s_step, 5)
                nc.vector.tensor_tensor(prob[:], prob[:], m[:].unsqueeze(2).to_broadcast(wide), ALU.mult).then_inc(s_step, 1)
                dve.wait_ge(s_step, 6)
                for t in range(NT):
                    last = nc.vector.max(top[:, t, :], prob[:, t, :])
                last.then_inc(s_step, 1)
                dve.wait_ge(s_step, 7)
                nc.vector.memset(top[:, :, TOP1:], -1.0).then_inc(s_step, 1)
                dve.wait_ge(s_step, 8)
                for t in range(NT):
                    last = nc.vector.match_replace(out=rest[:, t, :], in_to_replace=top[:, t, :], in_values=prob[:, t, :], imm_value=0.0)
                last.then_inc(s_step, 1)
                dve.wait_ge(s_step, 9)
                nc.vector.tensor_tensor(g["w_tok"][:, :, 0:E1], prob[:], rest[:], ALU.subtract).then_inc(s_weights, 1)

            @block.scalar
            def _(act):
                for k in range(0, 8, 2):
                    act.wait_ge(s_psT, k + 1)
                    nc.scalar.copy(g["xT_all"][:, 512 * k:512 * k + 512], psT[:, k % 4, :]).then_inc(s_xT_even, 1)
                act.wait_ge(s_step, 3)
                nc.scalar.activation(prob[:], prob[:], ACT.Exp).then_inc(s_exp, 1)
                for k in range(8):
                    act.wait_ge(s_psG, k + 1)
                    nc.scalar.copy(g["w_tokT"][:, 512 * k:512 * k + 512], psG[:, k % 2, :]).then_inc(s_wT, 1)

            @block.tensor
            def _(pe):
                pe.wait_ge(g["rou"].loaded, g["rou"].all)

                def logits(k):
                    pe.wait_ge(s_xT_even if k % 2 == 0 else s_xT_odd, k // 2 + 1)
                    for t in range(4 * k, 4 * k + 4):
                        last = nc.tensor.matmul(psR[:, t, :], g["xT_all"][:, 128 * t:128 * t + 128], gate_w[:], start=True, stop=True,
                                                skip_group_check=True)
                    last.then_inc(s_psR, 1)

                for k in range(8):
                    if k >= 4:
                        pe.wait_ge(s_xT_even if k % 2 == 0 else s_xT_odd, (k - 4) // 2 + 1)
                    for i in range(4):
                        last = nc.tensor.transpose(psT[:, k % 4, 128 * i:128 * i + 128], g["xn"][:, 4 * k + i, :], ident[:])
                    last.then_inc(s_psT, 1)
                    if k >= 2:
                        logits(k - 2)
                logits(6)
                logits(7)
                pe.wait_ge(s_weights, 1)
                pe.wait_ge(const, 1)
                for k in range(8):
                    if k >= 2:
                        pe.wait_ge(s_wT, k - 1)
                    for i in range(4):
                        last = nc.tensor.transpose(psG[:, k % 2, 128 * i:128 * i + 128], g["w_tok"][:, 4 * k + i, :], ident[:])
                    last.then_inc(s_psG, 1)


SHARED1 = 256 // INTER1


def phase_moe(nc, sem, io, g):
    resid = g["resid"]
    N = E1 + SHARED1
    with ExitStack() as stack:
        ph = Phase(nc, stack, "moe")
        w1 = g["moe"].at["w1"]
        w3 = g["moe"].at["w3"]
        w2 = g["moe"].at["w2"]
        b1 = g["moe"].at["b1"]
        b3 = g["moe"].at["b3"]
        b2 = g["moe"].at["b2"]
        wT = ph.sb("wT", [E1 + 1, 512])
        s1 = ph.sb("s1", [INTER1, 2, 512])
        hT = ph.sb("hT", [INTER1, 2, 512])
        hs = ph.sb("hs", [INTER1, SHARED1, 512])
        acc = ph.sb("acc", [128, 2, 4, C])
        total = ph.sb("total", [128, 4, C])
        stats = ph.sb("stats", [128, 4, 6])
        mv = ph.sb("mv", [128, 4, 2])
        var = ph.sb("var", [128, 4])
        rstd = ph.sb("rstd", [128, 4])
        halfneg = ph.sb("halfneg", [128, 4])
        eps = ph.sb("eps", [128, 4])
        wrow = ph.sb("wrow", [128, 4, E1])
        y = ph.sb("y", [128, 4, C])
        out = ph.sb("out", [128, 4, C])
        ps1 = ph.ps("ps1", [INTER1, 2, 512])
        ps3 = ph.ps("ps3", [INTER1, 2, 512])
        psY = ph.ps("psY", [128, 3, 4, C])

        def S(n):
            return sem("moe_" + n)

        s_wrow = S("wrow")
        (const, wT_loaded, s_up, s_silu, s_h, s_down, s_acc, s_stats, s_mv, s_var, s_rstd, s_y, s_out, stored) = (S(n) for n in (
            "const", "wT_loaded", "up", "silu", "h", "down", "acc", "stats", "mv", "var", "rstd", "y", "out", "stored"))
        TURNS = NT // 4
        D = E1 + 1
        loaded = g["moe"].loaded
        with nc.Block() as block:
            @block.sync
            def _(sp):
                with sp.Fori(0, TURNS) as i:
                    sp.wait_ge(s_down, D * i)
                    sp.dma_start(wT[:], g["w_tokT"][:, ds(512 * i, 512)]).then_inc(wT_loaded, 16)
                    sp.wait_ge(s_out, i + 1)
                    sp.dma_start(io["out"][:, ds(4 * i, 4), :], out[:]).then_inc(stored, 16)
                sp.wait_ge(stored, 16 * TURNS)

            @block.gpsimd
            def _(pool):
                nc.gpsimd.memset(eps[:], LN_EPS)
                nc.gpsimd.memset(halfneg[:], -0.5).then_inc(const, 1)
                pool.wait_ge(const, 1)
                with pool.Fori(0, TURNS) as i:
                    pool.wait_ge(s_mv, i + 1)
                    nc.gpsimd.tensor_tensor(var[:], mv[:, :, 1], eps[:], ALU.add).then_inc(s_var, 1)
                    pool.wait_ge(s_var, i + 1)
                    nc.gpsimd.tensor_tensor(rstd[:], var[:], halfneg[:], ALU.pow).then_inc(s_rstd, 1)
                    pool.wait_ge(s_y, i + 1)
                    pool.wait_ge(stored, 16 * i)
                    nc.gpsimd.tensor_tensor(out[:], resid[:, ds(4 * i, 4), :], y[:], ALU.add).then_inc(s_out, 1)

            @block.scalar
            def _(act):
                act.wait_ge(loaded, 16 * 6)
                with act.Fori(0, TURNS) as i:
                    for n in range(N):
                        act.wait_ge(s_up, N * i + n + 1)
                        act.wait_ge(s_h, N * i + max(n - 1, 0))
                        nc.scalar.activation(s1[:, n % 2, :], ps1[:, n % 2, :], ACT.Silu, bias=b1[:, n:n + 1]).then_inc(s_silu, 1)

            @block.vector
            def _(dve):
                dve.wait_ge(loaded, 16 * 6)

                def accumulate(i, e):
                    place = e if e < E1 - 1 else E1
                    dve.wait_ge(s_down, D * i + place + 1)
                    if e:
                        dve.wait_ge(s_acc, D * i + place)
                    for t in range(4):
                        down = psY[:, place % 3, t, :]
                        if e == 0:
                            last = nc.vector.tensor_scalar(acc[:, 0, t, :], down, wrow[:, t, 0:1], None, ALU.mult)
                        else:
                            dst = acc[:, e % 2, t, :] if e < E1 - 1 else total[:, t, :]
                            last = nc.vector.scalar_tensor_tensor(dst, down, wrow[:, t, e:e + 1], acc[:, 1 - place % 2, t, :],
                                                                  ALU.mult, ALU.add)
                    last.then_inc(s_acc, 1)

                def add_shared(i):
                    place = E1 - 1
                    dve.wait_ge(s_down, D * i + place + 1)
                    dve.wait_ge(s_acc, D * i + place)
                    nc.vector.tensor_tensor(acc[:, place % 2], psY[:, place % 3], acc[:, 1 - place % 2], ALU.add).then_inc(s_acc, 1)

                def moments(i):
                    settled = count_in_register(dve, D * i + D)
                    settle(dve, loaded)
                    dve.wait_ge(s_acc, settled)
                    for t in range(4):
                        last = nc.vector.bn_stats(stats[:, t, :], total[:, t, :])
                    last.then_inc(s_stats, 1)
                    settled = count_in_register(dve, i + 1)
                    settle(dve, loaded)
                    dve.wait_ge(s_stats, settled)
                    for t in range(4):
                        last = nc.vector.bn_aggr(mv[:, t, :], stats[:, t, :])
                    last.then_inc(s_mv, 1)

                def normalize(i):
                    dve.wait_ge(s_rstd, i + 1)
                    dve.wait_ge(s_out, i)
                    for t in range(4):
                        last = nc.vector.tensor_scalar(y[:, t, :], total[:, t, :], mv[:, t, 0:1], rstd[:, t:t + 1],
                                                       ALU.subtract, ALU.mult)
                    last.then_inc(s_y, 1)

                def body(i, follows):
                    if follows:
                        dve.wait_ge(s_acc, D * i)
                    nc.vector.tensor_copy(wrow[:], g["w_tok"][:, ds(4 * i, 4), 0:E1]).then_inc(s_wrow, 1)
                    dve.wait_ge(s_wrow, i + 1)
                    for n in range(N):
                        dve.wait_ge(s_silu, N * i + n + 1)
                        if n < SHARED1:
                            if follows:
                                dve.wait_ge(s_down, D * i)
                            dst = hs[:, n, :]
                        else:
                            if follows or n > SHARED1 + 1:
                                dve.wait_ge(s_down, D * i + max(n - SHARED1 - 1, 0))
                            dst = hT[:, n % 2, :]
                        nc.vector.scalar_tensor_tensor(dst, ps3[:, n % 2, :], b3[:, n:n + 1], s1[:, n % 2, :], ALU.add, ALU.mult).then_inc(s_h, 1)
                        if follows and n == SHARED1 - 1:
                            moments(i - 1)
                        if follows and n == SHARED1 + 1:
                            normalize(i - 1)
                        if n > SHARED1:
                            accumulate(i, n - SHARED1 - 1)
                    add_shared(i)
                    accumulate(i, E1 - 1)

                body(0, False)
                with dve.Fori(1, TURNS) as i:
                    body(i, True)
                moments(TURNS - 1)
                normalize(TURNS - 1)

            @block.tensor
            def _(pe):
                pe.wait_ge(loaded, 16 * 6)

                def mm(out, lhsT, rhs, start=True, stop=True):
                    return nc.tensor.matmul(out, lhsT, rhs, start=start, stop=stop, skip_group_check=True)

                with pe.Fori(0, TURNS) as i:
                    x = g["xT_all"][:, ds(512 * i, 512)]

                    def up(n):
                        pe.wait_ge(s_h, N * i + max(n - 1, 0))
                        mm(ps1[:, n % 2, :], w1[:, n, :], x)
                        mm(ps3[:, n % 2, :], w3[:, n, :], x).then_inc(s_up, 1)

                    def down(e, place):
                        pe.wait_ge(s_h, N * i + SHARED1 + e + 1)
                        pe.wait_ge(s_acc, D * i + max(place - 2, 0))
                        for t in range(4):
                            last = mm(psY[:, place % 3, t, :], hT[:, e % 2, 128 * t:128 * t + 128], w2[:, SHARED1 + e, :])
                        last.then_inc(s_down, 1)

                    for n in range(N):
                        up(n)
                        if n > SHARED1:
                            down(n - SHARED1 - 1, n - SHARED1 - 1)
                    place = E1 - 1
                    pe.wait_ge(wT_loaded, 16 * i + 16)
                    pe.wait_ge(s_acc, D * i + place - 2)
                    for t in range(4):
                        cols = slice(128 * t, 128 * t + 128)
                        for n in range(SHARED1):
                            mm(psY[:, place % 3, t, :], hs[:, n, cols], w2[:, n, :], n == 0, False)
                        last = mm(psY[:, place % 3, t, :], wT[:, cols], b2[:], False, True)
                    last.then_inc(s_down, 1)
                    down(E1 - 1, E1)


def build(nc, arrays):
    io = {}
    for name, a in arrays.items():
        io[name] = nc.dram_tensor(name, list(a.shape), F32, kind="ExternalInput").ap()
    io["ks_dram"] = nc.dram_tensor("ks_dram", [B, D0, 4, 4, KEEP], F32).ap()
    io["vs_dram"] = nc.dram_tensor("vs_dram", [B, KEEP, 512], F32).ap()
    io["o_dram"] = nc.dram_tensor("o_dram", [B, 32, C], F32).ap()
    io["out"] = nc.dram_tensor("out", [128, NT, C], F32, kind="ExternalOutput").ap()
    with ExitStack() as stack:
        def run(phase):
            held = []

            def sem(name):
                held.append(nc.alloc_semaphore(name))
                return held[-1]
            phase(nc, sem, io, g)
            nc.all_engine_barrier()
            nc.clear_and_free_semaphores(held)
            nc.all_engine_barrier()

        main = Phase(nc, stack, "main")
        g = {"resid": main.sb("resid", [128, NT, C]), "ident": main.sb("ident", [128, 128]),
             "ident_b": main.sb("ident_b", [128, 128], BF16), "xT_all": main.sb("xT_all", [C, B * T])}

        def early(stack, name, arrays):
            return Early(nc, Phase(nc, stack, name), arrays)

        g["cho"] = early(stack, "cho_e", {"gate_w": ([C, E0], "gate0_w"), "gate_b": ([128, 1], "gate0_b")})
        g["rou"] = early(stack, "rou_e", {"gate_w": ([C, E1], "gate1_w"), "gate_b": ([128, E1], "gate1_b")})
        with ExitStack() as layer0:
            l0 = Phase(nc, layer0, "l0")
            g["w_q"] = l0.sb("w_q", [QL, 4, 4, 128])
            g["w_val"] = l0.sb("w_val", [C, 2, 512])
            g["kv_scale"] = l0.sb("kv_scale", [128, 1])
            g["sel"] = l0.sb("sel", [C, B, KEEP])
            g["gates"] = l0.sb("gates", [128, B, 3])
            g["at0"] = early(layer0, "at0_e", {"w_tok": ([C, QL + KVL + ROPE], "w_tok"), "w_k": ([C, 3, 4, 128], "w_wink"), "w_out": ([128, 4, C], "w_proj"), "mask": ([128, 512], "c_mask"), "rope_q": ([128, 2, 512], "c_rope_q"), "rope_k": ([128, 2, 512], "c_rope_k"), "rope_t": ([128, 2, 128], "c_rope_t")})
            with ExitStack() as selection:
                g["sel_early"] = early(selection, "sel_e", {"w_imp": ([C, 128], "w_imp"), "before": ([128, 2, T], "c_before"), "upper": ([128, 128], "c_upper"), "iota": ([128, KEEP], "c_iota"), "w_gate": ([C, 3], "w_gate")})
                g["skv"] = early(selection, "skv_e", {"w_k": ([C, 3, 4, 128], "w_selk"), "w_v": ([C, 512], "w_selv"), "rope": ([128, 4, T], "c_rope_k")})
                run(phase_weights)
                run(phase_select)
                run(phase_sel_kv)
            run(phase_attend0)
        g["at1"] = early(stack, "at1_e", {"wqT": ([HD1, 8, C], "wq1T"), "wkuT": ([HD1, LAT1], "wk_upT"), "wvuT": ([HD1, LAT1], "wv_upT"), "wo": ([HD1, 8, C], "wo1"), "w_k": ([C, KV1, 128], "wk_down4"), "w_v": ([C, KV1 * LAT1], "wv_down"), "mask": ([128, 512], "c_mask")})
        g["moe"] = early(stack, "moe_e", {"w1": ([C, E1 + SHARED1, INTER1], "m_w1"), "w3": ([C, E1 + SHARED1, INTER1], "m_w3"), "w2": ([INTER1, E1 + SHARED1, C], "m_w2"), "b1": ([INTER1, E1 + SHARED1], "m_b1"), "b3": ([INTER1, E1 + SHARED1], "m_b3"), "b2": ([E1 + 1, C], "m_b2")})
        with ExitStack() as layer0:
            l0 = Phase(nc, layer0, "exp")
            g["pick"] = l0.sb("pick", [128, 4, T])
            g["merged"] = l0.sb("merged_all", [C, E0, B])
            g["exp_w1"] = l0.sb("w1", [128, 2, 4, HID0])
            g["exp_w1b"] = l0.sb("w1b", [4, 2, HID0])
            g["exp_w2"] = l0.sb("w2", [128, 2, 4, 4, C])
            g["exp_w2b"] = l0.sb("w2b", [4, 2, C])
            g["exp_rows"] = l0.sb("rows", [4, 128])
            g["exp_rows_loaded"] = nc.alloc_semaphore("exp_rows_loaded")
            for n in ("w1", "w2"):
                g[f"exp_{n}_loaded"] = [nc.alloc_semaphore(f"exp_{n}_loaded{x}") for x in range(2)]
            run(phase_choose)
            run(phase_experts)
            run(phase_spread)
        g["w_tok"] = main.sb("w_tok", [128, NT, E1 + 1])
        g["w_tokT"] = main.sb("w_tokT", [E1 + 1, B * T])
        with ExitStack() as ffn1:
            g["xn"] = Phase(nc, ffn1, "ffn1").sb("xn", [128, NT, C])
            run(phase_attend1)
            run(phase_route)
        run(phase_moe)


def lay_out(i):
    c = np.ascontiguousarray
    a = dict(causal_constants())
    a["x"] = c(i["L0_attn_x"].reshape(NT, 128, C).transpose(1, 0, 2))
    nope, rope = i["L0_attn_w_dq_nope"], i["L0_attn_w_dq_rope"].reshape(QL, H0, 2, HALF)
    a["w_q"] = c(np.stack([nope, rope[:, :, 0].reshape(QL, -1), rope[:, :, 1].reshape(QL, -1)], 1).reshape(QL, 3, 4, 128))
    a["w_dq_nopeT"] = c(nope.T.reshape(4, 128, QL).transpose(1, 0, 2))
    dk = i["L0_attn_w_dk_nope"].reshape(KVL, 4, 4, NOPE)
    diag = np.zeros((4, NOPE, 4, 4, KVL), np.float32)
    for j in range(4):
        diag[j, :, :, j, :] = dk[:, :, j, :].transpose(2, 1, 0)
    a["w_dk_diag"] = diag.reshape(128, 4, 128)
    a["w_ckvT"] = c(i["L0_attn_w_ckv"].T)
    a["w_dv"] = i["L0_attn_w_dv"]
    a["g_q"] = i["L0_attn_g_qnorm"].reshape(QL, 1)
    a["g_kv"] = i["L0_attn_g_kvnorm"].reshape(KVL, 1)
    a["w_winv"] = i["L0_attn_w_winv"]
    a["w_imp"] = c(np.broadcast_to(i["L0_attn_w_imp"], (C, 128)))
    a["w_gate"] = i["L0_attn_w_gate"]
    for n in ("wink", "selk"):
        w = i[f"L0_attn_w_{n}"].reshape(C, H0, 3, 32)
        a[f"w_{n}"] = c(w.transpose(0, 2, 1, 3).reshape(C, 3, 4, 128))
    a["w_selv"] = i["L0_attn_w_selv"]
    a["w_tok"] = np.concatenate([i["L0_attn_w_cq"], i["L0_attn_w_ckv"], i["L0_attn_w_krope"]], 1)
    a["w_proj"] = c(i["L0_attn_w_proj"].reshape(4, 128, C).transpose(1, 0, 2))
    a["gate0_w"] = c(i["L0_ffn_gate_w"].T)
    a["gate0_b"] = c(np.broadcast_to(i["L0_ffn_gate_b"], (4, 32))).reshape(128, 1)
    a["w1"], a["w2"] = i["L0_ffn_w1"], i["L0_ffn_w2"]
    a["wq1T"] = c(i["L1_attn_wq"].reshape(C, 8, HD1).transpose(2, 1, 0))
    a["wk_upT"], a["wv_upT"] = c(i["L1_attn_wk_up"].T), c(i["L1_attn_wv_up"].T)
    a["wo1"] = c(i["L1_attn_wo"].reshape(8, HD1, C).transpose(1, 0, 2))
    a["wk_down4"] = c(np.broadcast_to(i["L1_attn_wk_down"].reshape(C, KV1, 1, LAT1), (C, KV1, 4, LAT1))).reshape(C, KV1, 128)
    a["wv_down"] = i["L1_attn_wv_down"]
    a["gate1_w"] = c(i["L1_ffn_gate_w"].T)
    a["gate1_b"] = c(np.broadcast_to(i["L1_ffn_gate_b"], (128, E1)))
    shared = {k: i[f"L1_ffn_ws{k}"].reshape(SHARED1, INTER1, C) for k in (1, 3)}
    for k in (1, 3):
        a[f"m_w{k}"] = c(np.concatenate([shared[k], i[f"L1_ffn_w{k}"]]).transpose(2, 0, 1))
        a[f"m_b{k}"] = c(np.concatenate([i[f"L1_ffn_bs{k}"].reshape(SHARED1, INTER1), i[f"L1_ffn_b{k}"]]).T)
    ws2 = i["L1_ffn_ws2"].reshape(C, SHARED1, INTER1).transpose(2, 1, 0)
    a["m_w2"] = c(np.concatenate([ws2, i["L1_ffn_w2"].transpose(2, 0, 1)], 1))
    a["m_b2"] = np.concatenate([i["L1_ffn_b2"], i["L1_ffn_bs2"][None]])
    return {k: c(v) for k, v in a.items()}


def kernel(**inputs):
    import concourse.bacc as bacc
    from concourse.bass_utils import run_bass_kernel_spmd

    nc = bacc.Bacc("TRN2", target_bir_lowering=False, num_devices=1)
    arrays = lay_out({name: np.asarray(a) for name, a in inputs.items()})
    build(nc, arrays)
    out = run_bass_kernel_spmd(nc, [arrays], core_ids=[0]).results[0]["out"]
    return np.ascontiguousarray(out.transpose(1, 0, 2)).reshape(B, T, C)
```
